# Optimizing a Trainium2 kernel written in Bass

```python
import numpy as np
import jax
import jax.numpy as jnp

def _softmax(x, axis=-1):
    return jax.nn.softmax(x, axis=axis)

def _gelu(x):
    return jax.nn.gelu(x, approximate=True)

def _silu(x):
    return jax.nn.silu(x)

def _sigmoid(x):
    return jax.nn.sigmoid(x)

def _layernorm(x, axis=-1, eps=1e-05):
    m = jnp.mean(x, axis=axis, keepdims=True)
    v = jnp.var(x, axis=axis, keepdims=True)
    return (x - m) / jnp.sqrt(v + eps)

def _scatter_add(tgt, idx, src, axis=0):
    return tgt.at[idx].add(src)

def _segment_sum(src, seg, n):
    return jax.ops.segment_sum(src, seg, n)
kernel_name = 'mk_gnn_resnorm_d1_gnn_r16_4ca5b6'

def setup_inputs(seed: int=0):
    np.random.seed(seed)
    _w = jnp.asarray

    def _rec_inputs():
        import jax
        import jax.numpy as jnp
        _gk = jax.random.key(seed)
        x = -0.0002221 + 1 * jax.random.normal(jax.random.fold_in(_gk, 1), (3125, 768), jnp.float32)
        _s = jax.random.randint(jax.random.fold_in(_gk, 2), (25000,), 0, 3125, jnp.int32)
        _d = jax.random.randint(jax.random.fold_in(_gk, 3), (25000,), 0, 3125, jnp.int32)
        _loop = jnp.arange(3125, dtype=jnp.int32)
        src = jnp.concatenate([_s, _d, _loop])
        dst = jnp.concatenate([_d, _s, _loop])
        _o = jnp.argsort(dst, stable=True)
        src = src[_o]
        dst = dst[_o]
        edge_type_3 = jax.random.randint(jax.random.fold_in(_gk, 12), (53125,), 0, 3, jnp.int32)
        return (x, src, dst, edge_type_3)
    x, src, dst, edge_type_3 = _rec_inputs()

    def _L0_gnn_setup():
        import jax, jax.numpy as jnp
        import numpy as np
        NEG_SLOPE = 0.2
        EPS = 1e-16
        N_NODES = 2048
        N_EDGES = 10000
        DIM = 768
        HEADS1 = 4
        OUT1 = DIM // HEADS1
        HEADS2 = 1
        OUT2 = DIM
        N_REL = 3

        def rgat_conv(x, W, q, k, b, src, dst, etype, heads, out_ch, n_nodes):
            xr = jnp.einsum('nd,rdf->rnf', x, W)
            oi = xr[etype, dst]
            oj = xr[etype, src]
            qi = oi @ q
            kj = oj @ k
            alpha = jax.nn.leaky_relu(qi + kj, NEG_SLOPE)
            m = jax.ops.segment_max(alpha, dst, num_segments=n_nodes)
            e = jnp.exp(alpha - m[dst])
            z = jax.ops.segment_sum(e, dst, num_segments=n_nodes)
            a = e / (z[dst] + EPS)
            msg = (a[:, :, None] * oj.reshape(-1, heads, out_ch)).reshape(-1, heads * out_ch)
            out = jax.ops.segment_sum(msg, dst, num_segments=n_nodes)
            return out + b
        key = jax.random.key(seed)
        ks = jax.random.split(key, 12)
        s = 0.02
        return {'x': jax.random.normal(ks[0], (N_NODES, DIM), dtype=jnp.float32), 'edge_index': jax.random.randint(ks[1], (2, N_EDGES), 0, N_NODES, dtype=jnp.int64), 'edge_type': jax.random.randint(ks[2], (N_EDGES,), 0, N_REL, dtype=jnp.int64), 'W1': jax.random.normal(ks[3], (N_REL, DIM, HEADS1 * OUT1), dtype=jnp.float32) * s, 'q1': jax.random.normal(ks[4], (HEADS1 * OUT1, HEADS1), dtype=jnp.float32) * s, 'k1': jax.random.normal(ks[5], (HEADS1 * OUT1, HEADS1), dtype=jnp.float32) * s, 'b1': jnp.zeros((HEADS1 * OUT1,), dtype=jnp.float32), 'W2': jax.random.normal(ks[6], (N_REL, DIM, HEADS2 * OUT2), dtype=jnp.float32) * s, 'q2': jax.random.normal(ks[7], (HEADS2 * OUT2, HEADS2), dtype=jnp.float32) * s, 'k2': jax.random.normal(ks[8], (HEADS2 * OUT2, HEADS2), dtype=jnp.float32) * s, 'b2': jnp.zeros((HEADS2 * OUT2,), dtype=jnp.float32)}
    _L0_gnn_all = _L0_gnn_setup()
    _L0_gnn_in = {k: v for k, v in _L0_gnn_all.items() if k in ('W1', 'q1', 'k1', 'b1', 'W2', 'q2', 'k2', 'b2')}
    del _L0_gnn_all
    return {'x': x, 'src': src, 'dst': dst, 'edge_type_3': edge_type_3, 'L0_gnn_W1': _L0_gnn_in['W1'], 'L0_gnn_q1': _L0_gnn_in['q1'], 'L0_gnn_k1': _L0_gnn_in['k1'], 'L0_gnn_b1': _L0_gnn_in['b1'], 'L0_gnn_W2': _L0_gnn_in['W2'], 'L0_gnn_q2': _L0_gnn_in['q2'], 'L0_gnn_k2': _L0_gnn_in['k2'], 'L0_gnn_b2': _L0_gnn_in['b2']}

def reference(x, src, dst, edge_type_3, L0_gnn_W1, L0_gnn_q1, L0_gnn_k1, L0_gnn_b1, L0_gnn_W2, L0_gnn_q2, L0_gnn_k2, L0_gnn_b2):
    import jax
    import jax.numpy as jnp

    def _L0_gnn_ref(x, edge_index, edge_type, W1, q1, k1, b1, W2, q2, k2, b2):
        import jax, jax.numpy as jnp
        import numpy as np
        NEG_SLOPE = 0.2
        EPS = 1e-16
        N_NODES = 2048
        N_EDGES = 10000
        DIM = 768
        HEADS1 = 4
        OUT1 = DIM // HEADS1
        HEADS2 = 1
        OUT2 = DIM
        N_REL = 3

        def rgat_conv(x, W, q, k, b, src, dst, etype, heads, out_ch, n_nodes):
            xr = jnp.einsum('nd,rdf->rnf', x, W)
            oi = xr[etype, dst]
            oj = xr[etype, src]
            qi = oi @ q
            kj = oj @ k
            alpha = jax.nn.leaky_relu(qi + kj, NEG_SLOPE)
            m = jax.ops.segment_max(alpha, dst, num_segments=n_nodes)
            e = jnp.exp(alpha - m[dst])
            z = jax.ops.segment_sum(e, dst, num_segments=n_nodes)
            a = e / (z[dst] + EPS)
            msg = (a[:, :, None] * oj.reshape(-1, heads, out_ch)).reshape(-1, heads * out_ch)
            out = jax.ops.segment_sum(msg, dst, num_segments=n_nodes)
            return out + b
        src, dst = (edge_index[0], edge_index[1])
        n = x.shape[0]
        h = rgat_conv(x, W1, q1, k1, b1, src, dst, edge_type, HEADS1, OUT1, n)
        h = jax.nn.elu(h)
        out = rgat_conv(h, W2, q2, k2, b2, src, dst, edge_type, HEADS2, OUT2, n)
        return out
    edge_index = jnp.stack([src, dst])
    x = _layernorm(x + _L0_gnn_ref(x, edge_index, edge_type_3, L0_gnn_W1, L0_gnn_q1, L0_gnn_k1, L0_gnn_b1, L0_gnn_W2, L0_gnn_q2, L0_gnn_k2, L0_gnn_b2), axis=-1)
    return x

_drawn_inputs = setup_inputs


def setup_inputs(seed=0):
    import zlib

    import numpy as np

    out = dict(_drawn_inputs(seed))
    spreads = {'L0_gnn_b1': (0.0, 0.1), 'L0_gnn_b2': (0.0, 0.1)}
    factors = {'L0_gnn_W1': 2.93, 'L0_gnn_q1': 8.0, 'L0_gnn_k1': 8.0, 'L0_gnn_q2': 8.0, 'L0_gnn_k2': 8.0}
    for name, (base, spread) in spreads.items():
        noise = np.random.default_rng([zlib.crc32(name.encode()), seed]).standard_normal(out[name].shape)
        drawn = base * np.exp(spread * noise) if base else spread * noise
        out[name] = jnp.asarray(drawn.astype(out[name].dtype))
    for name, factor in factors.items():
        out[name] = (out[name] * factor).astype(out[name].dtype)
    return out
```

```python
from contextlib import ExitStack

import concourse.bass as bass
from concourse import mybir

F32 = mybir.dt.float32
BF16 = mybir.dt.bfloat16
I32 = mybir.dt.int32
ALU = mybir.AluOpType
ACT = mybir.ActivationFunctionType
AX = mybir.AxisListType

P = 128
BIG = 1.0e38
SLOPE = 0.2
SOFTMAX_EPS = 1e-16
NORM_EPS = 1e-5


def rgat_kernel(nc, x, src, dst, etype, W1, q1, k1, b1, W2, q2, k2, b2, out):
    N, D = x.shape
    E = src.shape[0]
    R = W1.shape[0]
    DC = D // P
    HALF = D // 2
    TN = 125
    NT = N // TN
    assert NT * TN == N and DC * P == D
    ETILES = -(-E // P)
    STEPS = E // P + NT
    RC = 4
    ROWS = STEPS // RC
    RL = RC * P
    assert ROWS * RC == STEPS and ROWS <= P
    EROWS = ETILES // RC
    assert EROWS * RC == ETILES
    LAST = E - (EROWS - 1) * RL
    PAD_DST = 32 * TN
    KEY = 8192.0
    HCOLS = E // TN
    HCH = HCOLS // NT
    HA = (HCH + 1) // 2
    HB = HCH - HA
    assert HCOLS * TN == E and HCH * NT == HCOLS
    AHEAD = 4
    GS = 8
    KG = 11
    assert STEPS % GS == 0 and STEPS % (2 * KG) == 0
    U = 5
    UW = 3
    WT = R * DC
    assert NT % U == 0 and WT % UW == 0
    PAT = [0, 1, 2, 0, 1]
    HEADS = [q1.shape[1], q2.shape[1]]
    HM = max(HEADS)
    HWS = [D // h + (1 if h > 1 else 2) for h in HEADS]
    ROWW = [h * w for h, w in zip(HEADS, HWS)]
    RW = max(ROWW)
    LAYERS = [(W1, q1, k1, b1), (W2, q2, k2, b2)]

    etab = nc.dram_tensor("edge_table", (ETILES * P, 3), F32, kind="Internal").ap()
    qfill = [nc.dram_tensor(f"q_fill{l}", (STEPS * P + N, R * HEADS[l]), F32, kind="Internal").ap() for l in range(2)]
    ktab = [nc.dram_tensor(f"k_table{l}", (N * R, HEADS[l]), F32, kind="Internal").ap() for l in range(2)]
    xrtab = [nc.dram_tensor(f"xr_table{l}", (N * R, ROWW[l]), F32, kind="Internal").ap() for l in range(2)]
    hid = nc.dram_tensor("hidden", (N, D), F32, kind="Internal").ap()

    ctx = ExitStack()
    with ctx:
        def sb(name, shape, dt=F32):
            return ctx.enter_context(nc.sbuf_tensor(name, shape, dt))

        def sem(name):
            return ctx.enter_context(nc.semaphore(name))

        banks = ctx.enter_context(nc.psum_tensor("banks", [P, 8, 512], F32))
        bank = [banks[:, i, :] for i in range(8)]

        ACCW = NT * RW
        big = sb("big", [P, ACCW])
        wsb = sb("wsb", [P, DC, R, D])
        ring = sb("ring", [P, GS, RW])
        xring = sb("xring", [P, U, D])
        xT = sb("xT", [P, 3, DC, P])
        qk_node = sb("qk_node", [P, NT, 2 * R * HM])
        wqk = sb("wqk", [P, WT, 2 * HM])
        qkw = sb("qkw", [P, DC, 2, HM])
        row_idx = sb("row_idx", [P, STEPS], I32)
        dloc = sb("dloc", [P, STEPS + AHEAD])
        wE = sb("wE", [P, STEPS + AHEAD, HM])
        acc_at = sb("acc_at", [RC, 2, ROWS], I32)
        ev = wE[0:ROWS, 0:RC * P * 3 // HM, :].rearrange("r a b -> r (a b)").rearrange("r (c j a) -> r c j a", c=RC, a=3)
        rel = sb("rel", [P, RL])
        pen = sb("pen", [P, RL + 1])
        same = sb("same", [P, RL])
        flag = sb("flag", [R * HM, 8, ROWS + 1])
        EQ, EQPEN, CONT, CONTPEN, CARRY, CONTPEN_B, UNI, RUN = range(8)
        brow = sb("brow", [P, D])
        ident = sb("ident", [P, P])
        iota_n = sb("iota_n", [P, TN])
        start_at = sb("start_at", [P, NT], I32)
        kidx = sb("kidx", [P, 2, KG], I32)
        gidx = sb("gidx", [P, 2, GS // 2], I32)
        small = sb("small", [P, 512])

        zeros = big[:, 0:STEPS * R * HM]
        qf_raw = big[0:ROWS, 0:RL * R * HM]
        o = RL * R * HM
        qf = big[0:ROWS, o:o + RL * R * HM].rearrange("r (q x) -> r q x", x=RL)
        rows_i = big[0:EROWS, o:o + 3 * RL].bitcast(I32).rearrange("r (a x) -> r a x", a=3)
        ev_rows = big[0:EROWS, o + 3 * RL:o + 6 * RL].rearrange("r (x a) -> r x a", a=3)
        o1 = o + 6 * RL
        dst_i = big[0:TN, o1:o1 + HCOLS].bitcast(I32)
        dst_f = big[0:TN, o1 + HCOLS:o1 + 2 * HCOLS]
        d_y = big[0:TN, o1 + 2 * HCOLS:o1 + 3 * HCOLS]
        d_i = big[0:TN, o1 + 3 * HCOLS:o1 + 4 * HCOLS].bitcast(I32)
        d_hi = big[0:TN, o1 + 4 * HCOLS:o1 + 5 * HCOLS]
        d_lo = big[0:TN, o1 + 5 * HCOLS:o1 + 6 * HCOLS]
        o += RL * R * HM
        alpha = big[0:ROWS, o:o + HM * RL].rearrange("r (h x) -> r h x", h=HM)
        o += HM * RL
        amax = big[0:ROWS, o:o + HM * RL].rearrange("r (h x) -> r h x", h=HM)
        o += HM * RL
        k_edge = big[:, o:o + STEPS * HM]
        o += STEPS * HM
        kring = big[:, o:o + 2 * KG * HM]
        o += 2 * KG * HM
        key = big[0:ROWS, o:o + RL]
        assert o + RL <= ACCW
        xt_flat = xring[:, :, :].rearrange("p u d -> p (u d)")
        S = xt_flat[:, 0:AHEAD * HM * TN].rearrange("p (s h n) -> p s h n", s=AHEAD, h=HM)
        hot = xt_flat[:, AHEAD * HM * TN:AHEAD * (HM + 1) * TN].rearrange("p (s n) -> p s n", s=AHEAD)
        hlo = [ring[0:TN, i, 0:640].bitcast(BF16)[:, 0:HA * TN].rearrange("p (a n) -> p a n", a=HA) for i in range(2)]
        hhi = [ring[0:TN, 2 + i, 0:128].bitcast(BF16)[:, 0:HA * NT].rearrange("p (a n) -> p a n", a=HA) for i in range(2)]
        zero_bf = ring[0:TN, 4, 0:64].bitcast(BF16)
        below = ring[0:TN, 5, 0:TN]
        ones = ring[0:TN, 6, 0:P]

        def cols(n, _at=[0]):
            _at[0] += n
            assert _at[0] <= 512
            return slice(_at[0] - n, _at[0])

        c_cnt, c_tot, c_inc, c_rp, c_y, c_f, c_St = (cols(NT) for _ in range(7))
        c_it, c_t125, c_trash = (cols(NT) for _ in range(3))
        c_sio, c_ts, c_is, c_t8, c_tn, c_ta = (cols(RC) for _ in range(6))
        c_ends = cols(2 * R * HM)
        c_last = cols(R * HM)
        c_carry = cols(R * HM)
        c_z = cols(NT * HM)
        c_mv = cols(2 * NT)
        c_iota = cols(NT)

        dve_step, pool_step, act_gate, pool_gate, dve_gate = (sem(n) for n in
            ("dve_step", "pool_step", "act_gate", "pool_gate", "dve_gate"))
        consts_ready, edges_loaded, pads_set, dst_loaded, qk_loaded = (sem(n) for n in
            ("consts_ready", "edges_loaded", "pads_set", "dst_loaded", "qk_loaded"))
        zeros_set, fills_zeroed, hot_ready, hot_used, counts_done, sums_done = (sem(n) for n in
            ("zeros_set", "fills_zeroed", "hot_ready", "hot_used", "counts_done", "sums_done"))
        cnt_ready, etab_src, etab_stored, steps_ready, ev_gathered, rows_ready, turned, lanes_ready = (sem(n) for n in
            ("cnt_ready", "etab_src", "etab_stored", "steps_ready", "ev_gathered", "rows_ready", "turned", "lanes_ready"))
        start_ready = sem("start_ready")
        
        shared = {n: sem(n) for n in
                  ("ones_set q_scattered q_loaded k_stored k_ready qend_ready qend_turned qcarry_ready qcarry_turned "
                   "qcarry_taken end_ready end_turned carry_ready carry_turned diff_ready e_ready w_ready sums_zeroed "
                   "brow_loaded w_loaded k_turned e_turned x_used x_added S_built").split()}
        shared["x_loaded"] = [sem(f"x_loaded{i}") for i in range(U)]
        LS = []
        for l in range(2):
            s = {n: sem(f"{n}_{l}") for n in
                 ("xT_turned xT_ready qk_done qk_copied kidx_staged k_taken dT_turned dT_ready dense_done dense_out "
                  "hot_built gidx_staged step_done sum_added u_ready exp_ready h_ready e_set h_out").split()}
            for n, k in (("row_loaded", U), ("drow_loaded", U), ("staged_stored", U), ("k_gathered", 2),
                         ("row_gathered", GS), ("h_stored", 3)):
                s[n] = [sem(f"{n}{i}_{l}") for i in range(k)]
            LS.append({**shared, **s})

        def heads(ap, h):
            return ap.rearrange("p (h w) -> p h w", h=h)

        def node_sum(l, t):
            return heads(big[0:TN, bass.ds(t * ROWW[l], ROWW[l])], HEADS[l])[:, :, 0:D // HEADS[l]]

        def turns(eng, total, per):
            n = total // per
            with eng.Fori(0, n - 1) as i:
                yield i, False
            yield n - 1, True

        block = ctx.enter_context(nc.Block())

        @block.sync
        def _(sp):
            sp.dma_start(dst_i, dst.rearrange("(p c) -> p c", c=HCOLS)).then_inc(dst_loaded, 16)
            sp.wait_ge(pads_set, 1)
            for a, arr in enumerate((src, etype, dst)):
                sp.dma_start(rows_i[0:EROWS - 1, a, :],
                             arr[0:(EROWS - 1) * RL].rearrange("(r x) -> r x", x=RL)).then_inc(edges_loaded, 16)
                sp.dma_start(rows_i[EROWS - 1:EROWS, a, 0:LAST],
                             arr[(EROWS - 1) * RL:E].rearrange("(r x) -> r x", r=1)).then_inc(edges_loaded, 16)

            def load_rows(l, sems, used, table, rows, n, slot, k):
                sp.wait_ge(used, n + 1)
                sp.dma_start(xring[0:rows, slot, :], table[bass.ds(k * rows, rows), :]).then_inc(sems[slot], 16)

            for l, (W, q, kk, b) in enumerate(LAYERS):
                s = LS[l]
                H = HEADS[l]
                table = x if l == 0 else hid
                if l == 1:
                    sp.wait_ge(LS[0]["qk_copied"], 1 + WT + NT)
                for a, arr in enumerate((q, kk)):
                    sp.dma_start(qkw[:, :, a, 0:H], arr.rearrange("(c p) h -> p c h", p=P), allow_slow_non_contiguous=True).then_inc(qk_loaded, 16)
                if l == 1:
                    sp.wait_ge(LS[0]["h_ready"], NT)
                    sp.wait_ge(LS[0]["h_out"], NT)
                    for i in range(3):
                        sp.wait_ge(LS[0]["h_stored"][i], 16 * (1 + (NT // U) * PAT.count(i)))
                sp.dma_start(brow[0:TN, :], b.partition_broadcast(TN)).then_inc(s["brow_loaded"], 16)
                W_rows = W.rearrange("r d f -> (r d) f")
                for i, last in turns(sp, WT, UW):
                    for k in range(UW):
                        load_rows(l, s["row_loaded"], s["xT_turned"], W_rows, P, UW * i + k, k, UW * i + k)
                if l == 0:
                    for r in range(R):
                        sp.dma_start(wsb[:, :, r, :], W[r].rearrange("(c p) f -> p c f", p=P)).then_inc(s["w_loaded"], 16)
                    sp.wait_ge(zeros_set, 1)
                    for m in range(2):
                        width = STEPS * R * HEADS[m]
                        sp.dma_start(qfill[m][0:STEPS * P, :].rearrange("(p y) q -> p (y q)", p=P),
                                     zeros[:, 0:width]).then_inc(fills_zeroed, 16)
                for i, last in turns(sp, NT, U):
                    for k in range(U):
                        load_rows(l, s["row_loaded"], s["xT_turned"], table, TN, U * i + k + WT, k, U * i + k)
                if l == 0:
                    sp.wait_ge(etab_src, 1)
                    sp.dma_start(etab.rearrange("(r x) a -> r x a", x=RL), ev_rows).then_inc(etab_stored, 16)
                sp.wait_ge(s["qk_copied"], 1 + WT + NT)
                sp.dma_start(ktab[l].rearrange("(t p r) h -> p t (r h)", p=TN, r=R),
                             qk_node[0:TN, :, R * H:2 * R * H]).then_inc(s["k_stored"], 16)
                for r in range(U):
                    sp.sem_inc(s["staged_stored"][r], 16)

                def load_dense(n, k):
                    sp.wait_ge(s["dT_turned"], n + 1)
                    sp.dma_start(xring[0:TN, k, :], table[bass.ds(n * TN, TN), :]).then_inc(s["drow_loaded"][k], 16)

                xr_rows = xrtab[l].rearrange("(n r) w -> n r w", r=R)
                for k in range(3):
                    load_dense(k, k)
                for i, last in turns(sp, NT, U):
                    for k in range(U):
                        if not last or k + 3 < U:
                            load_dense(U * i + k + 3, (k + 3) % U)
                        for r in range(R):
                            unit = R * k + r
                            sp.wait_ge(s["dense_out"], 2 * R + 2 * (R * (U * i + k) + r) + 2)
                            sp.dma_start(xr_rows[bass.ds((U * i + k) * TN, TN), r, :],
                                         ring[0:TN, unit % U, 0:ROWW[l]]).then_inc(s["staged_stored"][unit % U], 16)
                if l == 0:
                    sp.wait_ge(s["dense_done"], 2 * R * NT)
                    for r in range(R):
                        sp.dma_start(wsb[:, :, r, :], W2[r].rearrange("(c p) f -> p c f", p=P)
                                     ).then_inc(LS[1]["w_loaded"], 16)
                    for i in range(3):
                        sp.sem_inc(s["h_stored"][i], 16)
                    for i, last in turns(sp, NT, U):
                        for k in range(U):
                            sp.wait_ge(s["h_out"], U * i + k + 1)
                            sp.dma_start(hid[bass.ds((U * i + k) * TN, TN), :],
                                         ring[0:TN, 3 + PAT[k], 0:D]).then_inc(s["h_stored"][PAT[k]], 16)
                else:
                    for i in range(3):
                        sp.sem_inc(s["h_stored"][i], 16)
                    sp.wait_ge(s["sum_added"], AHEAD + STEPS)
                    for i, last in turns(sp, NT, U):
                        for k in range(U):
                            sp.wait_ge(s["x_used"], U * i + k + 1)
                            sp.dma_start(xring[0:TN, k, :], x[bass.ds((U * i + k) * TN, TN), :]
                                         ).then_inc(s["x_loaded"][k], 16)
                    for i, last in turns(sp, NT, U):
                        for k in range(U):
                            sp.wait_ge(s["h_out"], U * i + k + 1)
                            sp.dma_start(out[bass.ds((U * i + k) * TN, TN), :],
                                         ring[0:TN, 3 + PAT[k], 0:D]).then_inc(s["h_stored"][PAT[k]], 16)
                    for i in range(3):
                        sp.wait_ge(s["h_stored"][i], 16 * (1 + (NT // U) * PAT.count(i)))

        @block.tensor
        def _(pe):
            pe.wait_ge(consts_ready, 1)
            for l in range(2):
                s = LS[l]
                H = HEADS[l]
                HW = HWS[l]

                def turn(n, slot, rows, seen):
                    xs, pair = slot
                    pe.wait_ge(s["row_loaded"][xs], 16 * seen)
                    pe.wait_ge(s["xT_ready"], n + 1)
                    for c in range(DC):
                        last = pe.transpose(bank[2 * pair + c // 4][:, (c % 4) * P:(c % 4) * P + rows],
                                            xring[0:rows, xs, c * P:(c + 1) * P], ident[0:rows, 0:rows])
                        if c == DC - 1:
                            last.then_inc(s["xT_turned"], 1)

                def terms(n, pair, rows, rhs, width):
                    pe.wait_ge(s["xT_ready"], n + 3)
                    pe.wait_ge(s["qk_copied"], n + 1)
                    for c in range(DC):
                        last = pe.matmul(bank[6][0:rows, 0:width], xT[:, pair, c, 0:rows], rhs(c),
                                         start=(c == 0), stop=(c == DC - 1))
                    last.then_inc(s["qk_done"], 1)

                def w_rhs(c):
                    return qkw[:, c, :, 0:H]

                def x_rhs(c):
                    return wqk[:, :, 0:2 * H].rearrange("p (r c) (a h) -> p c a r h", c=DC, a=2)[:, c]

                def hist(t):
                    for half, n in ((0, HA), (1, HB)):
                        pe.wait_ge(hot_ready, 2 * t + half + 1)
                        for j in range(n):
                            last = pe.matmul(bank[7][0:TN, 0:NT], hlo[half][:, j, :], hhi[half][:, j, :],
                                             start=False, stop=False)
                        last.then_inc(hot_used, 1)

                pe.sem_inc(s["xT_turned"], 3)
                pe.sem_inc(s["dT_turned"], U)
                if l == 0:
                    pe.sem_inc(hot_used, 2)
                    pe.matmul(bank[7][0:TN, 0:NT], zero_bf[:, 0:TN], zero_bf[:, 0:NT], start=True, stop=False)
                pe.wait_ge(qk_loaded, 32 * (l + 1))
                turn(0, (0, 0), P, 1)
                for i, last_turn in turns(pe, WT, UW):
                    for k in range(UW):
                        n = UW * i + k
                        if k < UW - 1:
                            turn(n + 1, (k + 1, k + 1), P, i + 1)
                        elif not last_turn:
                            turn(n + 1, (0, 0), P, i + 2)
                        else:
                            turn(WT, (0, 0), TN, WT // UW + 1)
                        terms(n, k, P, w_rhs, 2 * H)
                for i, last_turn in turns(pe, NT, U):
                    for k in range(U):
                        n = WT + U * i + k
                        if k < U - 1:
                            turn(n + 1, (k + 1, PAT[k + 1]), TN, (WT // UW if k + 1 < UW else 0) + i + 1)
                        elif not last_turn:
                            turn(n + 1, (0, 0), TN, WT // UW + i + 2)
                        terms(n, PAT[k], TN, x_rhs, 2 * R * H)
                        if l == 0:
                            hist(U * i + k)
                pe.wait_ge(s["qk_copied"], 1 + WT + NT)
                if l == 0:
                    pe.matmul(bank[7][0:TN, 0:NT], zero_bf[:, 0:TN], zero_bf[:, 0:NT], start=False, stop=True
                              ).then_inc(counts_done, 1)
                    pe.wait_ge(cnt_ready, 1)
                    cnt = small[0:TN, c_cnt]
                    pe.matmul(bank[6][0:TN, 0:NT], below, cnt, start=True, stop=True)
                    pe.matmul(bank[6][0:P, 32:32 + NT], ones, cnt, start=True, stop=True).then_inc(sums_done, 1)
                    pe.wait_ge(rows_ready, 1)
                    for c in range(RC):
                        pe.transpose(bank[0][:, c * ROWS:(c + 1) * ROWS], ev[:, c, :, 0], ident[0:ROWS, 0:ROWS])
                        pe.transpose(bank[1][:, c * ROWS:(c + 1) * ROWS], ev[:, c, :, 2], ident[0:ROWS, 0:ROWS])
                    pe.transpose(bank[2][0:RC, 0:ROWS], small[0:ROWS, c_ta], ident[0:ROWS, 0:ROWS])
                    ends = small[0:ROWS, c_ends]
                    for a in range(2):
                        last = pe.transpose(bank[3][0:R * HM, a * P:a * P + ROWS], ends[:, a * R * HM:(a + 1) * R * HM],
                                            ident[0:ROWS, 0:ROWS])
                    last.then_inc(turned, 1)
                    pe.wait_ge(lanes_ready, 1)

                pe.wait_ge(s["w_loaded"], 16 * R * (l + 1))

                def dturn(n, k, seen):
                    pe.wait_ge(s["drow_loaded"][k], 16 * seen)
                    pe.wait_ge(s["dT_ready"], n + 1)
                    for c in range(DC):
                        last = pe.transpose(bank[6 + c // 4][:, (c % 4) * P:(c % 4) * P + TN],
                                            xring[0:TN, k, c * P:(c + 1) * P], ident[0:TN, 0:TN])
                    last.then_inc(s["dT_turned"], 1)

                def dense(n, k):
                    pe.wait_ge(s["dT_ready"], n + 2)
                    for r in range(R):
                        for half in range(2):
                            b = 2 * r + half
                            pe.wait_ge(s["dense_out"], 2 * R * n + b + 1)
                            for c in range(DC):
                                last = pe.matmul(bank[b][0:TN, 0:HALF], xT[:, PAT[k], c, 0:TN],
                                                 wsb[:, c, r, half * HALF:(half + 1) * HALF],
                                                 start=(c == 0), stop=(c == DC - 1))
                            last.then_inc(s["dense_done"], 1)

                def dense_turn(i, last_turn=False):
                    for k in range(U):
                        n = U * i + k
                        if k < U - 1:
                            dturn(n + 1, k + 1, i + 1)
                        elif not last_turn:
                            dturn(n + 1, 0, i + 2)
                        dense(n, k)

                MID = (NT // U) // 2
                dturn(0, 0, 1)
                with pe.Fori(0, MID) as i:
                    dense_turn(i)
                pe.wait_ge(s["qend_ready"], l + 1)
                pe.wait_ge(s["dT_ready"], U * MID + 2)
                pe.transpose(bank[7][0:R * H, 256:256 + ROWS], small[0:ROWS, c_last][:, 0:R * H], ident[0:ROWS, 0:ROWS]
                             ).then_inc(s["qend_turned"], 1)
                pe.wait_ge(s["qcarry_ready"], l + 1)
                pe.transpose(bank[7][0:ROWS, 384:384 + R * H], flag[0:R * H, CARRY, 0:ROWS], ident[0:R * H, 0:R * H]
                             ).then_inc(s["qcarry_turned"], 1)
                pe.wait_ge(s["qcarry_taken"], l + 1)
                with pe.Fori(MID, NT // U - 1) as i:
                    dense_turn(i)
                dense_turn(NT // U - 1, True)

                pe.wait_ge(s["dense_out"], 2 * R * (NT + 1))
                pe.wait_ge(s["k_ready"], l + 1)
                k_lanes = k_edge[:, 0:STEPS * H].rearrange("p (r c h) -> p c h r", c=RC, h=H)
                for h in range(H):
                    for c in range(RC):
                        last = pe.transpose(bank[h][0:ROWS, c * P:(c + 1) * P], k_lanes[:, c, h, :], ident[:, :])
                    last.then_inc(s["k_turned"], 1)
                for w in range(2):
                    pe.wait_ge(s["end_ready"], 2 * l + w + 1)
                    pe.transpose(bank[4 + w][0:H, 0:ROWS], small[0:ROWS, c_last][:, 0:H], ident[0:ROWS, 0:ROWS]
                                 ).then_inc(s["end_turned"], 1)
                    pe.wait_ge(s["carry_ready"], 2 * l + w + 1)
                    pe.transpose(bank[6 + w][0:ROWS, 0:H], flag[0:H, CARRY, 0:ROWS], ident[0:H, 0:H]
                                 ).then_inc(s["carry_turned"], 1)
                for h in range(H):
                    pe.wait_ge(s["e_ready"], l + 1)
                    for c in range(RC):
                        last = pe.transpose(bank[h][:, c * ROWS:(c + 1) * ROWS], amax[:, h, c * P:(c + 1) * P],
                                            ident[0:ROWS, 0:ROWS])
                    last.then_inc(s["e_turned"], 1)
                pe.wait_ge(s["w_ready"], l + 1)

                pe.sem_inc(s["step_done"], GS)
                HB2 = ROWW[l] // 2
                with pe.Fori(0, STEPS // GS) as i:
                    for j in range(GS):
                        st = GS * i + j
                        slot = j % AHEAD
                        pe.wait_ge(s["row_gathered"][j], 16 * (i + 1))
                        pe.wait_ge(s["S_built"] if H > 1 else s["hot_built"], st + 1 + (AHEAD if H > 1 else 0))
                        pe.wait_ge(s["sum_added"], st + 1)
                        for half in range(2):
                            for m in range(max(H // 2, 1)):
                                h = half * (H // 2) + m
                                w = HW if H > 1 else HB2
                                last = pe.matmul(bank[2 * slot + half][0:TN, m * w:(m + 1) * w],
                                                 S[:, slot, h, :],
                                                 ring[:, j, half * HB2 + m * w:half * HB2 + (m + 1) * w],
                                                 start=True, stop=True)
                        last.then_inc(s["step_done"], 1)

        @block.scalar
        def _(act):
            def gate(sm, value):
                act.wait_ge(sm, value)
                act.sem_inc(act_gate, 1)

            def from_banks(dst_slot, b, rows):
                nc.scalar.copy(xT[:, dst_slot, 0:4, 0:rows],
                               bank[b].rearrange("p (c n) -> p c n", c=4)[:, :, 0:rows])
                return nc.scalar.copy(xT[:, dst_slot, 4:DC, 0:rows],
                                      bank[b + 1].rearrange("p (c n) -> p c n", c=4)[:, 0:DC - 4, 0:rows])

            for l in range(2):
                s = LS[l]
                H = HEADS[l]
                act.sem_inc(s["xT_ready"], 2)
                act.sem_inc(s["qk_copied"], 1)
                act.sem_inc(s["dT_ready"], 1)
                act.sem_inc(s["dense_out"], 2 * R)
                if H > 1:
                    act.sem_inc(s["S_built"], AHEAD)

                def take(n, pair, rows):
                    act.wait_ge(s["xT_turned"], n + 4)
                    act.wait_ge(s["qk_done"], n + 1)
                    from_banks(pair, 2 * pair, rows).then_inc(s["xT_ready"], 1)

                def store_terms(n, rows, dest, width):
                    gate(s["qk_done"], n + 3)
                    nc.scalar.copy(dest, bank[6][0:rows, 0:width]).then_inc(s["qk_copied"], 1)

                act.sem_inc(s["qk_done"], 2)
                for i, last_turn in turns(act, WT, UW):
                    for k in range(UW):
                        n = UW * i + k
                        take(n, k, P)
                        store_terms(n, P, wqk[:, bass.ds(n, 1), 0:2 * H].rearrange("p a b -> p (a b)"), 2 * H)
                for i, last_turn in turns(act, NT, U):
                    for k in range(U):
                        t = U * i + k
                        take(WT + t, PAT[k], TN)
                        store_terms(WT + t, TN, qk_node[0:TN, bass.ds(t, 1), 0:2 * R * H].rearrange("p a b -> p (a b)"),
                                    2 * R * H)

                act.sem_inc(s["dense_done"], 4 * R)

                def dtake(n, k):
                    act.wait_ge(s["dT_turned"], n + 1 + U)
                    act.wait_ge(s["dense_done"], 2 * R * (n + 1))
                    from_banks(PAT[k], 6, TN).then_inc(s["dT_ready"], 1)

                def dense_turn(i, last_turn=False):
                    for k in range(U):
                        n = U * i + k
                        if k < U - 1:
                            dtake(n + 1, k + 1)
                        elif not last_turn:
                            dtake(n + 1, 0)
                        for r in range(R):
                            unit = R * k + r
                            slot = unit % U
                            act.wait_ge(s["staged_stored"][slot], 16 * (R * i + unit // U + 1))
                            for half in range(2):
                                act.wait_ge(s["dense_done"], 4 * R + 2 * R * n + 2 * r + half + 1)
                                if H > 1:
                                    o_ = ring[0:TN, slot, 0:ROWW[l]].rearrange("p (h w) -> p h w", h=H)[
                                        :, half * (H // 2):(half + 1) * (H // 2), 0:D // H]
                                    i_ = bank[2 * r + half][0:TN, 0:HALF].rearrange("p (h w) -> p h w", h=H // 2)
                                else:
                                    o_ = ring[0:TN, slot, half * HALF:(half + 1) * HALF]
                                    i_ = bank[2 * r + half][0:TN, 0:HALF]
                                nc.scalar.copy(o_, i_).then_inc(s["dense_out"], 1)

                act.wait_ge(s["ones_set"], l + 1)
                dtake(0, 0)
                with act.Fori(0, NT // U - 1) as i:
                    dense_turn(i)
                dense_turn(NT // U - 1, True)

                act.wait_ge(s["diff_ready"], l + 1)
                nc.scalar.activation(amax[:, 0:H, :], alpha[:, 0:H, :], ACT.Exp).then_inc(s["e_ready"], 1)

                if H > 1:
                    act.wait_ge(s["w_ready"], l + 1)
                    with act.Fori(0, STEPS // GS) as i:
                        for j in range(GS):
                            st = GS * i + j
                            slot = j % AHEAD
                            act.wait_ge(s["hot_built"], st + 1)
                            gate(s["step_done"], st + 1 + GS - AHEAD)
                            for h in range(H):
                                last = nc.scalar.activation(S[:, slot, h, :], hot[:, slot, :], ACT.Copy,
                                                            scale=wE[:, bass.ds(st, 1), h:h + 1].rearrange("p a b -> p (a b)"))
                            last.then_inc(s["S_built"], 1)

                if l == 0:
                    for i, last_turn in turns(act, NT, U):
                        for k in range(U):
                            t = U * i + k
                            gate(s["u_ready"], t + 1)
                            u = node_sum(l, t)
                            nc.scalar.activation(heads(ring[0:TN, PAT[k], 0:D], H), u, ACT.Exp).then_inc(s["e_set"], 1)
                            nc.scalar.activation(heads(xring[0:TN, PAT[k], :], H), u, ACT.Relu).then_inc(s["exp_ready"], 1)
                            act.wait_ge(s["h_ready"], t + 1)
                            act.wait_ge(s["h_stored"][PAT[k]], 16 * (PAT.count(PAT[k]) * i + PAT[:k].count(PAT[k]) + 1))
                            nc.scalar.activation(ring[0:TN, 3 + PAT[k], 0:D], xring[0:TN, PAT[k], :], ACT.Copy,
                                                 bias=-1.0).then_inc(s["h_out"], 1)
                else:
                    mv = small[0:TN, c_mv].rearrange("p (t a) -> p t a", a=2)
                    act.wait_ge(s["u_ready"], 1)
                    nc.scalar.activation(mv[:, :, 1], mv[:, :, 1], ACT.Sqrt).then_inc(s["exp_ready"], 1)
                    act.wait_ge(s["h_ready"], 1)
                    for i, last_turn in turns(act, NT, U):
                        for k in range(U):
                            t = U * i + k
                            gate(s["h_stored"][PAT[k]], 16 * (PAT.count(PAT[k]) * i + PAT[:k].count(PAT[k]) + 1))
                            m = mv[:, bass.ds(t, 1), :].rearrange("p a b -> p (a b)")
                            nc.scalar.activation(heads(ring[0:TN, 3 + PAT[k], 0:D], H), node_sum(l, t), ACT.Identity, scale=m[:, 1:2], bias=m[:, 0:1]).then_inc(s["h_out"], 1)

        @block.gpsimd
        def _(pool):
            chain = [0]

            def link(ins):
                chain[0] += 1
                ins.then_inc(pool_step, 1)
                pool.wait_ge(pool_step, chain[0])

            def gate(sm, value):
                pool.wait_ge(sm, value)
                pool.sem_inc(pool_gate, 1)

            link(nc.gpsimd.memset(ident[:, :], 0.0))
            link(nc.gpsimd.affine_select(out=ident[:, :], in_=ident[:, :], compare_op=ALU.not_equal, fill=1.0,
                                         base=0, pattern=[[-1, P]], channel_multiplier=1))
            link(nc.gpsimd.memset(below, 1.0))
            link(nc.gpsimd.affine_select(out=below, in_=below, compare_op=ALU.is_gt, fill=0.0,
                                         base=0, pattern=[[1, TN]], channel_multiplier=-1))
            link(nc.gpsimd.memset(ones, 1.0))
            link(nc.gpsimd.memset(zero_bf, 0.0))
            link(nc.gpsimd.iota(iota_n[:, :], [[1, TN]], base=0, channel_multiplier=0,
                                allow_small_or_imprecise_dtypes=True))
            link(nc.gpsimd.iota(small[:, c_it], [[1, NT]], base=0, channel_multiplier=0,
                                allow_small_or_imprecise_dtypes=True))
            link(nc.gpsimd.iota(small[:, c_t125], [[P, NT]], base=0, channel_multiplier=0,
                                allow_small_or_imprecise_dtypes=True))
            link(nc.gpsimd.iota(small[:, c_trash], [[TN, NT]], base=STEPS * P, channel_multiplier=1,
                                allow_small_or_imprecise_dtypes=True))
            link(nc.gpsimd.iota(small[:, c_sio], [[1, RC]], base=0, channel_multiplier=RC,
                                allow_small_or_imprecise_dtypes=True))
            pool.sem_inc(consts_ready, 1)
            nc.gpsimd.memset(zeros, 0.0).then_inc(zeros_set, 1)

            pool.wait_ge(etab_stored, 16)
            pool.wait_ge(steps_ready, 1)
            etab_rows = etab.rearrange("(i j) a -> i (j a)", j=P)
            for c in range(RC):
                nc.gpsimd.indirect_dma_start(
                    ev[:, c, :, :].rearrange("r j a -> r (j a)"), None, etab_rows,
                    bass.IndirectOffsetOnAxis(ap=small[0:ROWS, c_is].bitcast(I32)[:, c:c + 1], axis=0),
                ).then_inc(ev_gathered, 16)

            for l in range(2):
                s = LS[l]
                H = HEADS[l]
                pool.wait_ge(start_ready, 1)
                pool.wait_ge(fills_zeroed, 32)
                pool.wait_ge(s["qk_copied"], 1 + WT + NT)
                for t in range(NT):
                    nc.gpsimd.indirect_dma_start(
                        qfill[l], bass.IndirectOffsetOnAxis(ap=start_at[0:TN, t:t + 1], axis=0),
                        qk_node[0:TN, t, 0:R * H], None).then_inc(s["q_scattered"], 16)
                pool.wait_ge(s["q_scattered"], 16 * NT * (l + 1))
                pool.dma_start(qf_raw[:, 0:RL * R * H], qfill[l][0:STEPS * P, :].rearrange("(r x) q -> r (x q)", x=RL)
                               ).then_inc(s["q_loaded"], 16)

                pool.wait_ge(s["k_stored"], 16 * (l + 1))
                pool.wait_ge(lanes_ready, 1)
                pool.sem_inc(s["k_taken"], 2)

                def fetch(m, g, turn_):
                    gate(s["k_taken"], m + 1)
                    nc.gpsimd.tensor_copy(kidx[:, g, :], row_idx[:, bass.ds(m * KG, KG)]).then_inc(s["kidx_staged"], 1)
                    gate(s["kidx_staged"], m + 1)
                    for j in range(KG):
                        nc.gpsimd.indirect_dma_start(
                            kring[:, (g * KG + j) * H:(g * KG + j + 1) * H], None, ktab[l],
                            bass.IndirectOffsetOnAxis(ap=kidx[:, g, j:j + 1], axis=0)).then_inc(s["k_gathered"][g], 16)

                def take(m, g, turn_):
                    gate(s["k_gathered"][g], 16 * KG * (turn_ + 1))
                    nc.gpsimd.tensor_copy(k_edge[:, bass.ds(m * KG * H, KG * H)],
                                          kring[:, g * KG * H:(g + 1) * KG * H]).then_inc(s["k_taken"], 1)

                fetch(0, 0, 0)
                for i, last in turns(pool, STEPS // KG, 2):
                    fetch(2 * i + 1, 1, i)
                    take(2 * i, 0, i)
                    if not last:
                        fetch(2 * i + 2, 0, i + 1)
                    take(2 * i + 1, 1, i)
                pool.wait_ge(s["k_taken"], 2 + STEPS // KG)
                pool.sem_inc(s["k_ready"], 1)

                pool.wait_ge(s["w_ready"], l + 1)
                nc.gpsimd.memset(big[0:TN, ACCW // 2:ACCW], 0.0).then_inc(s["sums_zeroed"], 1)

                for i in range(U):
                    pool.wait_ge(s["staged_stored"][i], 16 * (1 + NT * R // U))
                half = GS // 2
                with pool.Fori(0, STEPS // GS) as i:
                    for g in range(2):
                        m = 2 * i + g
                        gate(s["step_done"], half * (m + 1))
                        nc.gpsimd.tensor_copy(gidx[:, g, :], row_idx[:, bass.ds(m * half, half)]
                                              ).then_inc(s["gidx_staged"], 1)
                        gate(s["gidx_staged"], m + 1)
                        for j in range(half):
                            nc.gpsimd.indirect_dma_start(
                                ring[:, g * half + j, 0:ROWW[l]], None, xrtab[l],
                                bass.IndirectOffsetOnAxis(ap=gidx[:, g, j:j + 1], axis=0)
                            ).then_inc(s["row_gathered"][g * half + j], 16)
                if l == 1:
                    pool.wait_ge(s["brow_loaded"], 16 * (l + 1))
                    for i, last in turns(pool, NT, U):
                        for k in range(U):
                            pool.wait_ge(s["x_loaded"][k], 16 * (i + 1))
                            nc.gpsimd.tensor_tensor(xring[0:TN, k, :], xring[0:TN, k, :], brow[0:TN, :], ALU.add
                                                    ).then_inc(s["x_added"], 1)

        @block.vector
        def _(dve):
            chain = [0]

            def link(ins):
                chain[0] += 1
                ins.then_inc(dve_step, 1)
                dve.wait_ge(dve_step, chain[0])

            def gate(sm, value):
                dve.wait_ge(sm, value)
                dve.sem_inc(dve_gate, 1)

            def floor(dst_f_, y, as_int):
                link(nc.vector.tensor_copy(as_int, y))
                link(nc.vector.tensor_copy(dst_f_, as_int))
                link(nc.vector.tensor_tensor(y, dst_f_, y, ALU.is_gt))
                link(nc.vector.tensor_tensor(dst_f_, dst_f_, y, ALU.subtract))

            link(nc.vector.memset(rows_i[:, 0:2, :], 0))
            nc.vector.memset(rows_i[:, 2, :], PAD_DST).then_inc(pads_set, 1)
            dve.wait_ge(dst_loaded, 16)
            link(nc.vector.tensor_copy(dst_f, dst_i))
            link(nc.vector.tensor_scalar(d_y, dst_f, 0.5, 1.0 / TN, ALU.add, ALU.mult))
            floor(d_hi, d_y, d_i)
            link(nc.vector.scalar_tensor_tensor(out=d_lo, in0=d_hi, scalar=-float(TN), in1=dst_f, op0=ALU.mult, op1=ALU.add))
            dve.wait_ge(edges_loaded, 16 * 6)
            link(nc.vector.scalar_tensor_tensor(out=ev_rows[:, :, 0], in0=rows_i[:, 0, :], scalar=float(R),
                                                in1=rows_i[:, 1, :], op0=ALU.mult, op1=ALU.add))
            link(nc.vector.tensor_copy(ev_rows[:, :, 1], rows_i[:, 1, :]))
            nc.vector.tensor_copy(ev_rows[:, :, 2], rows_i[:, 2, :]).then_inc(etab_src, 1)

            dve.wait_ge(consts_ready, 1)
            with dve.Fori(0, NT) as t:
                for half, n in ((0, HA), (1, HB)):
                    off = t * HCH + half * HA
                    dve.wait_ge(hot_used, 2 * t + half + 1)
                    nc.vector.tensor_tensor(hhi[half][:, 0:n, :], d_hi[:, bass.ds(off, n)].unsqueeze(2).to_broadcast([TN, n, NT]),
                                            small[0:TN, c_it].unsqueeze(1).to_broadcast([TN, n, NT]), ALU.is_equal)
                    nc.vector.tensor_tensor(hlo[half][:, 0:n, :], d_lo[:, bass.ds(off, n)].unsqueeze(2).to_broadcast([TN, n, TN]),
                                            iota_n[0:TN, :].unsqueeze(1).to_broadcast([TN, n, TN]), ALU.is_equal
                                            ).then_inc(hot_ready, 1)
            dve.wait_ge(counts_done, 1)
            nc.vector.tensor_copy(small[0:TN, c_cnt], bank[7][0:TN, 0:NT]).then_inc(cnt_ready, 1)
            dve.wait_ge(sums_done, 1)
            cnt, tot, inc, rp, y, f, St = (small[:, c] for c in (c_cnt, c_tot, c_inc, c_rp, c_y, c_f, c_St))
            link(nc.vector.tensor_copy(tot, bank[6][:, 32:32 + NT]))
            link(nc.vector.memset(y, 1.0))
            link(nc.vector.tensor_tensor_scan(inc, y, tot, 0.0, ALU.mult, ALU.add))
            link(nc.vector.tensor_tensor(inc, inc, tot, ALU.subtract))
            link(nc.vector.tensor_tensor(rp[0:TN], inc[0:TN], bank[6][0:TN, 0:NT], ALU.add))
            link(nc.vector.tensor_scalar(y, inc, 1.0 / P, None, ALU.mult))
            floor(f, y, St.bitcast(I32))
            link(nc.vector.tensor_tensor(St, f, small[:, c_it], ALU.add))
            hit = pen[0:ROWS, 0:RC * (NT - 1)].rearrange("r (c t) -> r c t", c=RC)
            sio, ts, is_, t8, tn, ta = (small[0:ROWS, c] for c in (c_sio, c_ts, c_is, c_t8, c_tn, c_ta))
            link(nc.vector.tensor_tensor(hit, St[0:ROWS, 1:NT].unsqueeze(1).to_broadcast([ROWS, RC, NT - 1]),
                                         sio.unsqueeze(2).to_broadcast([ROWS, RC, NT - 1]), ALU.is_le))
            link(nc.vector.tensor_reduce(ts, hit, AX.X, ALU.add))
            link(nc.vector.tensor_tensor(ta, sio, ts, ALU.subtract))
            nc.vector.tensor_copy(is_.bitcast(I32), ta).then_inc(steps_ready, 1)
            n_ = slice(0, TN)
            link(nc.vector.tensor_tensor(rp[n_], rp[n_], small[n_, c_t125], ALU.add))
            link(nc.vector.tensor_tensor(rp[n_], rp[n_], small[n_, c_trash], ALU.subtract))
            link(nc.vector.tensor_scalar(y[n_], cnt[n_], 0.0, None, ALU.is_gt))
            link(nc.vector.tensor_tensor(rp[n_], rp[n_], y[n_], ALU.mult))
            link(nc.vector.tensor_tensor(rp[n_], rp[n_], small[n_, c_trash], ALU.add))
            nc.vector.tensor_copy(start_at[n_, :], rp[n_]).then_inc(start_ready, 1)

            link(nc.vector.tensor_scalar(t8, ts, KEY, None, ALU.mult))
            link(nc.vector.tensor_scalar(tn, ts, float(TN), None, ALU.mult))
            dve.wait_ge(ev_gathered, 16 * RC)
            link(nc.vector.tensor_copy(ta, ts))
            link(nc.vector.tensor_copy(rel[0:ROWS, :].rearrange("r (c j) -> r c j", c=RC), ev[:, :, :, 1]))
            link(nc.vector.tensor_tensor(key.rearrange("r (c j) -> r c j", c=RC), ev[:, :, :, 2],
                                         t8.unsqueeze(2).to_broadcast([ROWS, RC, P]), ALU.add))
            link(nc.vector.tensor_tensor(ev[:, :, :, 2], ev[:, :, :, 2],
                                         tn.unsqueeze(2).to_broadcast([ROWS, RC, P]), ALU.subtract))
            NQ = R * HM
            ends = small[0:ROWS, c_ends]
            link(nc.vector.tensor_copy(ends[:, 0:NQ], key[:, 0:1].to_broadcast([ROWS, NQ])))
            nc.vector.tensor_copy(ends[:, NQ:2 * NQ], key[:, RL - 1:RL].to_broadcast([ROWS, NQ])).then_inc(rows_ready, 1)
            r_ = slice(0, ROWS)
            link(nc.vector.memset(pen[r_, :], 0.0))
            link(nc.vector.tensor_tensor(pen[r_, 1:RL], key[:, 1:RL], key[:, 0:RL - 1], ALU.not_equal))
            link(nc.vector.tensor_scalar(same[r_, :], pen[r_, 0:RL], -1.0, 1.0, ALU.mult, ALU.add))
            link(nc.vector.tensor_scalar(pen[r_, :], pen[r_, :], -BIG, None, ALU.mult))
            dve.wait_ge(turned, 1)
            link(nc.vector.tensor_copy(row_idx[:, :].rearrange("p (r c) -> p c r", c=RC),
                                       bank[0][:, 0:STEPS].rearrange("p (c r) -> p c r", c=RC)))
            link(nc.vector.tensor_copy(dloc[:, 0:STEPS].rearrange("p (r c) -> p c r", c=RC),
                                       bank[1][:, 0:STEPS].rearrange("p (c r) -> p c r", c=RC)))
            link(nc.vector.memset(dloc[:, STEPS:], -1.0))
            for l in range(2):
                link(nc.vector.tensor_scalar(acc_at[:, l, :], bank[2][0:RC, 0:ROWS], float(ROWW[l]), None, ALU.mult))
            k0, k1 = bank[3][0:NQ, 0:ROWS], bank[3][0:NQ, P:P + ROWS]
            link(nc.vector.memset(flag[:, :, :], 0.0))
            link(nc.vector.tensor_copy(flag[:, RUN, 0:ROWS], k1))
            link(nc.vector.tensor_tensor(flag[:, EQ, 1:ROWS], k0[:, 1:ROWS], flag[:, RUN, 0:ROWS - 1], ALU.is_equal))
            link(nc.vector.tensor_tensor(flag[:, UNI, 0:ROWS], k0, flag[:, RUN, 0:ROWS], ALU.is_equal))
            link(nc.vector.tensor_tensor(flag[:, CONT, 0:ROWS], flag[:, UNI, 0:ROWS], flag[:, EQ, 0:ROWS], ALU.mult))
            link(nc.vector.tensor_tensor(flag[:, CONTPEN_B, 0:ROWS], flag[:, UNI, 0:ROWS], flag[:, EQ, 1:ROWS + 1], ALU.mult))
            for a, b in ((EQPEN, EQ), (CONTPEN, CONT), (CONTPEN_B, CONTPEN_B)):
                link(nc.vector.tensor_scalar(flag[:, a, :], flag[:, b, :], -1.0, BIG, ALU.add, ALU.mult))
            dve.sem_inc(lanes_ready, 1)

            for l in range(2):
                s = LS[l]
                H = HEADS[l]
                HW = HWS[l]
                RWL = ROWW[l]
                if l == 1:
                    for i in range(3):
                        dve.wait_ge(LS[0]["h_stored"][i], 16 * (1 + (NT // U) * PAT.count(i)))
                nc.vector.memset(ring[0:TN, 0:U, 0:RWL].rearrange("p u (h w) -> p u h w", h=H)[:, :, :, D // H:HW], 1.0
                                 ).then_inc(s["ones_set"], 1)

                dve.wait_ge(s["q_loaded"], 16 * (l + 1))
                raw = qf_raw[:, 0:RL * R * H].rearrange("r (x q) -> r q x", q=R * H)
                c_in = small[0:ROWS, c_carry]
                c_out = small[0:ROWS, c_last]
                for q in range(R * H):
                    link(nc.vector.tensor_tensor_scan(qf[:, q, :], same[0:ROWS, :], raw[:, q, :], 0.0, ALU.mult, ALU.add))
                nc.vector.tensor_copy(c_out[:, 0:R * H], qf[:, 0:R * H, RL - 1]).then_inc(s["qend_ready"], 1)
                dve.wait_ge(s["qend_turned"], l + 1)
                fl = flag[0:R * H]
                link(nc.vector.tensor_tensor_scan(fl[:, RUN, 0:ROWS], fl[:, CONT, 0:ROWS], bank[7][0:R * H, 256:256 + ROWS],
                                                  0.0, ALU.mult, ALU.add))
                link(nc.vector.memset(fl[:, CARRY, 0:1], 0.0))
                nc.vector.tensor_tensor(fl[:, CARRY, 1:ROWS], fl[:, RUN, 0:ROWS - 1], fl[:, EQ, 1:ROWS], ALU.mult
                                        ).then_inc(s["qcarry_ready"], 1)
                dve.wait_ge(s["qcarry_turned"], l + 1)
                link(nc.vector.tensor_copy(c_in[:, 0:R * H], bank[7][0:ROWS, 384:384 + R * H]))
                dve.sem_inc(s["qcarry_taken"], 1)
                for q in range(R * H):
                    link(nc.vector.tensor_tensor_scan(qf[:, q, :], same[0:ROWS, :], raw[:, q, :], c_in[:, q:q + 1],
                                                      ALU.mult, ALU.add))
                for r in range(R):
                    link(nc.vector.scalar_tensor_tensor(
                        out=qf[:, r * H:(r + 1) * H, :], in0=rel[0:ROWS, :].unsqueeze(1).to_broadcast([ROWS, H, RL]),
                        scalar=float(r), in1=qf[:, r * H:(r + 1) * H, :], op0=ALU.is_equal, op1=ALU.mult))
                al = alpha[:, 0:H, :]
                link(nc.vector.tensor_tensor(al, qf[:, 0:H, :], qf[:, H:2 * H, :], ALU.add))
                for r in range(2, R):
                    link(nc.vector.tensor_tensor(al, al, qf[:, r * H:(r + 1) * H, :], ALU.add))
                for h in range(H):
                    dve.wait_ge(s["k_turned"], HM * l + h + 1)
                    link(nc.vector.tensor_tensor(alpha[:, h, :], alpha[:, h, :], bank[h][0:ROWS, :], ALU.add))
                link(nc.vector.scalar_tensor_tensor(out=al, in0=al, scalar=SLOPE, in1=al, op0=ALU.mult, op1=ALU.max))
                fl = flag[0:H]
                for w in range(2):
                    def scan(h, first):
                        if w == 0:
                            return nc.vector.tensor_tensor_scan(amax[:, h, :], pen[0:ROWS, 0:RL], alpha[:, h, :],
                                                                first, ALU.add, ALU.max)
                        return nc.vector.tensor_tensor_scan(amax[:, h, ::-1], pen[0:ROWS, RL:0:-1], amax[:, h, ::-1],
                                                            first, ALU.add, ALU.max)
                    for h in range(H):
                        link(scan(h, -BIG))
                    nc.vector.tensor_copy(c_out[:, 0:H], amax[:, 0:H, RL - 1 if w == 0 else 0]).then_inc(s["end_ready"], 1)
                    dve.wait_ge(s["end_turned"], 2 * l + w + 1)
                    turned_ends = bank[4 + w][0:H, 0:ROWS]
                    if w == 0:
                        link(nc.vector.tensor_tensor_scan(fl[:, RUN, 0:ROWS], fl[:, CONTPEN, 0:ROWS], turned_ends,
                                                          -BIG, ALU.add, ALU.max))
                        link(nc.vector.memset(fl[:, CARRY, 0:1], -BIG))
                        last = nc.vector.tensor_tensor(fl[:, CARRY, 1:ROWS], fl[:, RUN, 0:ROWS - 1],
                                                       fl[:, EQPEN, 1:ROWS], ALU.add)
                    else:
                        link(nc.vector.tensor_tensor_scan(fl[:, RUN, ROWS - 1::-1], fl[:, CONTPEN_B, ROWS - 1::-1],
                                                          turned_ends[:, ::-1], -BIG, ALU.add, ALU.max))
                        link(nc.vector.memset(fl[:, CARRY, ROWS - 1:ROWS], -BIG))
                        last = nc.vector.tensor_tensor(fl[:, CARRY, 0:ROWS - 1], fl[:, RUN, 1:ROWS],
                                                       fl[:, EQPEN, 1:ROWS], ALU.add)
                    last.then_inc(s["carry_ready"], 1)
                    dve.wait_ge(s["carry_turned"], 2 * l + w + 1)
                    link(nc.vector.tensor_copy(c_in[:, 0:H], bank[6 + w][0:ROWS, 0:H]))
                    for h in range(H):
                        link(scan(h, c_in[:, h:h + 1]))
                nc.vector.tensor_tensor(al, al, amax[:, 0:H, :], ALU.subtract).then_inc(s["diff_ready"], 1)
                for h in range(H):
                    dve.wait_ge(s["e_turned"], HM * l + h + 1)
                    link(nc.vector.tensor_copy(wE[:, 0:STEPS, h].rearrange("p (r c) -> p c r", c=RC),
                                               bank[h][:, 0:STEPS].rearrange("p (c r) -> p c r", c=RC)))
                link(nc.vector.memset(wE[:, STEPS:, :], 0.0))
                dve.sem_inc(s["w_ready"], 1)

                nc.vector.memset(big[0:TN, 0:ACCW // 2], 0.0).then_inc(s["sums_zeroed"], 1)
                dve.sem_inc(s["sum_added"], AHEAD)
                dve.wait_ge(s["dT_turned"], U + NT)

                def one_hot(st, slot):
                    at = dloc[:, bass.ds(st, 1)]
                    if H > 1:
                        dve.wait_ge(s["S_built"], st + 1)
                        nc.vector.tensor_scalar(hot[:, slot, :], iota_n[:, :], at, None, ALU.is_equal
                                                ).then_inc(s["hot_built"], 1)
                    else:
                        dve.wait_ge(s["step_done"], st + 1 + GS - AHEAD)
                        nc.vector.tensor_scalar(S[:, slot, 0, :], iota_n[:, :], at,
                                                wE[:, bass.ds(st, 1), 0:1].rearrange("p a b -> p (a b)"),
                                                ALU.is_equal, ALU.mult).then_inc(s["hot_built"], 1)

                for j in range(AHEAD):
                    one_hot(j, j)
                dve.wait_ge(s["sums_zeroed"], 2 * (l + 1))
                with dve.Fori(0, STEPS // GS) as i:
                    for j in range(GS):
                        st = GS * i + j
                        one_hot(st + AHEAD, j % AHEAD)
                        at = dve.value_load(acc_at[j % RC:j % RC + 1, l, bass.ds(i * (GS // RC) + j // RC, 1)],
                                            min_val=0, max_val=(NT - 1) * RWL)
                        dve.wait_ge(s["step_done"], GS + st + 1)
                        dve.wait_ge(s["sum_added"], AHEAD + st)
                        tile = big[0:TN, bass.ds(at, RWL)].rearrange("p (a w) -> p a w", a=2)
                        nc.vector.tensor_tensor(tile, tile, banks[0:TN, 2 * (j % AHEAD):2 * (j % AHEAD) + 2, 0:RWL // 2],
                                                ALU.add).then_inc(s["sum_added"], 1)

                dve.wait_ge(s["sum_added"], AHEAD + STEPS)
                z = small[0:TN, c_z][:, 0:NT * H]
                link(nc.vector.tensor_scalar(z.rearrange("p (t h) -> p t h", h=H),
                                             big[0:TN, 0:NT * RWL].rearrange("p (t h w) -> p t h w", t=NT, h=H)[:, :, :, D // H],
                                             SOFTMAX_EPS, None, ALU.add))
                link(nc.vector.reciprocal(z, z))
                dve.wait_ge(s["brow_loaded"], 16 * (l + 1))

                def divide(t, add):
                    for h in range(H):
                        u = node_sum(l, t)[:, h, :]
                        last = nc.vector.scalar_tensor_tensor(out=u, in0=u, scalar=z[:, bass.ds(t * H + h, 1)],
                                                              in1=add[:, h * (D // H):(h + 1) * (D // H)],
                                                              op0=ALU.mult, op1=ALU.add)
                    return last

                if l == 0:
                    divide(0, brow[0:TN, :]).then_inc(s["u_ready"], 1)
                    for i, last_turn in turns(dve, NT, U):
                        for k in range(U):
                            t = U * i + k
                            if k < U - 1 or not last_turn:
                                divide(t + 1, brow[0:TN, :]).then_inc(s["u_ready"], 1)
                            dve.wait_ge(s["exp_ready"], t + 1)
                            nc.vector.scalar_tensor_tensor(out=xring[0:TN, PAT[k], :], in0=ring[0:TN, PAT[k], 0:D], scalar=1.0,
                                                           in1=xring[0:TN, PAT[k], :], op0=ALU.min, op1=ALU.add
                                                           ).then_inc(s["h_ready"], 1)
                else:
                    dve.sem_inc(s["x_used"], U)
                    stats = same[0:TN, 0:12 * NT].rearrange("p (t a) -> p t a", a=12)
                    mv = small[0:TN, c_mv].rearrange("p (t a) -> p t a", a=2)
                    for i, last_turn in turns(dve, NT, U):
                        for k in range(U):
                            t = U * i + k
                            dve.wait_ge(s["x_added"], t + 1)
                            divide(t, xring[0:TN, k, :]).then_inc(s["x_used"], 1)
                            gate(s["x_used"], U + t + 1)
                            for half in range(2):
                                nc.vector.bn_stats(stats[:, bass.ds(t, 1), 6 * half:6 * half + 6].rearrange("p a b -> p (a b)"),
                                                   node_sum(l, t)[:, 0, half * HALF:(half + 1) * HALF]).then_inc(s["e_set"], 1)
                    dve.wait_ge(s["e_set"], 2 * NT)
                    for t in range(NT):
                        link(nc.vector.bn_aggr(mv[:, t, :], stats[:, t, :].rearrange("p (a b) -> p a b", a=2)))
                    link(nc.vector.tensor_scalar(mv[:, :, 1], mv[:, :, 1], NORM_EPS, None, ALU.add))
                    dve.sem_inc(s["u_ready"], 1)
                    dve.wait_ge(s["exp_ready"], 1)
                    link(nc.vector.reciprocal(mv[:, :, 1], mv[:, :, 1]))
                    link(nc.vector.scalar_tensor_tensor(out=mv[:, :, 0], in0=mv[:, :, 0], scalar=-1.0, in1=mv[:, :, 1],
                                                        op0=ALU.mult, op1=ALU.mult))
                    dve.sem_inc(s["h_ready"], 1)


_INS = ["x", "src", "dst", "edge_type_3", "L0_gnn_W1", "L0_gnn_q1", "L0_gnn_k1", "L0_gnn_b1",
        "L0_gnn_W2", "L0_gnn_q2", "L0_gnn_k2", "L0_gnn_b2"]


def kernel(**inputs):
    import numpy as np
    import concourse.bacc as bacc
    from concourse.bass_utils import run_bass_kernel_spmd

    nc = bacc.Bacc("TRN2", target_bir_lowering=False, num_devices=1)
    arrays, args = {}, []
    for name in _INS:
        a = np.ascontiguousarray(inputs[name])
        arrays[f"in_{name}"] = a
        args.append(nc.dram_tensor(f"in_{name}", a.shape, mybir.dt.from_np(a.dtype), kind="ExternalInput").ap())
    shape = inputs["x"].shape
    args.append(nc.dram_tensor("out_0", shape, F32, kind="ExternalOutput").ap())
    rgat_kernel(nc, *args)
    r = run_bass_kernel_spmd(nc, [arrays], core_ids=[0])
    return r.results[0]["out_0"]
```

```python
from contextlib import ExitStack

import concourse.bass as bass
from concourse import mybir

F32 = mybir.dt.float32
BF16 = mybir.dt.bfloat16
I32 = mybir.dt.int32
ALU = mybir.AluOpType
ACT = mybir.ActivationFunctionType
AX = mybir.AxisListType

P = 128
BIG = 1.0e38
SLOPE = 0.2
SOFTMAX_EPS = 1e-16
NORM_EPS = 1e-5


def rgat_kernel(nc, x, src, dst, etype, W1, q1, k1, b1, W2, q2, k2, b2, out):
    N, D = x.shape
    E = src.shape[0]
    R = W1.shape[0]
    DC = D // P
    HALF = D // 2
    TN = 125
    NT = N // TN
    assert NT * TN == N and DC * P == D
    ETILES = -(-E // P)
    STEPS = E // P + NT
    RC = 4
    ROWS = STEPS // RC
    RL = RC * P
    assert ROWS * RC == STEPS and ROWS <= P
    EROWS = ETILES // RC
    assert EROWS * RC == ETILES
    LAST = E - (EROWS - 1) * RL
    PAD_DST = 32 * TN
    KEY = 8192.0
    HCOLS = E // TN
    HROUNDS = HCOLS // NT
    HPARTS = [NT // 3 + (1 if i < NT % 3 else 0) for i in range(3)]
    assert HCOLS * TN == E and HROUNDS * NT == HCOLS and HROUNDS == R * DC - 1
    ORDER_P = max(d for d in range(1, TN + 1) if (E - 1) % d == 0)
    ORDER_C = (E - 1) // ORDER_P
    AHEAD = 4
    GS = 8
    KG = 11
    assert STEPS % GS == 0 and STEPS % (2 * KG) == 0
    U = 5
    WT = R * DC
    assert NT % U == 0 and NT // U >= R + 2 and DC % 3 == 0 and DC % 2 == 0
    PAT = [0, 1, 2, 0, 1]
    HEADS = [q1.shape[1], q2.shape[1]]
    HM = max(HEADS)
    HWS = [D // h + (1 if h > 1 else 2) for h in HEADS]
    ROWW = [h * w for h, w in zip(HEADS, HWS)]
    RW = max(ROWW)
    NQK = 2 * R * HM
    PIECE = D // HM
    HC0 = [w if h > 1 else PIECE for h, w in zip(HEADS, HWS)]
    UNIT = [(0, PIECE, HALF - PIECE)] + [(r, h * HALF, HALF) for r in range(R) for h in range(2)][1:]
    UNITS = len(UNIT)
    DBANKS = 5
    assert HEADS[1] == 1 and HEADS[0] == HM and U * UNITS % DBANKS == 0 and UNITS == 2 * R
    LAYERS = [(W1, q1, k1, b1), (W2, q2, k2, b2)]

    etab = nc.dram_tensor("edge_table", (ETILES * P, 3), F32, kind="Internal").ap()
    qfill = [nc.dram_tensor(f"q_fill{l}", (STEPS * P + N, R * HEADS[l]), F32, kind="Internal").ap() for l in range(2)]
    ktab = [nc.dram_tensor(f"k_table{l}", (N * R, HEADS[l]), F32, kind="Internal").ap() for l in range(2)]
    xrtab = [nc.dram_tensor(f"xr_table{l}", (N * R, ROWW[l]), F32, kind="Internal").ap() for l in range(2)]
    cursor = nc.dram_tensor("cursor", (N + P, 1), F32, kind="Internal").ap()
    hid = nc.dram_tensor("hidden", (N, D), F32, kind="Internal").ap()

    ctx = ExitStack()
    with ctx:
        def sb(name, shape, dt=F32):
            return ctx.enter_context(nc.sbuf_tensor(name, shape, dt))

        def sem(name):
            return ctx.enter_context(nc.semaphore(name))

        banks = ctx.enter_context(nc.psum_tensor("banks", [P, 8, 512], F32))
        bank = [banks[:, i, :] for i in range(8)]

        ACCW = NT * RW
        big = sb("big", [P, ACCW])
        wsb = sb("wsb", [P, DC, NQK + R * D])
        ring = sb("ring", [P, GS, RW])
        xring = sb("xring", [P, U, D])
        xT = sb("xT", [P, 3, DC, P])
        E_BANK = [5, 0, 1, 2]
        qk_node = sb("qk_node", [P, NT, 2 * R * HM])
        qkw = sb("qkw", [P, DC, 2, HM])
        row_idx = sb("row_idx", [P, STEPS], I32)
        dloc = sb("dloc", [P, STEPS + AHEAD])
        wE = sb("wE", [P, STEPS + AHEAD, HM])
        acc_at = sb("acc_at", [RC, 2, ROWS], I32)
        ev = wE[0:ROWS, 0:RC * P * 3 // HM, :].rearrange("r a b -> r (a b)").rearrange("r (c j a) -> r c j a", c=RC, a=3)
        rel = sb("rel", [P, RL])
        pen = sb("pen", [P, RL + 1])
        same = sb("same", [P, RL])
        flag = sb("flag", [R * HM, 8, ROWS + 1])
        EQ, EQPEN, CONT, CONTPEN, CARRY, CONTPEN_B, UNI, RUN = range(8)
        brow = sb("brow", [P, D])
        ident = sb("ident", [P, P])
        iota_n = sb("iota_n", [P, TN])
        start_at = sb("start_at", [P, NT], I32)
        kidx = sb("kidx", [P, 2, KG], I32)
        gidx = sb("gidx", [P, 2, GS // 2], I32)
        small = sb("small", [P, 512])

        zeros = big[:, 0:STEPS * R * HM]
        qf_raw = big[0:ROWS, 0:RL * R * HM]
        o = RL * R * HM
        qf = big[0:ROWS, o:o + RL * R * HM].rearrange("r (q x) -> r q x", x=RL)
        rows_i = big[0:EROWS, o:o + 3 * RL].bitcast(I32).rearrange("r (a x) -> r a x", a=3)
        ev_rows = big[0:EROWS, o + 3 * RL:o + 6 * RL].rearrange("r (x a) -> r x a", a=3)
        o1 = o + 6 * RL
        dst_i = big[0:TN, o1:o1 + HCOLS].bitcast(I32)
        dst_f = big[0:TN, o1 + HCOLS:o1 + 2 * HCOLS]
        d_y = big[0:TN, o1 + 2 * HCOLS:o1 + 3 * HCOLS]
        d_i = big[0:TN, o1 + 3 * HCOLS:o1 + 4 * HCOLS].bitcast(I32)
        d_hi = big[0:TN, o1 + 4 * HCOLS:o1 + 5 * HCOLS]
        d_lo = big[0:TN, o1 + 5 * HCOLS:o1 + 6 * HCOLS]
        o1 += 6 * HCOLS
        d_this = big[0:ORDER_P, o1:o1 + ORDER_C].bitcast(I32)
        d_next = big[0:ORDER_P, o1 + ORDER_C:o1 + 2 * ORDER_C].bitcast(I32)
        d_falls = big[0:ORDER_P, o1 + 2 * ORDER_C:o1 + 3 * ORDER_C]
        o += RL * R * HM
        ALPHA_AT = o
        alpha = big[0:ROWS, o:o + HM * RL].rearrange("r (h x) -> r h x", h=HM)
        o += HM * RL
        AMAX_AT = o
        amax = big[0:ROWS, o:o + HM * RL].rearrange("r (h x) -> r h x", h=HM)
        o += HM * RL
        K_AT = o
        k_edge = big[:, o:o + STEPS * HM]
        o += STEPS * HM
        s_before, s_equal, s_row, s_count = (k_edge[:, i * P:(i + 1) * P] for i in range(4))
        s_rowi = k_edge[:, 4 * P:5 * P].bitcast(I32)
        s_edge = k_edge[:, 5 * P:5 * P + 3]
        s_int = k_edge[:, 5 * P + 4:5 * P + 7].bitcast(I32)
        s_rank, s_base, s_pos, s_new, s_at, s_last, s_lane = (k_edge[:, 5 * P + 8 + i:5 * P + 9 + i] for i in range(7))
        kring = big[:, o:o + 2 * KG * HM]
        o += 2 * KG * HM
        key = big[0:ROWS, o:o + RL]
        assert o + RL <= ACCW
        deviation = same[0:TN, 14 * U:15 * U]
        xt_flat = xring[:, :, :].rearrange("p u d -> p (u d)")
        S = xt_flat[:, 0:AHEAD * HM * TN].rearrange("p (s h n) -> p s h n", s=AHEAD, h=HM)
        hot = xt_flat[:, AHEAD * HM * TN:AHEAD * (HM + 1) * TN].rearrange("p (s n) -> p s n", s=AHEAD)
        hlo = [ring[0:TN, i, 0:640].bitcast(BF16)[:, 0:HPARTS[0] * TN].rearrange("p (a n) -> p a n", n=TN) for i in range(3)]
        hhi = [ring[0:TN, 3, i * 128:(i + 1) * 128].bitcast(BF16)[:, 0:HPARTS[0] * NT].rearrange("p (a n) -> p a n", n=NT)
               for i in range(3)]
        zero_bf = ring[0:TN, 4, 0:64].bitcast(BF16)
        below = same[0:TN, 0:TN]
        ones = same[0:TN, P:2 * P]
        counts = same[0:NT, 2 * P:2 * P + TN]
        q2_row, k2_row = xring[:, 3, :], xring[:, 4, :]

        def w_cols(r, first, n):
            return wsb[:, :, NQK + r * D + first:NQK + r * D + first + n]

        def qk_cols(l):
            n = 2 * R * HEADS[l]
            return wsb[:, :, NQK - n:NQK].rearrange("p c (a r h) -> p c a r h", a=2, r=R)

        def turned_chunks(pair):
            return banks[:, 2 * pair:2 * pair + 2, :].rearrange("p b x -> p (b x)")[:, 0:DC * P]

        def cols(n, _at=[0]):
            _at[0] += n
            assert _at[0] <= 512
            return slice(_at[0] - n, _at[0])

        c_cnt, c_tot = cols(NT + 1), cols(NT + 1)
        c_inc, c_rp, c_y, c_f, c_St, c_cur = (cols(NT) for _ in range(6))
        c_it, c_t125, c_trash = (cols(NT) for _ in range(3))
        c_sio, c_ts, c_is, c_t8, c_tn, c_ta = (cols(RC) for _ in range(6))
        c_ends = cols(2 * R * HM)
        c_last = cols(R * HM)
        c_carry = cols(R * HM)
        c_z = cols(NT * HM)
        c_mv = cols(2 * NT)
        c_w2 = cols(2 * DC)

        dve_step, pool_step, act_gate, pool_gate, dve_gate = (sem(n) for n in
            ("dve_step", "pool_step", "act_gate", "pool_gate", "dve_gate"))
        consts_ready, edges_loaded, pads_set, dst_loaded, qk_loaded = (sem(n) for n in
            ("consts_ready", "edges_loaded", "pads_set", "dst_loaded", "qk_loaded"))
        zeros_set, fills_zeroed, hot_ready, hot_used, counts_done, sums_done = (sem(n) for n in
            ("zeros_set", "fills_zeroed", "hot_ready", "hot_used", "counts_done", "sums_done"))
        cnt_ready, etab_src, etab_stored, steps_ready, ev_gathered, rows_ready, turned, lanes_ready = (sem(n) for n in
            ("cnt_ready", "etab_src", "etab_stored", "steps_ready", "ev_gathered", "rows_ready", "turned", "lanes_ready"))
        start_ready, cursor_ready, sort_step, sort_moved = (sem(n) for n in
            ("start_ready", "cursor_ready", "sort_step", "sort_moved"))
        
        shared = {n: sem(n) for n in
                  ("ones_set q_scattered q_loaded k_stored k_ready qend_ready qend_turned qcarry_ready qcarry_turned "
                   "qcarry_taken k_added turned_taken w0_loaded end_ready end_turned carry_ready carry_turned diff_ready e_ready w_ready sums_zeroed "
                   "brow_loaded w_loaded k_turned e_turned x_used x_added S_built").split()}
        for n in ("x_loaded", "drow_loaded"):
            shared[n] = [sem(f"{n}{i}") for i in range(U)]
        w2_ready = sem("w2_ready")
        halves_set, w2_used, var_ready, dev_ready = (sem(n) for n in ("halves_set", "w2_used", "var_ready", "dev_ready"))
        w2_loaded = [sem(f"w2_loaded{i}") for i in range(2)]
        LS = []
        for l in range(2):
            s = {n: sem(f"{n}_{l}") for n in
                 ("xT_turned xT_ready qk_done qk_copied kidx_staged k_taken dT_turned dT_ready dense_done dense_out "
                  "hot_built gidx_staged step_done sum_added h_ready e_set " + ("u_ready exp_ready" if l == 0 else "h_out")).split()}
            for n, k in (("row_loaded", U if l == 0 else 0), ("staged_stored", U), ("k_gathered", 2),
                         ("row_gathered", GS), ("half_stored", 3), ("h_stored", U if l == 0 else 3)):
                s[n] = [sem(f"{n}{i}_{l}") for i in range(k)]
            LS.append({**shared, **s})

        def heads(ap, h):
            return ap.rearrange("p (h w) -> p h w", h=h)

        def node_sum(l, t):
            return heads(big[0:TN, bass.ds(t * ROWW[l], ROWW[l])], HEADS[l])[:, :, 0:D // HEADS[l]]

        def turns(eng, total, per):
            n = total // per
            with eng.Fori(0, n - 1) as i:
                yield i, False
            yield n - 1, True

        block = ctx.enter_context(nc.Block())

        @block.sync
        def _(sp):
            sp.dma_start(dst_i, dst.rearrange("(p c) -> p c", c=HCOLS)).then_inc(dst_loaded, 16)
            W_rows = W1.rearrange("r d f -> (r d) f")

            def load_w(i, c):
                sp.wait_ge(LS[0]["xT_turned"], DC * i + c + 1)
                sp.dma_start(xring[:, c % 3, :], W_rows[bass.ds(DC * P * i + c * P, P), :]
                             ).then_inc(LS[0]["row_loaded"][c % 3], 16)

            load_w(0, 0)
            for a, arr in enumerate((q1, k1)):
                sp.dma_start(qkw[:, :, a, :], arr.rearrange("(c p) h -> p c h", p=P), allow_slow_non_contiguous=True
                             ).then_inc(qk_loaded, 16)
            for c in range(1, 3):
                load_w(0, c)
            sp.wait_ge(pads_set, 1)
            for a, arr in enumerate((src, etype, dst)):
                sp.dma_start(rows_i[0:EROWS - 1, a, :],
                             arr[0:(EROWS - 1) * RL].rearrange("(r x) -> r x", x=RL)).then_inc(edges_loaded, 16)
                sp.dma_start(rows_i[EROWS - 1:EROWS, a, 0:LAST],
                             arr[(EROWS - 1) * RL:E].rearrange("(r x) -> r x", r=1)).then_inc(edges_loaded, 16)
            sp.dma_start(d_this, dst[0:E - 1].rearrange("(p c) -> p c", c=ORDER_C)).then_inc(edges_loaded, 16)
            sp.dma_start(d_next, dst[1:E].rearrange("(p c) -> p c", c=ORDER_C)).then_inc(edges_loaded, 16)
            for c in range(3, DC):
                load_w(0, c)
            with sp.Fori(1, R) as i:
                for c in range(DC):
                    load_w(i, c)
            sp.dma_start(w_cols(0, 0, D), W1[0].rearrange("(c p) f -> p c f", p=P)).then_inc(LS[0]["w0_loaded"], 16)
            sp.dma_start(brow[0:TN, :], b1.partition_broadcast(TN)).then_inc(LS[0]["brow_loaded"], 16)

            for l in range(2):
                s = LS[l]
                H = HEADS[l]
                W0 = WT if l == 0 else 0
                table = x if l == 0 else hid
                xr_rows = xrtab[l].rearrange("(n r) w -> n r w", r=R)
                for i in range(3):
                    sp.sem_inc(s["half_stored"][i], 16)

                def store_half(t, k):
                    sp.wait_ge(s["qk_copied"], 2 + W0 + t + 1)
                    sp.dma_start(xr_rows[bass.ds(t * TN, TN), 0, 0:HC0[l]], ring[0:TN, 5 + PAT[k], 0:HC0[l]]
                                 ).then_inc(s["half_stored"][PAT[k]], 16)

                if l == 0:
                    def load_x(t, k):
                        sp.wait_ge(s["xT_turned"], WT + t + 1)
                        sp.dma_start(xring[0:TN, k, :], x[bass.ds(t * TN, TN), :]).then_inc(s["row_loaded"][k], 16)

                    for k in range(3):
                        load_x(k, k)
                    sp.wait_ge(etab_src, 1)
                    sp.dma_start(etab.rearrange("(r x) a -> r x a", x=RL), ev_rows).then_inc(etab_stored, 16)
                    for i, last in turns(sp, NT, U):
                        for k in range(U):
                            if not last or k + 3 < U:
                                load_x(U * i + k + 3, (k + 3) % U)
                            store_half(U * i + k, k)
                else:
                    for k in range(U):
                        sp.sem_inc(LS[0]["h_stored"][k], 16)
                    for i, last in turns(sp, NT, U):
                        for k in range(U):
                            t = U * i + k
                            sp.wait_ge(LS[0]["h_ready"], 2 + t + 1)
                            sp.dma_start(hid[bass.ds(t * TN, TN), :], xring[0:TN, k, :]).then_inc(LS[0]["h_stored"][k], 16)
                            store_half(t, k)
                for i in range(U):
                    sp.sem_inc(s["staged_stored"][i], 16)

                def load_dense(n, k):
                    sp.wait_ge(s["dT_turned"], n + 1)
                    sp.dma_start(xring[0:TN, PAT[k], :], table[bass.ds(n * TN, TN), :]).then_inc(s["drow_loaded"][k], 16)

                for k in range(2):
                    sp.wait_ge(s["xT_turned"], (3 if l == 0 else U) + W0 + NT - U + k + 1)
                    if l == 1:
                        sp.wait_ge(LS[0]["h_stored"][k], 16 * (1 + NT // U))
                    load_dense(k, k)
                sp.wait_ge(s["qk_copied"], 2 + W0 + NT)
                sp.dma_start(ktab[l].rearrange("(t p r) h -> p t (r h)", p=TN, r=R),
                             qk_node[0:TN, :, R * H:2 * R * H]).then_inc(s["k_stored"], 16)
                sp.wait_ge(s["xT_turned"], (3 if l == 0 else U) + W0 + NT)
                if l == 1:
                    for k in range(2, U):
                        sp.wait_ge(LS[0]["h_stored"][k], 16 * (1 + NT // U))
                sp.wait_ge(s["q_scattered"], 16 * NT * (l + 1))
                sp.dma_start(qf_raw[:, 0:RL * R * H], qfill[l][0:STEPS * P, :].rearrange("(r x) q -> r (x q)", x=RL)
                             ).then_inc(s["q_loaded"], 16)
                if l == 0:
                    for row, arr in ((q2_row, q2), (k2_row, k2)):
                        sp.dma_start(row, arr.rearrange("f h -> (f h)").partition_broadcast(P)).then_inc(qk_loaded, 16)
                else:
                    sp.dma_start(brow[0:TN, :], b2.partition_broadcast(TN)).then_inc(s["brow_loaded"], 16)
                for i in range(3):
                    sp.wait_ge(s["half_stored"][i], 16 * (1 + (NT // U) * PAT.count(i)))
                W2_rows = W2.rearrange("r d f -> (r d) f")

                def load_w2(r, c):
                    sp.wait_ge(w2_used, 2 * (DC * r + c + 1))
                    sp.dma_start(ring[:, 5 + c % 2, 0:D], W2_rows[bass.ds(D * r + c * P, P), :]).then_inc(w2_loaded[c % 2], 16)

                def dense_turn(i, last=False, w2_tile=None):
                    for k in range(U):
                        if not last or k + 2 < U:
                            load_dense(U * i + k + 2, (k + 2) % U)
                        for r in range(R):
                            unit = R * k + r
                            first = HC0[l] if r == 0 else 0
                            sp.wait_ge(s["dense_out"], DBANKS + UNITS * (U * i + k) + 2 * r + 2)
                            sp.dma_start(xr_rows[bass.ds((U * i + k) * TN, TN), r, first:ROWW[l]],
                                         ring[0:TN, unit % U, first:ROWW[l]]).then_inc(s["staged_stored"][unit % U], 16)
                        if w2_tile is not None:
                            load_w2(w2_tile, k)
                            for c in range(U, DC) if k == U - 1 else ():
                                load_w2(w2_tile, c)

                dense_turn(0)
                with sp.Fori(1, 1 + R) as i:
                    dense_turn(i, w2_tile=i - 1 if l == 0 else None)
                for i in range(1 + R, NT // U):
                    dense_turn(i, i == NT // U - 1)
                if l == 0:
                    spread = STEPS // (WT + 4)
                    sp.wait_ge(s["dense_done"], UNITS * (NT + 2))
                    for r in range(R):
                        for c in range(DC):
                            sp.wait_ge(s["sum_added"], AHEAD + spread * (DC * r + c + 1))
                            sp.dma_start(w_cols(r, 0, D)[:, c, :], W2[r, c * P:(c + 1) * P, :]
                                         ).then_inc(LS[1]["w0_loaded" if r == 0 else "w_loaded"], 16)
                else:
                    for i in range(3):
                        sp.sem_inc(s["h_stored"][i], 16)

                    def load_res(t, k):
                        sp.wait_ge(s["x_used"], t + 1)
                        sp.dma_start(xring[0:TN, U - 1 - k, :], x[bass.ds(t * TN, TN), :]).then_inc(s["x_loaded"][k], 16)

                    assert AHEAD * (HM + 1) * TN <= (U - 1) * D
                    sp.wait_ge(s["dT_turned"], 2 + NT)
                    load_res(0, 0)
                    sp.wait_ge(s["sum_added"], AHEAD + STEPS)
                    for k in range(1, U):
                        load_res(k, k)
                    for i, last in turns(sp, NT, U):
                        if not last:
                            for k in range(U):
                                load_res(U * (i + 1) + k, k)
                        for k in range(U):
                            sp.wait_ge(s["h_out"], U * i + k + 1)
                            sp.dma_start(out[bass.ds((U * i + k) * TN, TN), :],
                                         ring[0:TN, 3 + PAT[k], 0:D]).then_inc(s["h_stored"][PAT[k]], 16)
                    for i in range(3):
                        sp.wait_ge(s["h_stored"][i], 16 * (1 + (NT // U) * PAT.count(i)))

        @block.tensor
        def _(pe):
            pe.wait_ge(consts_ready, 1)
            for l in range(2):
                s = LS[l]
                H = HEADS[l]
                HW = HWS[l]
                W0 = WT if l == 0 else 0

                def turn(n, xs, pair, rows):
                    pe.wait_ge(s["xT_ready"], n + 1)
                    for c in range(DC):
                        last = pe.transpose(turned_chunks(pair)[:, c * P:c * P + rows],
                                            xring[0:rows, xs, c * P:(c + 1) * P], ident[0:rows, 0:rows])
                    last.then_inc(s["xT_turned"], 1)

                def w_turn(i, c):
                    pe.wait_ge(s["row_loaded"][c % 3], 16 * (DC // 3 * i + c // 3 + 1))
                    turn(DC * i + c, c % 3, c % 3, P)

                def x_turn(i, k):
                    if l == 0:
                        pe.wait_ge(s["row_loaded"][k], 16 * ((WT // 3 if k < 3 else 0) + i + 1))
                    else:
                        pe.wait_ge(LS[0]["h_ready"], 2 + U * i + k + 1)
                    turn(W0 + U * i + k, k, PAT[k], TN)

                def products(n, pair, acc, rows, rhs, width, fresh):
                    pe.wait_ge(s["xT_ready"], n + 3)
                    pe.wait_ge(s["qk_copied"], n + 2 if fresh else n + 1)
                    for c in range(DC):
                        last = pe.matmul(bank[acc][0:rows, 0:width], xT[:, pair, c, 0:rows], rhs(c),
                                         start=(c == 0), stop=(c == DC - 1))
                    last.then_inc(s["qk_done"], 1)

                def w_rhs(c):
                    return qkw[:, c, :, :]

                def x_rhs(c):
                    return wsb[:, c, NQK - 2 * R * H:NQK + PIECE]

                def hist(n):
                    for part in range(3):
                        pe.wait_ge(hot_ready, 3 * n + part + 1)
                        for j in range(HPARTS[part]):
                            last = pe.matmul(bank[7][0:NT, 0:TN], hhi[part][:, j, :], hlo[part][:, j, :],
                                             start=False, stop=False)
                        last.then_inc(hot_used, 1)

                pe.sem_inc(s["xT_turned"], 3 if l == 0 else U)
                pe.sem_inc(s["dT_turned"], 2)
                if l == 0:
                    pe.sem_inc(hot_used, 3)
                    pe.wait_ge(qk_loaded, 32)
                    pe.matmul(bank[7][0:NT, 0:TN], zero_bf[:, 0:NT], zero_bf[:, 0:TN], start=True, stop=False)
                    w_turn(0, 0)
                    for i, last_turn in turns(pe, WT, DC):
                        for c in range(DC):
                            if c < DC - 1:
                                w_turn(i, c + 1)
                            elif not last_turn:
                                w_turn(i + 1, 0)
                            products(DC * i + c, c % 3, 6, P, w_rhs, 2 * H, True)
                            if c < DC - 1 or not last_turn:
                                hist(DC * i + c)
                    pe.matmul(bank[7][0:NT, 0:TN], zero_bf[:, 0:NT], zero_bf[:, 0:TN], start=False, stop=True
                              ).then_inc(counts_done, 1)
                    x_turn(0, 0)
                    pe.wait_ge(cnt_ready, 1)
                    pe.transpose(bank[4][0:TN, 256:256 + NT], counts, ident[0:NT, 0:NT]).then_inc(sums_done, 1)
                    pe.wait_ge(cnt_ready, 2)
                    cnt = small[0:TN, c_cnt]
                    pe.matmul(bank[5][0:TN, 320:320 + NT], below, cnt[:, 0:NT], start=True, stop=True)
                    pe.matmul(bank[5][0:P, 384:385 + NT], ones, cnt, start=True, stop=True).then_inc(sums_done, 1)
                    pe.wait_ge(cnt_ready, 3)
                else:
                    x_turn(0, 0)
                    pe.wait_ge(w2_ready, 1 + R)
                pe.wait_ge(s["w0_loaded"], 16 * (1 + DC * l))

                def x_turns(i, last_turn=False):
                    for k in range(U):
                        if k < U - 1:
                            x_turn(i, k + 1)
                        elif not last_turn:
                            x_turn(i + 1, 0)
                        products(W0 + U * i + k, PAT[k], 6 + k % 2, TN, x_rhs, 2 * R * H + PIECE, k == 0)

                MEET = 2
                with pe.Fori(0, MEET) as i:
                    x_turns(i)
                if l == 0:
                    pe.wait_ge(rows_ready, 1)
                    for c in range(RC):
                        pe.transpose(bank[2][:, c * ROWS:(c + 1) * ROWS], ev[:, c, :, 0], ident[0:ROWS, 0:ROWS])
                        pe.transpose(bank[3][:, c * ROWS:(c + 1) * ROWS], ev[:, c, :, 2], ident[0:ROWS, 0:ROWS])
                    ends = small[0:ROWS, c_ends]
                    pe.transpose(bank[4][0:RC, 256:256 + ROWS], small[0:ROWS, c_ta], ident[0:ROWS, 0:ROWS])
                    pe.transpose(bank[4][0:R * HM, 384:384 + ROWS], ends[:, 0:R * HM], ident[0:ROWS, 0:ROWS])
                    pe.transpose(bank[5][0:R * HM, 0:ROWS], ends[:, R * HM:2 * R * HM], ident[0:ROWS, 0:ROWS]
                                 ).then_inc(turned, 1)
                    pe.wait_ge(s["turned_taken"], 1)
                with pe.Fori(MEET, NT // U - 1) as i:
                    x_turns(i)
                x_turns(NT // U - 1, True)
                pe.wait_ge(s["qk_copied"], 2 + W0 + NT)

                pe.wait_ge(s["w_loaded"], 16 * (R - 1) * (1 + DC * l))

                def dturn(n, k, seen):
                    pe.wait_ge(s["drow_loaded"][k], 16 * (l * (NT // U) + seen))
                    pe.wait_ge(s["dT_ready"], n + 1)
                    for c in range(DC):
                        last = pe.transpose(bank[6 + c // 4][:, (c % 4) * P:(c % 4) * P + TN],
                                            xring[0:TN, PAT[k], c * P:(c + 1) * P], ident[0:TN, 0:TN])
                    last.then_inc(s["dT_turned"], 1)

                def dense(n, k, between):
                    pe.wait_ge(s["dT_ready"], n + 2)
                    for u, (r, first, n_cols) in enumerate(UNIT):
                        b = (UNITS * k + u) % DBANKS
                        pe.wait_ge(s["dense_out"], UNITS * n + u + 1)
                        for c in range(DC):
                            last = pe.matmul(bank[b][0:TN, 0:n_cols], xT[:, PAT[k], c, 0:TN],
                                             w_cols(r, first, n_cols)[:, c, :],
                                             start=(c == 0), stop=(c == DC - 1))
                        last.then_inc(s["dense_done"], 1)
                        if (k, u) in between:
                            between[k, u]()

                def dense_turn(i, last_turn=False, between=()):
                    for k in range(U):
                        n = U * i + k
                        if k < U - 1:
                            dturn(n + 1, k + 1, i + 1)
                        elif not last_turn:
                            dturn(n + 1, 0, i + 2)
                        dense(n, k, between)

                dturn(0, 0, 1)
                with pe.Fori(0, 1) as i:
                    dense_turn(i)
                pe.wait_ge(s["qend_ready"], l + 1)
                pe.transpose(bank[5][0:R * H, 0:ROWS], small[0:ROWS, c_last][:, 0:R * H], ident[0:ROWS, 0:ROWS]
                             ).then_inc(s["qend_turned"], 1)
                pe.wait_ge(s["qcarry_ready"], l + 1)
                pe.transpose(bank[5][0:ROWS, 0:R * H], flag[0:R * H, CARRY, 0:ROWS], ident[0:R * H, 0:R * H]
                             ).then_inc(s["qcarry_turned"], 1)
                pe.wait_ge(s["qcarry_taken"], l + 1)
                with pe.Fori(1, NT // U - 1) as i:
                    dense_turn(i)

                def turn_k(h):
                    if h == 0:
                        pe.wait_ge(s["k_ready"], l + 1)
                    else:
                        pe.wait_ge(s["k_added"], HM * l + h)
                    k_lanes = k_edge[:, 0:STEPS * H].rearrange("p (r c h) -> p c h r", c=RC, h=H)
                    for c in range(RC):
                        last = pe.transpose(bank[5][0:ROWS, c * P:(c + 1) * P], k_lanes[:, c, h, :], ident[:, :])
                    last.then_inc(s["k_turned"], 1)

                def turn_ends(w):
                    pe.wait_ge(s["end_ready"], 2 * l + w + 1)
                    pe.transpose(bank[5][0:H, 0:ROWS], small[0:ROWS, c_last][:, 0:H], ident[0:ROWS, 0:ROWS]
                                 ).then_inc(s["end_turned"], 1)

                def turn_carry(w):
                    pe.wait_ge(s["carry_ready"], 2 * l + w + 1)
                    pe.transpose(bank[5][0:ROWS, 0:H], flag[0:H, CARRY, 0:ROWS], ident[0:H, 0:H]
                                 ).then_inc(s["carry_turned"], 1)

                def turn_e(h):
                    pe.wait_ge(s["e_ready"], l + 1)
                    for c in range(RC):
                        last = pe.transpose(bank[E_BANK[h]][:, c * ROWS:(c + 1) * ROWS], amax[:, h, c * P:(c + 1) * P],
                                            ident[0:ROWS, 0:ROWS])
                    last.then_inc(s["e_turned"], 1)

                meets = [lambda h=h: turn_k(h) for h in range(H)]
                meets += [lambda f=f, w=w: f(w) for w in range(2) for f in (turn_ends, turn_carry)]
                if H > 1:
                    spots = [(3, 0), (3, 1), (3, 2), (3, 3), (3, 5), (4, 0), (4, 2), (4, 3)]
                else:
                    meets.append(lambda: turn_e(0))
                    spots = [(3, 2), (3, 3), (3, 4), (3, 5), (4, 0), (4, 2)]
                pe.sem_inc(s["step_done"], GS)
                dense_turn(NT // U - 1, True, dict(zip(spots, meets)))
                pe.wait_ge(s["dense_out"], DBANKS + UNITS * NT)
                if H > 1:
                    for h in range(H):
                        turn_e(h)
                pe.wait_ge(s["w_ready"], l + 1)

                HB2 = ROWW[l] // 2
                with pe.Fori(0, STEPS // GS) as i:
                    for j in range(GS):
                        st = GS * i + j
                        slot = j % AHEAD
                        pe.wait_ge(s["row_gathered"][j], 16 * (i + 1))
                        pe.wait_ge(s["S_built"] if H > 1 else s["hot_built"], st + 1 + (AHEAD if H > 1 else 0))
                        pe.wait_ge(s["sum_added"], st + 1)
                        for half in range(2):
                            for m in range(max(H // 2, 1)):
                                h = half * (H // 2) + m
                                w = HW if H > 1 else HB2
                                last = pe.matmul(bank[2 * slot + half][0:TN, m * w:(m + 1) * w],
                                                 S[:, slot, h, :],
                                                 ring[:, j, half * HB2 + m * w:half * HB2 + (m + 1) * w],
                                                 start=True, stop=True)
                        last.then_inc(s["step_done"], 1)

        @block.scalar
        def _(act):
            def gate(sm, value):
                act.wait_ge(sm, value)
                act.sem_inc(act_gate, 1)

            for l in range(2):
                s = LS[l]
                H = HEADS[l]
                W0 = WT if l == 0 else 0
                act.sem_inc(s["xT_ready"], 2)
                act.sem_inc(s["qk_copied"], 2)
                act.sem_inc(s["dT_ready"], 1)
                act.sem_inc(s["dense_out"], DBANKS)
                if H > 1:
                    act.sem_inc(s["S_built"], AHEAD)
                act.sem_inc(s["qk_done"], 2)

                def take(n, pair, rows):
                    act.wait_ge(s["xT_turned"], n + 1 + (3 if l == 0 else U))
                    act.wait_ge(s["qk_done"], n + 1)
                    nc.scalar.copy(xT[:, pair, :, 0:rows], turned_chunks(pair).rearrange("p (c n) -> p c n", c=DC)[:, :, 0:rows]
                                   ).then_inc(s["xT_ready"], 1)

                if l == 0:
                    take(0, 0, P)
                    for i, last_turn in turns(act, WT, DC):
                        for c in range(DC):
                            n = DC * i + c
                            if c < DC - 1 or not last_turn:
                                take(n + 1, (c + 1) % 3, P)
                            gate(s["qk_done"], n + 3)
                            nc.scalar.copy(qk_cols(0)[:, c, :, bass.ds(i, 1), :].rearrange("p a r h -> p a (r h)"),
                                           bank[6][:, 0:2 * H].rearrange("p (a h) -> p a h", a=2)
                                           ).then_inc(s["qk_copied"], 1)

                    for r in range(1, R):
                        act.dma_start(w_cols(r, 0, D), W1[r].rearrange("(c p) f -> p c f", p=P)).then_inc(s["w_loaded"], 16)

                def exp_hidden(t, k):
                    act.wait_ge(LS[0]["h_ready"], t + 1)
                    gate(LS[0]["u_ready"], t + 1)
                    nc.scalar.activation(heads(ring[0:TN, PAT[k], 0:D], HEADS[0]), node_sum(0, t), ACT.Exp
                                         ).then_inc(LS[0]["exp_ready"], 1)

                def x_turns(i, last_turn=False):
                    for k in range(U):
                        t = U * i + k
                        n = W0 + t
                        if l == 1 and (k + 2 < U or not last_turn):
                            exp_hidden(t + 2, (k + 2) % U)
                        if k < U - 1 or not last_turn:
                            take(n + 1, PAT[(k + 1) % U], TN)
                        gate(s["qk_done"], n + 3)
                        acc = bank[6 + k % 2][0:TN]
                        nc.scalar.copy(qk_node[0:TN, bass.ds(t, 1), 0:2 * R * H].rearrange("p a b -> p (a b)"), acc[:, 0:2 * R * H])
                        act.wait_ge(s["half_stored"][PAT[k]], 16 * (PAT.count(PAT[k]) * i + PAT[:k].count(PAT[k]) + 1))
                        nc.scalar.copy(ring[0:TN, 5 + PAT[k], 0:PIECE], acc[:, 2 * R * H:2 * R * H + PIECE]
                                       ).then_inc(s["qk_copied"], 1)

                if l == 0:
                    act.wait_ge(halves_set, 1)
                else:
                    exp_hidden(0, 0)
                    exp_hidden(1, 1)
                take(W0, 0, TN)
                with act.Fori(0, NT // U - 1) as i:
                    x_turns(i)
                x_turns(NT // U - 1, True)

                act.sem_inc(s["dense_done"], 2 * UNITS)

                def dtake(n, k):
                    act.wait_ge(s["dT_turned"], n + 3)
                    act.wait_ge(s["dense_done"], UNITS * (n + 1))
                    for b, c0, c1 in ((6, 0, 4), (7, 4, DC)):
                        last = nc.scalar.copy(xT[:, PAT[k], c0:c1, 0:TN],
                                              bank[b].rearrange("p (c n) -> p c n", c=4)[:, 0:c1 - c0, 0:TN])
                    last.then_inc(s["dT_ready"], 1)

                def exponentials():
                    act.wait_ge(s["diff_ready"], l + 1)
                    nc.scalar.activation(amax[:, 0:H, :], alpha[:, 0:H, :], ACT.Exp).then_inc(s["e_ready"], 1)

                def dense_turn(i, last_turn=False, between=()):
                    for k in range(U):
                        n = U * i + k
                        if k < U - 1:
                            dtake(n + 1, k + 1)
                        elif not last_turn:
                            dtake(n + 1, 0)
                        for u, (r, first, n_cols) in enumerate(UNIT):
                            unit = R * k + r
                            slot = unit % U
                            if u % 2 == 0:
                                act.wait_ge(s["staged_stored"][slot], 16 * (R * i + unit // U + 1))
                            act.wait_ge(s["dense_done"], 2 * UNITS + UNITS * n + u + 1)
                            o_ = ring[0:TN, slot, first:first + n_cols]
                            i_ = bank[(UNITS * k + u) % DBANKS][0:TN, 0:n_cols]
                            if H > 1:
                                h0, nh = first // PIECE, n_cols // PIECE
                                o_ = heads(ring[0:TN, slot, 0:ROWW[l]], H)[:, h0:h0 + nh, 0:PIECE]
                                i_ = heads(i_, nh)
                            nc.scalar.copy(o_, i_).then_inc(s["dense_out"], 1)
                            if (k, u) in between:
                                between[k, u]()

                act.wait_ge(s["ones_set"], l + 1)
                dtake(0, 0)
                with act.Fori(0, NT // U - 1) as i:
                    dense_turn(i)
                dense_turn(NT // U - 1, True, {(U - 1, 4 if H > 1 else 1): exponentials})

                if H > 1:
                    act.wait_ge(s["w_ready"], l + 1)
                    with act.Fori(0, STEPS // GS) as i:
                        for j in range(GS):
                            st = GS * i + j
                            slot = j % AHEAD
                            act.wait_ge(s["hot_built"], st + 1)
                            gate(s["step_done"], st + 1 + GS - AHEAD)
                            for h in range(H):
                                last = nc.scalar.activation(S[:, slot, h, :], hot[:, slot, :], ACT.Copy,
                                                            scale=wE[:, bass.ds(st, 1), h:h + 1].rearrange("p a b -> p (a b)"))
                            last.then_inc(s["S_built"], 1)

                if l == 1:
                    mv = small[0:TN, c_mv].rearrange("p (t a) -> p t a", a=2)
                    for i, last_turn in turns(act, NT, U):
                        for k in range(U):
                            t = U * i + k
                            if k == 0:
                                act.wait_ge(var_ready, i + 1)
                                nc.scalar.activation(deviation, deviation, ACT.Sqrt).then_inc(dev_ready, 1)
                                act.wait_ge(s["h_ready"], i + 1)
                            gate(s["h_stored"][PAT[k]], 16 * (PAT.count(PAT[k]) * i + PAT[:k].count(PAT[k]) + 1))
                            m = mv[:, bass.ds(t, 1), :].rearrange("p a b -> p (a b)")
                            nc.scalar.activation(heads(ring[0:TN, 3 + PAT[k], 0:D], H), node_sum(l, t), ACT.Identity,
                                                 scale=m[:, 1:2], bias=m[:, 0:1]).then_inc(s["h_out"], 1)

        @block.gpsimd
        def _(pool):
            chain = [0]

            def link(ins):
                chain[0] += 1
                ins.then_inc(pool_step, 1)
                pool.wait_ge(pool_step, chain[0])

            def gate(sm, value):
                pool.wait_ge(sm, value)
                pool.sem_inc(pool_gate, 1)

            link(nc.gpsimd.memset(ident[:, :], 0.0))
            link(nc.gpsimd.affine_select(out=ident[:, :], in_=ident[:, :], compare_op=ALU.not_equal, fill=1.0,
                                         base=0, pattern=[[-1, P]], channel_multiplier=1))
            link(nc.gpsimd.memset(below, 1.0))
            link(nc.gpsimd.affine_select(out=below, in_=below, compare_op=ALU.is_gt, fill=0.0,
                                         base=0, pattern=[[1, TN]], channel_multiplier=-1))
            link(nc.gpsimd.memset(ones, 1.0))
            link(nc.gpsimd.memset(zero_bf, 0.0))
            link(nc.gpsimd.iota(iota_n[:, :], [[1, TN]], base=0, channel_multiplier=0,
                                allow_small_or_imprecise_dtypes=True))
            link(nc.gpsimd.iota(small[:, c_it], [[1, NT]], base=0, channel_multiplier=0,
                                allow_small_or_imprecise_dtypes=True))
            link(nc.gpsimd.iota(small[:, c_t125], [[P, NT]], base=0, channel_multiplier=0,
                                allow_small_or_imprecise_dtypes=True))
            link(nc.gpsimd.iota(small[:, c_trash], [[TN, NT]], base=STEPS * P, channel_multiplier=1,
                                allow_small_or_imprecise_dtypes=True))
            link(nc.gpsimd.iota(small[:, c_sio], [[1, RC]], base=0, channel_multiplier=RC,
                                allow_small_or_imprecise_dtypes=True))
            pool.sem_inc(consts_ready, 1)
            nc.gpsimd.memset(zeros, 0.0).then_inc(zeros_set, 1)
            pool.wait_ge(zeros_set, 1)
            for m in range(2):
                pool.dma_start(qfill[m][0:STEPS * P, :].rearrange("(p y) q -> p (y q)", p=P),
                               zeros[:, 0:STEPS * R * HEADS[m]]).then_inc(fills_zeroed, 16)

            pool.wait_ge(etab_stored, 16)
            pool.wait_ge(cursor_ready, 1)

            TILE_MOVES = 16 * 7

            def place(i, n):
                first = i * P
                seen = {sort_step: 0, sort_moved: 0}

                def then(ins, by):
                    done = sort_step if by == 1 else sort_moved
                    seen[done] += by
                    ins.then_inc(done, by)
                    if by == 1:
                        pool.wait_ge(sort_step, seen[done])
                    else:
                        gate(sort_moved, 16 + TILE_MOVES * i + seen[done])

                def row_sum(v):
                    w = P // 2
                    while w:
                        then(nc.gpsimd.tensor_tensor(v[:, 0:w], v[:, 0:w], v[:, w:2 * w], ALU.add), 1)
                        w //= 2

                if n < P:
                    then(nc.gpsimd.memset(s_row, -1.0), 1)
                for a, arr in enumerate((src, etype, dst)):
                    then(pool.dma_start(s_int[0:n, a:a + 1], arr[bass.ds(first, n)].rearrange("(p o) -> p o", o=1),
                                        allow_slow_non_contiguous=True), 16)
                then(pool.dma_start(s_rowi[0:n, 0:n], dst[bass.ds(first, n)].partition_broadcast(n)), 16)
                then(nc.gpsimd.tensor_copy(s_row[0:n, 0:n], s_rowi[0:n, 0:n]), 1)
                then(nc.gpsimd.tensor_copy(s_edge[0:n, :], s_int[0:n, :]), 1)
                then(nc.gpsimd.tensor_scalar(s_edge[0:n, 0:1], s_edge[0:n, 0:1], float(R), s_edge[0:n, 1:2],
                                             ALU.mult, ALU.add), 1)
                then(nc.gpsimd.tensor_scalar(s_equal[0:n, :], s_row[0:n, :], s_edge[0:n, 2:3], None, ALU.is_equal), 1)
                then(nc.gpsimd.tensor_tensor(s_count[0:n, :], s_equal[0:n, :], s_before[0:n, :], ALU.mult), 1)
                row_sum(s_equal[0:n, :])
                row_sum(s_count[0:n, :])
                then(nc.gpsimd.indirect_dma_start(
                    s_base[0:n], None, cursor[0:N], bass.IndirectOffsetOnAxis(ap=s_int[0:n, 2:3], axis=0)), 16)
                then(nc.gpsimd.tensor_tensor(s_rank[0:n], s_base[0:n], s_count[0:n, 0:1], ALU.add), 1)
                then(nc.gpsimd.tensor_copy(s_pos[0:n].bitcast(I32), s_rank[0:n]), 1)
                then(nc.gpsimd.tensor_tensor(s_new[0:n], s_base[0:n], s_equal[0:n, 0:1], ALU.add), 1)
                then(nc.gpsimd.indirect_dma_start(
                    etab, bass.IndirectOffsetOnAxis(ap=s_pos[0:n].bitcast(I32), axis=0), s_edge[0:n, :], None), 16)
                then(nc.gpsimd.tensor_tensor(s_last[0:n], s_count[0:n, 0:1], s_equal[0:n, 0:1], ALU.subtract), 1)
                then(nc.gpsimd.tensor_scalar(s_last[0:n], s_last[0:n], -1.0, None, ALU.is_equal), 1)
                then(nc.gpsimd.tensor_tensor(s_rank[0:n], s_edge[0:n, 2:3], s_lane[0:n], ALU.subtract), 1)
                then(nc.gpsimd.tensor_tensor(s_rank[0:n], s_rank[0:n], s_last[0:n], ALU.mult), 1)
                then(nc.gpsimd.tensor_tensor(s_rank[0:n], s_rank[0:n], s_lane[0:n], ALU.add), 1)
                then(nc.gpsimd.tensor_copy(s_at[0:n].bitcast(I32), s_rank[0:n]), 1)
                then(nc.gpsimd.indirect_dma_start(
                    cursor, bass.IndirectOffsetOnAxis(ap=s_at[0:n].bitcast(I32), axis=0), s_new[0:n], None), 16)
                assert seen[sort_moved] == TILE_MOVES
                pool.sem_clear(sort_step)

            out_of_order = pool.value_load(small[0:1, c_tot][:, NT:NT + 1].bitcast(I32), min_val=0, max_val=E)
            with pool.If(out_of_order > 0):
                nc.gpsimd.memset(s_before, 1.0).then_inc(sort_step, 1)
                pool.wait_ge(sort_step, 1)
                nc.gpsimd.affine_select(out=s_before, in_=s_before, compare_op=ALU.is_gt, fill=0.0,
                                        base=0, pattern=[[-1, P]], channel_multiplier=1).then_inc(sort_step, 1)
                pool.wait_ge(sort_step, 2)
                nc.gpsimd.iota(s_lane, [[1, 1]], base=N, channel_multiplier=1,
                               allow_small_or_imprecise_dtypes=True).then_inc(sort_step, 1)
                pool.wait_ge(sort_step, 3)
                pool.dma_start(cursor[0:N].rearrange("(t p) o -> p (t o)", p=TN), small[0:TN, c_cur],
                               allow_slow_non_contiguous=True).then_inc(sort_moved, 16)
                pool.wait_ge(sort_moved, 16)
                pool.sem_clear(sort_step)
                with pool.Fori(0, E // P) as i:
                    place(i, P)
                if E % P:
                    place(E // P, E % P)

            pool.wait_ge(steps_ready, 1)
            etab_rows = etab.rearrange("(i j) a -> i (j a)", j=P)
            for c in range(RC):
                nc.gpsimd.indirect_dma_start(
                    ev[:, c, :, :].rearrange("r j a -> r (j a)"), None, etab_rows,
                    bass.IndirectOffsetOnAxis(ap=small[0:ROWS, c_is].bitcast(I32)[:, c:c + 1], axis=0),
                ).then_inc(ev_gathered, 16)

            for l in range(2):
                s = LS[l]
                H = HEADS[l]
                pool.wait_ge(start_ready, 1)
                pool.wait_ge(fills_zeroed, 32)
                for t in range(NT):
                    pool.wait_ge(s["qk_copied"], 2 + (WT if l == 0 else 0) + t + 1)
                    nc.gpsimd.indirect_dma_start(
                        qfill[l], bass.IndirectOffsetOnAxis(ap=start_at[0:TN, t:t + 1], axis=0),
                        qk_node[0:TN, t, 0:R * H], None).then_inc(s["q_scattered"], 16)

                pool.wait_ge(s["k_stored"], 16 * (l + 1))
                pool.wait_ge(lanes_ready, 1)
                pool.sem_inc(s["k_taken"], 2)

                def fetch(m, g, turn_):
                    gate(s["k_taken"], m + 1)
                    nc.gpsimd.tensor_copy(kidx[:, g, :], row_idx[:, bass.ds(m * KG, KG)]).then_inc(s["kidx_staged"], 1)
                    gate(s["kidx_staged"], m + 1)
                    for j in range(KG):
                        nc.gpsimd.indirect_dma_start(
                            kring[:, (g * KG + j) * H:(g * KG + j + 1) * H], None, ktab[l],
                            bass.IndirectOffsetOnAxis(ap=kidx[:, g, j:j + 1], axis=0)).then_inc(s["k_gathered"][g], 16)

                def take(m, g, turn_):
                    gate(s["k_gathered"][g], 16 * KG * (turn_ + 1))
                    nc.gpsimd.tensor_copy(k_edge[:, bass.ds(m * KG * H, KG * H)],
                                          kring[:, g * KG * H:(g + 1) * KG * H]).then_inc(s["k_taken"], 1)

                fetch(0, 0, 0)
                for i, last in turns(pool, STEPS // KG, 2):
                    fetch(2 * i + 1, 1, i)
                    take(2 * i, 0, i)
                    if not last:
                        fetch(2 * i + 2, 0, i + 1)
                    take(2 * i + 1, 1, i)
                pool.wait_ge(s["k_taken"], 2 + STEPS // KG)
                pool.sem_inc(s["k_ready"], 1)

                pool.wait_ge(s["k_added"], HM * l + H)
                nc.gpsimd.memset(big[0:TN, K_AT:ACCW], 0.0).then_inc(s["sums_zeroed"], 1)
                pool.wait_ge(s["e_ready"], l + 1)
                nc.gpsimd.memset(big[0:TN, ALPHA_AT:AMAX_AT], 0.0).then_inc(s["sums_zeroed"], 1)

                for i in range(U):
                    pool.wait_ge(s["staged_stored"][i], 16 * (1 + NT * R // U))
                half = GS // 2
                with pool.Fori(0, STEPS // GS) as i:
                    for g in range(2):
                        m = 2 * i + g
                        gate(s["step_done"], half * (m + 1))
                        nc.gpsimd.tensor_copy(gidx[:, g, :], row_idx[:, bass.ds(m * half, half)]
                                              ).then_inc(s["gidx_staged"], 1)
                        gate(s["gidx_staged"], m + 1)
                        for j in range(half):
                            nc.gpsimd.indirect_dma_start(
                                ring[:, g * half + j, 0:ROWW[l]], None, xrtab[l],
                                bass.IndirectOffsetOnAxis(ap=gidx[:, g, j:j + 1], axis=0)
                            ).then_inc(s["row_gathered"][g * half + j], 16)
                if l == 1:
                    pool.wait_ge(s["brow_loaded"], 16 * (l + 1))
                    for i, last in turns(pool, NT, U):
                        for k in range(U):
                            pool.wait_ge(s["x_loaded"][k], 16 * (i + 1))
                            nc.gpsimd.tensor_tensor(xring[0:TN, U - 1 - k, :], xring[0:TN, U - 1 - k, :], brow[0:TN, :], ALU.add
                                                    ).then_inc(s["x_added"], 1)

        @block.vector
        def _(dve):
            chain = [0]

            def link(ins):
                chain[0] += 1
                ins.then_inc(dve_step, 1)
                dve.wait_ge(dve_step, chain[0])

            def gate(sm, value):
                dve.wait_ge(sm, value)
                dve.sem_inc(dve_gate, 1)

            def floor(dst_f_, y, as_int):
                link(nc.vector.tensor_copy(as_int, y))
                link(nc.vector.tensor_copy(dst_f_, as_int))
                link(nc.vector.tensor_tensor(y, dst_f_, y, ALU.is_gt))
                link(nc.vector.tensor_tensor(dst_f_, dst_f_, y, ALU.subtract))

            dve.sem_inc(LS[1]["x_used"], U)
            link(nc.vector.memset(rows_i[:, 0:2, :], 0))
            nc.vector.memset(rows_i[:, 2, :], PAD_DST).then_inc(pads_set, 1)
            dve.wait_ge(dst_loaded, 16)
            link(nc.vector.tensor_copy(dst_f, dst_i))
            link(nc.vector.tensor_scalar(d_y, dst_f, 0.5, 1.0 / TN, ALU.add, ALU.mult))
            floor(d_hi, d_y, d_i)
            link(nc.vector.scalar_tensor_tensor(out=d_lo, in0=d_hi, scalar=-float(TN), in1=dst_f, op0=ALU.mult, op1=ALU.add))
            nc.vector.memset(ring[0:TN, 5:8, PIECE:HC0[0]], 1.0).then_inc(halves_set, 1)

            dve.wait_ge(consts_ready, 1)
            with dve.Fori(0, HROUNDS) as n_:
                for part in range(3):
                    off, n = n_ * NT + sum(HPARTS[:part]), HPARTS[part]
                    dve.wait_ge(hot_used, 3 * n_ + part + 1)
                    nc.vector.tensor_tensor(hhi[part][:, 0:n, :], d_hi[:, bass.ds(off, n)].unsqueeze(2).to_broadcast([TN, n, NT]),
                                            small[0:TN, c_it].unsqueeze(1).to_broadcast([TN, n, NT]), ALU.is_equal)
                    nc.vector.tensor_tensor(hlo[part][:, 0:n, :], d_lo[:, bass.ds(off, n)].unsqueeze(2).to_broadcast([TN, n, TN]),
                                            iota_n[0:TN, :].unsqueeze(1).to_broadcast([TN, n, TN]), ALU.is_equal
                                            ).then_inc(hot_ready, 1)
            dve.wait_ge(edges_loaded, 16 * 8)
            link(nc.vector.scalar_tensor_tensor(out=ev_rows[:, :, 0], in0=rows_i[:, 0, :], scalar=float(R),
                                                in1=rows_i[:, 1, :], op0=ALU.mult, op1=ALU.add))
            link(nc.vector.tensor_copy(ev_rows[:, :, 1], rows_i[:, 1, :]))
            nc.vector.tensor_copy(ev_rows[:, :, 2], rows_i[:, 2, :]).then_inc(etab_src, 1)
            link(nc.vector.memset(small[:, c_cnt], 0.0))
            link(nc.vector.tensor_tensor(d_falls, d_this, d_next, ALU.is_gt))
            link(nc.vector.tensor_reduce(small[0:ORDER_P, c_cnt][:, NT:NT + 1], d_falls, AX.X, ALU.add))

            dve.wait_ge(counts_done, 1)
            nc.vector.tensor_copy(counts, bank[7][0:NT, 0:TN]).then_inc(cnt_ready, 1)
            dve.wait_ge(sums_done, 1)
            nc.vector.tensor_copy(small[0:TN, c_cnt][:, 0:NT], bank[4][0:TN, 256:256 + NT]).then_inc(cnt_ready, 1)
            dve.wait_ge(sums_done, 2)
            cnt, tot, inc, rp, y, f, St, cur = (small[:, c] for c in (c_cnt, c_tot, c_inc, c_rp, c_y, c_f, c_St, c_cur))
            cnt, tot, falls = cnt[:, 0:NT], tot[:, 0:NT], tot[:, NT:NT + 1]
            link(nc.vector.tensor_copy(tot, bank[5][:, 384:384 + NT]))
            link(nc.vector.tensor_copy(falls.bitcast(I32), bank[5][:, 384 + NT:385 + NT]))
            nc.vector.tensor_copy(rp[0:TN], bank[5][0:TN, 320:320 + NT]).then_inc(cnt_ready, 1)
            dve.wait_ge(cnt_ready, 3)
            link(nc.vector.memset(y, 1.0))
            link(nc.vector.tensor_tensor_scan(inc, y, tot, 0.0, ALU.mult, ALU.add))
            link(nc.vector.tensor_tensor(inc, inc, tot, ALU.subtract))
            link(nc.vector.tensor_tensor(rp[0:TN], inc[0:TN], rp[0:TN], ALU.add))
            nc.vector.tensor_copy(cur[0:TN], rp[0:TN]).then_inc(cursor_ready, 1)
            link(nc.vector.tensor_scalar(y, inc, 1.0 / P, None, ALU.mult))
            floor(f, y, St.bitcast(I32))
            link(nc.vector.tensor_tensor(St, f, small[:, c_it], ALU.add))
            hit = pen[0:ROWS, 0:RC * (NT - 1)].rearrange("r (c t) -> r c t", c=RC)
            sio, ts, is_, t8, tn, ta = (small[0:ROWS, c] for c in (c_sio, c_ts, c_is, c_t8, c_tn, c_ta))
            link(nc.vector.tensor_tensor(hit, St[0:ROWS, 1:NT].unsqueeze(1).to_broadcast([ROWS, RC, NT - 1]),
                                         sio.unsqueeze(2).to_broadcast([ROWS, RC, NT - 1]), ALU.is_le))
            link(nc.vector.tensor_reduce(ts, hit, AX.X, ALU.add))
            link(nc.vector.tensor_tensor(ta, sio, ts, ALU.subtract))
            nc.vector.tensor_copy(is_.bitcast(I32), ta).then_inc(steps_ready, 1)
            n_ = slice(0, TN)
            link(nc.vector.tensor_tensor(rp[n_], rp[n_], small[n_, c_t125], ALU.add))
            link(nc.vector.tensor_tensor(rp[n_], rp[n_], small[n_, c_trash], ALU.subtract))
            link(nc.vector.tensor_scalar(y[n_], cnt[n_], 0.0, None, ALU.is_gt))
            link(nc.vector.tensor_tensor(rp[n_], rp[n_], y[n_], ALU.mult))
            link(nc.vector.tensor_tensor(rp[n_], rp[n_], small[n_, c_trash], ALU.add))
            nc.vector.tensor_copy(start_at[n_, :], rp[n_]).then_inc(start_ready, 1)

            link(nc.vector.tensor_scalar(t8, ts, KEY, None, ALU.mult))
            link(nc.vector.tensor_scalar(tn, ts, float(TN), None, ALU.mult))
            dve.wait_ge(ev_gathered, 16 * RC)
            link(nc.vector.tensor_copy(ta, ts))
            link(nc.vector.tensor_copy(rel[0:ROWS, :].rearrange("r (c j) -> r c j", c=RC), ev[:, :, :, 1]))
            link(nc.vector.tensor_tensor(key.rearrange("r (c j) -> r c j", c=RC), ev[:, :, :, 2],
                                         t8.unsqueeze(2).to_broadcast([ROWS, RC, P]), ALU.add))
            link(nc.vector.tensor_tensor(ev[:, :, :, 2], ev[:, :, :, 2],
                                         tn.unsqueeze(2).to_broadcast([ROWS, RC, P]), ALU.subtract))
            NQ = R * HM
            ends = small[0:ROWS, c_ends]
            link(nc.vector.tensor_copy(ends[:, 0:NQ], key[:, 0:1].to_broadcast([ROWS, NQ])))
            nc.vector.tensor_copy(ends[:, NQ:2 * NQ], key[:, RL - 1:RL].to_broadcast([ROWS, NQ])).then_inc(rows_ready, 1)
            r_ = slice(0, ROWS)
            link(nc.vector.memset(pen[r_, :], 0.0))
            link(nc.vector.tensor_tensor(pen[r_, 1:RL], key[:, 1:RL], key[:, 0:RL - 1], ALU.not_equal))
            link(nc.vector.tensor_scalar(same[r_, :], pen[r_, 0:RL], -1.0, 1.0, ALU.mult, ALU.add))
            link(nc.vector.tensor_scalar(pen[r_, :], pen[r_, :], -BIG, None, ALU.mult))
            dve.wait_ge(turned, 1)
            link(nc.vector.memset(flag[:, :, :], 0.0))
            link(nc.vector.tensor_copy(flag[:, RUN, 0:ROWS], bank[5][0:NQ, 0:ROWS]))
            link(nc.vector.tensor_copy(flag[:, CARRY, 0:ROWS], bank[4][0:NQ, 384:384 + ROWS]))
            for l in range(2):
                link(nc.vector.tensor_scalar(acc_at[:, l, :], bank[4][0:RC, 256:256 + ROWS], float(ROWW[l]), None, ALU.mult))
            link(nc.vector.tensor_copy(row_idx[:, :].rearrange("p (r c) -> p c r", c=RC),
                                       bank[2][:, 0:STEPS].rearrange("p (c r) -> p c r", c=RC)))
            link(nc.vector.tensor_copy(dloc[:, 0:STEPS].rearrange("p (r c) -> p c r", c=RC),
                                       bank[3][:, 0:STEPS].rearrange("p (c r) -> p c r", c=RC)))
            dve.sem_inc(LS[0]["turned_taken"], 1)
            link(nc.vector.memset(dloc[:, STEPS:], -1.0))
            k0 = flag[:, CARRY, 0:ROWS]
            link(nc.vector.tensor_tensor(flag[:, EQ, 1:ROWS], k0[:, 1:ROWS], flag[:, RUN, 0:ROWS - 1], ALU.is_equal))
            link(nc.vector.tensor_tensor(flag[:, UNI, 0:ROWS], k0, flag[:, RUN, 0:ROWS], ALU.is_equal))
            link(nc.vector.tensor_tensor(flag[:, CONT, 0:ROWS], flag[:, UNI, 0:ROWS], flag[:, EQ, 0:ROWS], ALU.mult))
            link(nc.vector.tensor_tensor(flag[:, CONTPEN_B, 0:ROWS], flag[:, UNI, 0:ROWS], flag[:, EQ, 1:ROWS + 1], ALU.mult))
            for a, b in ((EQPEN, EQ), (CONTPEN, CONT), (CONTPEN_B, CONTPEN_B)):
                link(nc.vector.tensor_scalar(flag[:, a, :], flag[:, b, :], -1.0, BIG, ALU.add, ALU.mult))
            dve.sem_inc(lanes_ready, 1)

            for l in range(2):
                s = LS[l]
                H = HEADS[l]
                HW = HWS[l]
                RWL = ROWW[l]
                nc.vector.memset(ring[0:TN, 0:U, 0:RWL].rearrange("p u (h w) -> p u h w", h=H)[:, :, :, D // H:HW], 1.0
                                 ).then_inc(s["ones_set"], 1)

                dve.wait_ge(s["q_loaded"], 16 * (l + 1))
                raw = qf_raw[:, 0:RL * R * H].rearrange("r (x q) -> r q x", q=R * H)
                c_in = small[0:ROWS, c_carry]
                c_out = small[0:ROWS, c_last]
                for q in range(R * H):
                    link(nc.vector.tensor_tensor_scan(qf[:, q, :], same[0:ROWS, :], raw[:, q, :], 0.0, ALU.mult, ALU.add))
                nc.vector.tensor_copy(c_out[:, 0:R * H], qf[:, 0:R * H, RL - 1]).then_inc(s["qend_ready"], 1)
                dve.wait_ge(s["qend_turned"], l + 1)
                fl = flag[0:R * H]
                link(nc.vector.tensor_tensor_scan(fl[:, RUN, 0:ROWS], fl[:, CONT, 0:ROWS], bank[5][0:R * H, 0:ROWS],
                                                  0.0, ALU.mult, ALU.add))
                link(nc.vector.memset(fl[:, CARRY, 0:1], 0.0))
                nc.vector.tensor_tensor(fl[:, CARRY, 1:ROWS], fl[:, RUN, 0:ROWS - 1], fl[:, EQ, 1:ROWS], ALU.mult
                                        ).then_inc(s["qcarry_ready"], 1)
                dve.wait_ge(s["qcarry_turned"], l + 1)
                link(nc.vector.tensor_copy(c_in[:, 0:R * H], bank[5][0:ROWS, 0:R * H]))
                dve.sem_inc(s["qcarry_taken"], 1)
                for q in range(R * H):
                    link(nc.vector.tensor_tensor_scan(qf[:, q, :], same[0:ROWS, :], raw[:, q, :], c_in[:, q:q + 1],
                                                      ALU.mult, ALU.add))
                for r in range(R):
                    link(nc.vector.scalar_tensor_tensor(
                        out=qf[:, r * H:(r + 1) * H, :], in0=rel[0:ROWS, :].unsqueeze(1).to_broadcast([ROWS, H, RL]),
                        scalar=float(r), in1=qf[:, r * H:(r + 1) * H, :], op0=ALU.is_equal, op1=ALU.mult))
                al = alpha[:, 0:H, :]
                link(nc.vector.tensor_tensor(al, qf[:, 0:H, :], qf[:, H:2 * H, :], ALU.add))
                for r in range(2, R):
                    link(nc.vector.tensor_tensor(al, al, qf[:, r * H:(r + 1) * H, :], ALU.add))
                nc.vector.memset(big[0:TN, 0:ALPHA_AT], 0.0).then_inc(s["sums_zeroed"], 1)
                if l == 0:
                    dve.sem_inc(w2_used, 4)
                    dve.sem_inc(w2_ready, 1)
                    dve.wait_ge(qk_loaded, 64)
                    w2_terms = small[:, c_w2].rearrange("p (c a) -> p c a", a=2)
                    with dve.Fori(0, R) as r:
                        dve.wait_ge(w2_ready, r + 1)
                        for c in range(DC):
                            dve.wait_ge(w2_loaded[c % 2], 16 * (DC // 2 * r + c // 2 + 1))
                            w_tile, product = ring[:, 5 + c % 2, 0:D], ring[:, 7, 0:D]
                            for a, row in enumerate((q2_row, k2_row)):
                                dve.wait_ge(w2_used, 4 + 2 * (DC * r + c) + a)
                                nc.vector.tensor_tensor_reduce(product, w_tile, row, 1.0, 0.0, ALU.mult, ALU.add,
                                                               w2_terms[:, c, a:a + 1]).then_inc(w2_used, 1)
                        gate(w2_used, 4 + 2 * DC * (r + 1))
                        nc.vector.tensor_scalar(qk_cols(1)[:, :, :, bass.ds(r, 1), 0].rearrange("p c a r -> p c (a r)"),
                                                w2_terms, 1.0, None, ALU.mult).then_inc(w2_ready, 1)
                for h in range(H):
                    dve.wait_ge(s["k_turned"], HM * l + h + 1)
                    nc.vector.tensor_tensor(alpha[:, h, :], alpha[:, h, :], bank[5][0:ROWS, :], ALU.add).then_inc(s["k_added"], 1)
                dve.wait_ge(s["k_added"], HM * l + H)
                link(nc.vector.scalar_tensor_tensor(out=al, in0=al, scalar=SLOPE, in1=al, op0=ALU.mult, op1=ALU.max))
                fl = flag[0:H]
                for w in range(2):
                    def scan(h, first):
                        if w == 0:
                            return nc.vector.tensor_tensor_scan(amax[:, h, :], pen[0:ROWS, 0:RL], alpha[:, h, :],
                                                                first, ALU.add, ALU.max)
                        return nc.vector.tensor_tensor_scan(amax[:, h, ::-1], pen[0:ROWS, RL:0:-1], amax[:, h, ::-1],
                                                            first, ALU.add, ALU.max)
                    for h in range(H):
                        link(scan(h, -BIG))
                    nc.vector.tensor_copy(c_out[:, 0:H], amax[:, 0:H, RL - 1 if w == 0 else 0]).then_inc(s["end_ready"], 1)
                    dve.wait_ge(s["end_turned"], 2 * l + w + 1)
                    turned_ends = bank[5][0:H, 0:ROWS]
                    if w == 0:
                        link(nc.vector.tensor_tensor_scan(fl[:, RUN, 0:ROWS], fl[:, CONTPEN, 0:ROWS], turned_ends,
                                                          -BIG, ALU.add, ALU.max))
                        link(nc.vector.memset(fl[:, CARRY, 0:1], -BIG))
                        last = nc.vector.tensor_tensor(fl[:, CARRY, 1:ROWS], fl[:, RUN, 0:ROWS - 1],
                                                       fl[:, EQPEN, 1:ROWS], ALU.add)
                    else:
                        link(nc.vector.tensor_tensor_scan(fl[:, RUN, ROWS - 1::-1], fl[:, CONTPEN_B, ROWS - 1::-1],
                                                          turned_ends[:, ::-1], -BIG, ALU.add, ALU.max))
                        link(nc.vector.memset(fl[:, CARRY, ROWS - 1:ROWS], -BIG))
                        last = nc.vector.tensor_tensor(fl[:, CARRY, 0:ROWS - 1], fl[:, RUN, 1:ROWS],
                                                       fl[:, EQPEN, 1:ROWS], ALU.add)
                    last.then_inc(s["carry_ready"], 1)
                    dve.wait_ge(s["carry_turned"], 2 * l + w + 1)
                    link(nc.vector.tensor_copy(c_in[:, 0:H], bank[5][0:ROWS, 0:H]))
                    for h in range(H):
                        link(scan(h, c_in[:, h:h + 1]))
                nc.vector.tensor_tensor(al, al, amax[:, 0:H, :], ALU.subtract).then_inc(s["diff_ready"], 1)
                for h in range(H):
                    dve.wait_ge(s["e_turned"], HM * l + h + 1)
                    link(nc.vector.tensor_copy(wE[:, 0:STEPS, h].rearrange("p (r c) -> p c r", c=RC),
                                               bank[E_BANK[h]][:, 0:STEPS].rearrange("p (c r) -> p c r", c=RC)))
                link(nc.vector.memset(wE[:, STEPS:, :], 0.0))
                dve.sem_inc(s["w_ready"], 1)

                nc.vector.memset(big[0:TN, AMAX_AT:K_AT], 0.0).then_inc(s["sums_zeroed"], 1)
                dve.sem_inc(s["sum_added"], AHEAD)
                dve.wait_ge(s["dT_turned"], 2 + NT)

                def one_hot(st, slot):
                    at = dloc[:, bass.ds(st, 1)]
                    if H > 1:
                        dve.wait_ge(s["S_built"], st + 1)
                        nc.vector.tensor_scalar(hot[:, slot, :], iota_n[:, :], at, None, ALU.is_equal
                                                ).then_inc(s["hot_built"], 1)
                    else:
                        dve.wait_ge(s["step_done"], st + 1 + GS - AHEAD)
                        nc.vector.tensor_scalar(S[:, slot, 0, :], iota_n[:, :], at,
                                                wE[:, bass.ds(st, 1), 0:1].rearrange("p a b -> p (a b)"),
                                                ALU.is_equal, ALU.mult).then_inc(s["hot_built"], 1)

                for j in range(AHEAD):
                    one_hot(j, j)
                dve.wait_ge(s["sums_zeroed"], 4 * (l + 1))
                with dve.Fori(0, STEPS // GS) as i:
                    for j in range(GS):
                        st = GS * i + j
                        one_hot(st + AHEAD, j % AHEAD)
                        at = dve.value_load(acc_at[j % RC:j % RC + 1, l, bass.ds(i * (GS // RC) + j // RC, 1)],
                                            min_val=0, max_val=(NT - 1) * RWL)
                        dve.wait_ge(s["step_done"], GS + st + 1)
                        dve.wait_ge(s["sum_added"], AHEAD + st)
                        tile = big[0:TN, bass.ds(at, RWL)].rearrange("p (a w) -> p a w", a=2)
                        nc.vector.tensor_tensor(tile, tile, banks[0:TN, 2 * (j % AHEAD):2 * (j % AHEAD) + 2, 0:RWL // 2],
                                                ALU.add).then_inc(s["sum_added"], 1)

                dve.wait_ge(s["sum_added"], AHEAD + STEPS)
                z = small[0:TN, c_z][:, 0:NT * H]
                link(nc.vector.tensor_scalar(z.rearrange("p (t h) -> p t h", h=H),
                                             big[0:TN, 0:NT * RWL].rearrange("p (t h w) -> p t h w", t=NT, h=H)[:, :, :, D // H],
                                             SOFTMAX_EPS, None, ALU.add))
                link(nc.vector.reciprocal(z, z))
                dve.wait_ge(s["brow_loaded"], 16 * (l + 1))

                def divide(t, add):
                    for h in range(H):
                        u = node_sum(l, t)[:, h, :]
                        last = nc.vector.scalar_tensor_tensor(out=u, in0=u, scalar=z[:, bass.ds(t * H + h, 1)],
                                                              in1=add[:, h * (D // H):(h + 1) * (D // H)],
                                                              op0=ALU.mult, op1=ALU.add)
                    return last

                if l == 0:
                    dve.sem_inc(s["h_ready"], 2)
                    divide(0, brow[0:TN, :]).then_inc(s["u_ready"], 1)
                    divide(1, brow[0:TN, :]).then_inc(s["u_ready"], 1)
                    for i, last_turn in turns(dve, NT, U):
                        for k in range(U):
                            t = U * i + k
                            if k + 2 < U or not last_turn:
                                divide(t + 2, brow[0:TN, :]).then_inc(s["u_ready"], 1)
                            e = ring[0:TN, PAT[k], 0:D]
                            dve.wait_ge(s["exp_ready"], t + 1)
                            nc.vector.tensor_scalar(e, e, 1.0, -1.0, ALU.min, ALU.add).then_inc(s["e_set"], 1)
                            dve.wait_ge(s["e_set"], t + 1)
                            dve.wait_ge(LS[1]["xT_turned"], t + 1)
                            gate(s["h_stored"][k], 16 * (i + 1))
                            nc.vector.scalar_tensor_tensor(out=heads(xring[0:TN, k, :], H), in0=node_sum(l, t), scalar=0.0,
                                                           in1=heads(e, H), op0=ALU.max, op1=ALU.add).then_inc(s["h_ready"], 1)
                else:
                    PER_TURN = 3 * U + 1
                    stats = same[0:TN, 0:12 * U].rearrange("p (t a) -> p t a", a=12)
                    tile_mv = same[0:TN, 12 * U:14 * U].rearrange("p (t a) -> p t a", a=2)
                    mv = small[0:TN, c_mv].rearrange("p (t a) -> p t a", a=2)
                    for i, last_turn in turns(dve, NT, U):
                        for k in range(U):
                            t = U * i + k
                            dve.wait_ge(s["x_added"], t + 1)
                            divide(t, xring[0:TN, U - 1 - k, :]).then_inc(s["x_used"], 1)
                            gate(s["x_used"], U + t + 1)
                            for half in range(2):
                                nc.vector.bn_stats(stats[:, k, 6 * half:6 * half + 6],
                                                   node_sum(l, t)[:, 0, half * HALF:(half + 1) * HALF]).then_inc(s["e_set"], 1)
                        gate(s["e_set"], PER_TURN * i + 2 * U)
                        for k in range(U):
                            nc.vector.bn_aggr(tile_mv[:, k, :], stats[:, k, :].rearrange("p (a b) -> p a b", a=2)
                                              ).then_inc(s["e_set"], 1)
                        dve.wait_ge(s["e_set"], PER_TURN * i + 3 * U)
                        nc.vector.tensor_scalar(deviation, tile_mv[:, :, 1], NORM_EPS, None, ALU.add).then_inc(var_ready, 1)
                        dve.wait_ge(dev_ready, i + 1)
                        nc.vector.reciprocal(deviation, deviation).then_inc(s["e_set"], 1)
                        turn_mv = mv[:, bass.ds(U * i, U), :]
                        gate(s["e_set"], PER_TURN * (i + 1))
                        nc.vector.scalar_tensor_tensor(out=turn_mv[:, :, 0], in0=tile_mv[:, :, 0], scalar=-1.0,
                                                       in1=deviation, op0=ALU.mult, op1=ALU.mult)
                        nc.vector.tensor_scalar(turn_mv[:, :, 1], deviation, 1.0, None, ALU.mult).then_inc(s["h_ready"], 1)


_INS = ["x", "src", "dst", "edge_type_3", "L0_gnn_W1", "L0_gnn_q1", "L0_gnn_k1", "L0_gnn_b1",
        "L0_gnn_W2", "L0_gnn_q2", "L0_gnn_k2", "L0_gnn_b2"]


def kernel(**inputs):
    import numpy as np
    import concourse.bacc as bacc
    from concourse.bass_utils import run_bass_kernel_spmd

    nc = bacc.Bacc("TRN2", target_bir_lowering=False, num_devices=1)
    arrays, args = {}, []
    for name in _INS:
        a = np.ascontiguousarray(inputs[name])
        arrays[f"in_{name}"] = a
        args.append(nc.dram_tensor(f"in_{name}", a.shape, mybir.dt.from_np(a.dtype), kind="ExternalInput").ap())
    shape = inputs["x"].shape
    args.append(nc.dram_tensor("out_0", shape, F32, kind="ExternalOutput").ap())
    rgat_kernel(nc, *args)
    r = run_bass_kernel_spmd(nc, [arrays], core_ids=[0])
    return r.results[0]["out_0"]
```

```python
from contextlib import ExitStack

import concourse.bass as bass
from concourse import mybir

F32 = mybir.dt.float32
BF16 = mybir.dt.bfloat16
I32 = mybir.dt.int32
ALU = mybir.AluOpType
ACT = mybir.ActivationFunctionType
AX = mybir.AxisListType

P = 128
BIG = 1.0e38
SLOPE = 0.2
SOFTMAX_EPS = 1e-16
NORM_EPS = 1e-5


def rgat_kernel(nc, x, src, dst, etype, W1, q1, k1, b1, W2, q2, k2, b2, out):
    N, D = x.shape
    E = src.shape[0]
    R = W1.shape[0]
    DC = D // P
    HALF = D // 2
    TN = 125
    NT = N // TN
    assert NT * TN == N and DC * P == D
    ETILES = -(-E // P)
    STEPS = E // P + NT
    RC = 4
    ROWS = STEPS // RC
    RL = RC * P
    assert ROWS * RC == STEPS and ROWS <= P
    EROWS = ETILES // RC
    assert EROWS * RC == ETILES
    LAST = E - (EROWS - 1) * RL
    PAD_DST = 32 * TN
    KEY = 8192.0
    HCOLS = E // TN
    HROUNDS = HCOLS // NT
    HPARTS = [NT // 3 + (1 if i < NT % 3 else 0) for i in range(3)]
    assert HCOLS * TN == E and HROUNDS * NT == HCOLS and HROUNDS == R * DC - 1
    ORDER_P = max(d for d in range(1, TN + 1) if (E - 1) % d == 0)
    ORDER_C = (E - 1) // ORDER_P
    AHEAD = 4
    GS = 8
    KG = 11
    assert STEPS % GS == 0 and STEPS % (2 * KG) == 0
    U = 5
    WT = R * DC
    assert NT % U == 0 and NT // U >= R + 2 and DC % 3 == 0 and DC % 2 == 0
    PAT = [0, 1, 2, 0, 1]
    HEADS = [q1.shape[1], q2.shape[1]]
    HM = max(HEADS)
    HWS = [D // h + (1 if h > 1 else 2) for h in HEADS]
    ROWW = [h * w for h, w in zip(HEADS, HWS)]
    RW = max(ROWW)
    NQK = 2 * R * HM
    PIECE = D // HM
    HC0 = [w if h > 1 else PIECE for h, w in zip(HEADS, HWS)]
    UNIT = [(0, PIECE, HALF - PIECE)] + [(r, h * HALF, HALF) for r in range(R) for h in range(2)][1:]
    UNITS = len(UNIT)
    STAGED = 1 + NT * R // U
    DBANKS = 5
    assert HEADS[1] == 1 and HEADS[0] == HM and U * UNITS % DBANKS == 0 and UNITS == 2 * R
    LAYERS = [(W1, q1, k1, b1), (W2, q2, k2, b2)]

    etab = nc.dram_tensor("edge_table", (ETILES * P, 3), F32, kind="Internal").ap()
    qfill = [nc.dram_tensor(f"q_fill{l}", (STEPS * P + N, R * HEADS[l]), F32, kind="Internal").ap() for l in range(2)]
    ktab = [nc.dram_tensor(f"k_table{l}", (N * R, HEADS[l]), F32, kind="Internal").ap() for l in range(2)]
    xrtab = [nc.dram_tensor(f"xr_table{l}", (N * R, ROWW[l]), F32, kind="Internal").ap() for l in range(2)]
    cursor = nc.dram_tensor("cursor", (N + P, 1), F32, kind="Internal").ap()
    xttab = [nc.dram_tensor(f"x_turned{l}", (N - U * TN, DC * P), F32, kind="Internal").ap() for l in range(2)]

    ctx = ExitStack()
    with ctx:
        def sb(name, shape, dt=F32):
            return ctx.enter_context(nc.sbuf_tensor(name, shape, dt))

        def sem(name):
            return ctx.enter_context(nc.semaphore(name))

        banks = ctx.enter_context(nc.psum_tensor("banks", [P, 8, 512], F32))
        bank = [banks[:, i, :] for i in range(8)]

        ACCW = NT * RW
        big = sb("big", [P, ACCW])
        WORK = [DC * (NQK + R * D), 3 * DC * P, U * D]
        work = sb("work", [P, sum(WORK)])
        wsb, xT, xring = (work[:, sum(WORK[:i]):sum(WORK[:i + 1])] for i in range(3))
        wsb = wsb.rearrange("p (c f) -> p c f", c=DC)
        xT = xT.rearrange("p (u x) -> p u x", u=3)
        xring = xring.rearrange("p (u d) -> p u d", u=U)
        ring = sb("ring", [P, GS, RW])
        E_BANK = [5, 0, 1, 2]
        qk_node = sb("qk_node", [P, NT, 2 * R * HM])
        qkw = sb("qkw", [P, DC, 2, HM])
        row_idx = sb("row_idx", [P, STEPS], I32)
        dloc = sb("dloc", [P, STEPS + AHEAD])
        wE = sb("wE", [P, STEPS + AHEAD, HM])
        acc_at = sb("acc_at", [RC, 2, ROWS], I32)
        ev = wE[0:ROWS, 0:RC * P * 3 // HM, :].rearrange("r a b -> r (a b)").rearrange("r (c j a) -> r c j a", c=RC, a=3)
        rel = sb("rel", [P, RL])
        pen = sb("pen", [P, RL + 1])
        same = sb("same", [P, RL])
        flag = sb("flag", [R * HM, 8, ROWS + 1])
        EQ, EQPEN, CONT, CONTPEN, CARRY, CONTPEN_B, UNI, RUN = range(8)
        brow = sb("brow", [P, D])
        ident = sb("ident", [P, P])
        iota_n = sb("iota_n", [P, TN])
        start_at = sb("start_at", [P, NT], I32)
        kidx = sb("kidx", [P, 2, KG], I32)
        gidx = sb("gidx", [P, 2, GS // 2], I32)
        small = sb("small", [P, 512])

        zeros = big[:, 0:STEPS * R * HM]
        qf_raw = big[0:ROWS, 0:RL * R * HM]
        o = RL * R * HM
        qf = big[0:ROWS, o:o + RL * R * HM].rearrange("r (q x) -> r q x", x=RL)
        rows_i = big[0:EROWS, o:o + 3 * RL].bitcast(I32).rearrange("r (a x) -> r a x", a=3)
        ev_rows = big[0:EROWS, o + 3 * RL:o + 6 * RL].rearrange("r (x a) -> r x a", a=3)
        o1 = o + 6 * RL
        dst_i = big[0:TN, o1:o1 + HCOLS].bitcast(I32)
        dst_f = big[0:TN, o1 + HCOLS:o1 + 2 * HCOLS]
        d_y = big[0:TN, o1 + 2 * HCOLS:o1 + 3 * HCOLS]
        d_i = big[0:TN, o1 + 3 * HCOLS:o1 + 4 * HCOLS].bitcast(I32)
        d_hi = big[0:TN, o1 + 4 * HCOLS:o1 + 5 * HCOLS]
        o1 += 5 * HCOLS
        d_this = big[0:ORDER_P, o1:o1 + ORDER_C].bitcast(I32)
        d_next = big[0:ORDER_P, o1 + ORDER_C:o1 + 2 * ORDER_C].bitcast(I32)
        d_falls = big[0:ORDER_P, o1 + 2 * ORDER_C:o1 + 3 * ORDER_C]
        o += RL * R * HM
        ALPHA_AT = o
        alpha = big[0:ROWS, o:o + HM * RL].rearrange("r (h x) -> r h x", h=HM)
        o += HM * RL
        AMAX_AT = o
        amax = big[0:ROWS, o:o + HM * RL].rearrange("r (h x) -> r h x", h=HM)
        o += HM * RL
        K_AT = o
        k_edge = big[:, o:o + STEPS * HM]
        o += STEPS * HM
        s_before, s_equal, s_row, s_count = (k_edge[:, i * P:(i + 1) * P] for i in range(4))
        s_rowi = k_edge[:, 4 * P:5 * P].bitcast(I32)
        s_edge = k_edge[:, 5 * P:5 * P + 3]
        s_int = k_edge[:, 5 * P + 4:5 * P + 7].bitcast(I32)
        s_rank, s_base, s_pos, s_new, s_at, s_last, s_lane = (k_edge[:, 5 * P + 8 + i:5 * P + 9 + i] for i in range(7))
        kring = big[:, o:o + 2 * KG * HM]
        o += 2 * KG * HM
        key = big[0:ROWS, o:o + RL]
        assert o + RL <= ACCW
        deviation = same[0:TN, 14 * U:15 * U]
        one_hots = [work[:, sum(WORK) - AHEAD * h * TN:].rearrange("p (s h n) -> p s h n", s=AHEAD, h=h) for h in HEADS]
        hot = work[:, sum(WORK) - AHEAD * (HM + 1) * TN:sum(WORK) - AHEAD * HM * TN].rearrange("p (s n) -> p s n", s=AHEAD)
        assert AHEAD * (HM + 1) * TN <= WORK[2] and NT * D + AHEAD * HEADS[1] * TN <= sum(WORK)

        def residual(t):
            return work[0:TN, bass.ds(t * D, D)]

        HA = HPARTS[0] + HPARTS[0] % 2
        as_numbers = lambda ap, n: ap.bitcast(BF16)[:, 0:n * HA].rearrange("p (n a) -> p n a", a=HA)
        hlo = [as_numbers(ring[0:TN, i, 0:D], TN) for i in range(3)]
        hhi = [as_numbers(ring[0:TN, 3, i * 160:(i + 1) * 160], NT) for i in range(3)]
        lo_numbers = as_numbers(ring[0:TN, 4, 64:D], TN)
        hi_numbers = as_numbers(ring[0:TN, 3, 480:640], NT)
        d_lo_16, d_hi_16 = d_y.bitcast(BF16)[:, 0:HCOLS], d_i.bitcast(BF16)[:, 0:HCOLS]
        zero_bf = ring[0:TN, 4, 0:64].bitcast(BF16)
        below = same[0:TN, 0:TN]
        ones = same[0:TN, P:2 * P]
        counts = same[0:NT, 2 * P:2 * P + TN]
        q2_row, k2_row = xring[:, 0, :], xring[:, 1, :]

        def w_cols(r, first, n):
            return wsb[:, :, NQK + r * D + first:NQK + r * D + first + n]

        def qk_cols(l):
            n = 2 * R * HEADS[l]
            return wsb[:, :, NQK - n:NQK].rearrange("p c (a r h) -> p c a r h", a=2, r=R)

        def x_slot(k):
            return xring[:, k, :] if k < 3 else ring[:, k, 0:D]

        def xT_slot(k, rows):
            flat = xT[:, k, :] if k < 3 else xring[:, k, :]
            return flat[:, 0:DC * rows].rearrange("p (c n) -> p c n", c=DC)

        def turned_chunks(pair):
            return banks[:, 2 * pair:2 * pair + 2, :].rearrange("p b x -> p (b x)")[:, 0:DC * P]

        def cols(n, _at=[0]):
            _at[0] += n
            assert _at[0] <= 512
            return slice(_at[0] - n, _at[0])

        c_cnt, c_tot = cols(NT + 1), cols(NT + 1)
        c_inc, c_rp, c_y, c_f, c_St, c_cur = (cols(NT) for _ in range(6))
        c_it, c_t125, c_trash = (cols(NT) for _ in range(3))
        c_sio, c_ts, c_is, c_t8, c_tn, c_ta = (cols(RC) for _ in range(6))
        c_ends = cols(2 * R * HM)
        c_last = cols(R * HM)
        c_carry = cols(R * HM)
        c_z = cols(NT * HM)
        c_mv = cols(2 * NT)
        c_w2 = cols(2 * DC)

        dve_step, pool_step, act_gate, pool_gate, dve_gate = (sem(n) for n in
            ("dve_step", "pool_step", "act_gate", "pool_gate", "dve_gate"))
        consts_ready, edges_loaded, pads_set, dst_loaded, qk_loaded = (sem(n) for n in
            ("consts_ready", "edges_loaded", "pads_set", "dst_loaded", "qk_loaded"))
        zeros_set, fills_zeroed, hot_ready, hot_used, counts_done, sums_done = (sem(n) for n in
            ("zeros_set", "fills_zeroed", "hot_ready", "hot_used", "counts_done", "sums_done"))
        cnt_ready, etab_src, etab_stored, steps_ready, ev_gathered, rows_ready, turned, lanes_ready = (sem(n) for n in
            ("cnt_ready", "etab_src", "etab_stored", "steps_ready", "ev_gathered", "rows_ready", "turned", "lanes_ready"))
        start_ready, cursor_ready, sort_step, sort_moved = (sem(n) for n in
            ("start_ready", "cursor_ready", "sort_step", "sort_moved"))

        shared = {n: sem(n) for n in
                  ("ones_set q_scattered q_loaded k_stored k_ready qend_ready qend_turned qcarry_ready qcarry_turned "
                   "qcarry_taken k_added turned_taken w0_loaded end_ready end_turned carry_ready carry_turned diff_ready e_ready w_ready sums_zeroed "
                   "brow_loaded w_loaded k_turned e_turned x_used x_added S_built").split()}
        for n in ("x_loaded", "drow_loaded", "staged_stored"):
            shared[n] = [sem(f"{n}{i}") for i in range(U)]
        w2_ready = sem("w2_ready")
        piece_ones_set, w2_used, var_ready, dev_ready, numbers_set = (sem(n) for n in
            ("piece_ones_set", "w2_used", "var_ready", "dev_ready", "numbers_set"))
        w2_loaded = [sem(f"w2_loaded{i}") for i in range(2)]
        LS = []
        for l in range(2):
            s = {n: sem(f"{n}_{l}") for n in
                 ("xT_turned xT_ready qk_done qk_copied kidx_staged k_taken dense_done dense_out "
                  "hot_built gidx_staged step_done sum_added h_ready e_set " + ("u_ready exp_ready" if l == 0 else "h_out")).split()}
            for n, k in (("row_loaded", U if l == 0 else 0), ("k_gathered", 2),
                         ("row_gathered", GS), ("piece_stored", 3), ("h_stored", 0 if l == 0 else U), ("xT_stored", U)):
                s[n] = [sem(f"{n}{i}_{l}") for i in range(k)]
            LS.append({**shared, **s})

        def heads(ap, h):
            return ap.rearrange("p (h w) -> p h w", h=h)

        def node_sum(l, t):
            return heads(big[0:TN, bass.ds(t * ROWW[l], ROWW[l])], HEADS[l])[:, :, 0:D // HEADS[l]]

        def turns(eng, total, per):
            n = total // per
            with eng.Fori(0, n - 1) as i:
                yield i, False
            yield n - 1, True

        block = ctx.enter_context(nc.Block())

        @block.sync
        def _(sp):
            sp.dma_start(dst_i, dst.rearrange("(p c) -> p c", c=HCOLS)).then_inc(dst_loaded, 16)
            W_rows = W1.rearrange("r d f -> (r d) f")

            def load_w(i, c):
                sp.wait_ge(LS[0]["xT_turned"], DC * i + c + 1)
                sp.dma_start(xring[:, c % 3, :], W_rows[bass.ds(DC * P * i + c * P, P), :]
                             ).then_inc(LS[0]["row_loaded"][c % 3], 16)

            load_w(0, 0)
            for c in range(1, 3):
                load_w(0, c)
            sp.wait_ge(pads_set, 1)
            for a, arr in enumerate((src, etype, dst)):
                sp.dma_start(rows_i[0:EROWS - 1, a, :],
                             arr[0:(EROWS - 1) * RL].rearrange("(r x) -> r x", x=RL)).then_inc(edges_loaded, 16)
                sp.dma_start(rows_i[EROWS - 1:EROWS, a, 0:LAST],
                             arr[(EROWS - 1) * RL:E].rearrange("(r x) -> r x", r=1)).then_inc(edges_loaded, 16)
            sp.dma_start(d_this, dst[0:E - 1].rearrange("(p c) -> p c", c=ORDER_C)).then_inc(edges_loaded, 16)
            sp.dma_start(d_next, dst[1:E].rearrange("(p c) -> p c", c=ORDER_C)).then_inc(edges_loaded, 16)
            for c in range(3, DC):
                load_w(0, c)
            with sp.Fori(1, R) as i:
                for c in range(DC):
                    load_w(i, c)
            sp.dma_start(w_cols(0, 0, D), W1[0].rearrange("(c p) f -> p c f", p=P)).then_inc(LS[0]["w0_loaded"], 16)
            sp.dma_start(brow[0:TN, :], b1.partition_broadcast(TN)).then_inc(LS[0]["brow_loaded"], 16)

            for l in range(2):
                s = LS[l]
                H = HEADS[l]
                W0 = WT if l == 0 else 0
                xr_rows = xrtab[l].rearrange("(n r) w -> n r w", r=R)
                for i in range(3):
                    sp.sem_inc(s["piece_stored"][i], 16)

                for k in range(U):
                    sp.sem_inc(s["xT_stored"][k], 16)

                def xT_place(t):
                    return xttab[l].rearrange("n f -> (n f)").rearrange("(t p x) -> t p x", p=P, x=DC * TN)[bass.ds(t, 1)
                                                                                        ].rearrange("o p x -> (o p) x")

                def store_xT(t, k):
                    sp.wait_ge(s["xT_ready"], 2 + W0 + t + 1)
                    sp.dma_start(xT_place(t), xT_slot(k, TN).rearrange("p c n -> p (c n)")).then_inc(s["xT_stored"][k], 16)

                def store_piece(t, k):
                    sp.wait_ge(s["qk_copied"], 2 + W0 + t + 1)
                    sp.dma_start(xr_rows[bass.ds(t * TN, TN), 0, 0:HC0[l]], ring[0:TN, 5 + PAT[k], 0:HC0[l]]
                                 ).then_inc(s["piece_stored"][PAT[k]], 16)

                if l == 0:
                    def load_x(t, k):
                        sp.wait_ge(s["xT_turned"], WT + t + 1)
                        sp.dma_start(x_slot(k)[0:TN, :], x[bass.ds(t * TN, TN), :]).then_inc(s["row_loaded"][k], 16)

                    for k in range(3):
                        load_x(k, k)
                    sp.wait_ge(etab_src, 1)
                    sp.dma_start(etab.rearrange("(r x) a -> r x a", x=RL), ev_rows).then_inc(etab_stored, 16)
                    for i, last in turns(sp, NT, U):
                        for k in range(U):
                            if not last or k + 3 < U:
                                load_x(U * i + k + 3, (k + 3) % U)
                            if not last:
                                store_xT(U * i + k, k)
                            store_piece(U * i + k, k)
                else:
                    for i, last in turns(sp, NT, U):
                        for k in range(U):
                            if not last:
                                store_xT(U * i + k, k)
                            store_piece(U * i + k, k)
                for i in range(U):
                    sp.sem_inc(s["staged_stored"][i], 16)
                    sp.sem_inc(s["drow_loaded"][i], 16)
                sp.wait_ge(s["qk_copied"], 2 + W0 + NT)
                sp.dma_start(ktab[l].rearrange("(t p r) h -> p t (r h)", p=TN, r=R),
                             qk_node[0:TN, :, R * H:2 * R * H]).then_inc(s["k_stored"], 16)
                sp.wait_ge(s["xT_turned"], (3 if l == 0 else U) + W0 + NT)
                for k in range(U):
                    sp.wait_ge(s["xT_stored"][k], 16 * (NT // U))
                sp.wait_ge(s["q_scattered"], 16 * NT * (l + 1))
                sp.dma_start(qf_raw[:, 0:RL * R * H], qfill[l][0:STEPS * P, :].rearrange("(r x) q -> r (x q)", x=RL)
                             ).then_inc(s["q_loaded"], 16)
                if l == 0:
                    for row, arr in ((q2_row, q2), (k2_row, k2)):
                        sp.dma_start(row, arr.rearrange("f h -> (f h)").partition_broadcast(P)).then_inc(qk_loaded, 16)
                else:
                    sp.dma_start(brow[0:TN, :], b2.partition_broadcast(TN)).then_inc(s["brow_loaded"], 16)
                for i in range(3):
                    sp.wait_ge(s["piece_stored"][i], 16 * (1 + (NT // U) * PAT.count(i)))
                W2_rows = W2.rearrange("r d f -> (r d) f")

                def load_w2(r, c):
                    sp.wait_ge(w2_used, 2 * (DC * r + c + 1))
                    sp.dma_start(ring[:, 5 + c % 2, 0:D], W2_rows[bass.ds(D * r + c * P, P), :]).then_inc(w2_loaded[c % 2], 16)

                def load_dense(i, k):
                    sp.wait_ge(s["dense_done"], 2 * UNITS + UNITS * (U * (i - 1) + k + 1))
                    sp.dma_start(xT_slot(k, TN).rearrange("p c n -> p (c n)"), xT_place(U * (i - 1) + k)
                                 ).then_inc(s["drow_loaded"][k], 16)

                def dense_turn(i, tile0, last=False, w2_tile=None):
                    for k in range(U):
                        for r in range(R):
                            unit = R * k + r
                            first = HC0[l] if r == 0 else 0
                            sp.wait_ge(s["dense_out"], DBANKS + UNITS * (U * i + k) + 2 * r + 2)
                            sp.dma_start(xr_rows[bass.ds((tile0 + k) * TN, TN), r, first:ROWW[l]],
                                         ring[0:TN, unit % U, first:ROWW[l]]).then_inc(s["staged_stored"][unit % U], 16)
                        if not last:
                            load_dense(i + 1, k)
                        if w2_tile is not None:
                            load_w2(w2_tile, k)
                            for c in range(U, DC) if k == U - 1 else ():
                                load_w2(w2_tile, c)

                dense_turn(0, NT - U)
                with sp.Fori(1, 1 + R) as i:
                    dense_turn(i, U * (i - 1), w2_tile=i - 1 if l == 0 else None)
                for i in range(1 + R, NT // U):
                    dense_turn(i, U * (i - 1), i == NT // U - 1)
                if l == 0:
                    spread = STEPS // (WT + 4)
                    sp.wait_ge(s["dense_done"], UNITS * (NT + 2))
                    for r in range(R):
                        for c in range(DC):
                            sp.wait_ge(s["sum_added"], AHEAD + spread * (DC * r + c + 1))
                            sp.dma_start(w_cols(r, 0, D)[:, c, :], W2[r, c * P:(c + 1) * P, :]
                                         ).then_inc(LS[1]["w0_loaded" if r == 0 else "w_loaded"], 16)
                else:
                    for k in range(U):
                        sp.sem_inc(s["h_stored"][k], 16)

                    sp.wait_ge(s["dense_done"], UNITS * (NT + 2))
                    spread = STEPS // (NT + 2)
                    for k in range(U):
                        sp.sem_inc(s["x_loaded"][k], 16)
                    with sp.Fori(0, NT // U) as i:
                        for k in range(U):
                            t = U * i + k
                            sp.wait_ge(s["sum_added"], AHEAD + spread * t + 1)
                            sp.wait_ge(s["x_loaded"][k], 16 * (i + 1))
                            sp.dma_start(residual(t), x[bass.ds(t * TN, TN), :]).then_inc(s["x_loaded"][k], 16)
                    with sp.Fori(0, NT // U) as i:
                        for k in range(U):
                            sp.wait_ge(s["h_out"], U * i + k + 1)
                            sp.dma_start(out[bass.ds((U * i + k) * TN, TN), :],
                                         ring[0:TN, k, 0:D]).then_inc(s["h_stored"][k], 16)
                    for k in range(U):
                        sp.wait_ge(s["h_stored"][k], 16 * (1 + NT // U))

        @block.tensor
        def _(pe):
            for l in range(2):
                s = LS[l]
                H = HEADS[l]
                HW = HWS[l]
                W0 = WT if l == 0 else 0

                def turn(n, xs, pair, rows):
                    pe.wait_ge(s["xT_ready"], n + 1)
                    for c in range(DC):
                        last = pe.transpose(turned_chunks(pair)[:, c * P:c * P + rows],
                                            x_slot(xs)[0:rows, c * P:(c + 1) * P], ident[0:rows, 0:rows])
                    last.then_inc(s["xT_turned"], 1)

                def w_turn(i, c):
                    pe.wait_ge(s["row_loaded"][c % 3], 16 * (DC // 3 * i + c // 3 + 1))
                    turn(DC * i + c, c % 3, c % 3, P)

                def x_turn(i, k):
                    if l == 0:
                        pe.wait_ge(s["row_loaded"][k], 16 * ((WT // 3 if k < 3 else 0) + i + 1))
                    else:
                        pe.wait_ge(LS[0]["h_ready"], 2 + U * i + k + 1)
                    turn(W0 + U * i + k, k, PAT[k], TN)

                def products(n, slot, acc, rows, rhs, width, fresh):
                    pe.wait_ge(s["xT_ready"], n + 3)
                    pe.wait_ge(s["qk_copied"], n + 2 if fresh else n + 1)
                    for c in range(DC):
                        last = pe.matmul(bank[acc][0:rows, 0:width], xT_slot(slot, rows)[:, c, :], rhs(c),
                                         start=(c == 0), stop=(c == DC - 1))
                    last.then_inc(s["qk_done"], 1)

                def w_rhs(c):
                    return qkw[:, c, :, :]

                def x_rhs(c):
                    return wsb[:, c, NQK - 2 * R * H:NQK + PIECE]

                def hist(n):
                    for part in range(3):
                        pe.wait_ge(hot_ready, 3 * n + part + 1)
                        for j in range(HPARTS[part]):
                            last = pe.matmul(bank[7][0:NT, 0:TN], hhi[part][:, :, j], hlo[part][:, :, j],
                                             start=False, stop=False)
                        last.then_inc(hot_used, 1)

                pe.sem_inc(s["xT_turned"], 3 if l == 0 else U)
                if l == 0:
                    pe.sem_inc(hot_used, 3)
                    pe.wait_ge(consts_ready, 2)
                    pe.wait_ge(qk_loaded, 32)
                    pe.matmul(bank[7][0:NT, 0:TN], zero_bf[:, 0:NT], zero_bf[:, 0:TN], start=True, stop=False)
                    w_turn(0, 0)
                    for i, last_turn in turns(pe, WT, DC):
                        for c in range(DC):
                            if c < DC - 1:
                                w_turn(i, c + 1)
                            elif not last_turn:
                                w_turn(i + 1, 0)
                            products(DC * i + c, c % 3, 6, P, w_rhs, 2 * H, True)
                            if c < DC - 1 or not last_turn:
                                hist(DC * i + c)
                    pe.matmul(bank[7][0:NT, 0:TN], zero_bf[:, 0:NT], zero_bf[:, 0:TN], start=False, stop=True
                              ).then_inc(counts_done, 1)
                    x_turn(0, 0)
                    pe.wait_ge(cnt_ready, 1)
                    pe.transpose(bank[4][0:TN, 256:256 + NT], counts, ident[0:NT, 0:NT]).then_inc(sums_done, 1)
                    pe.wait_ge(cnt_ready, 2)
                    cnt = small[0:TN, c_cnt]
                    pe.matmul(bank[5][0:TN, 320:320 + NT], below, cnt[:, 0:NT], start=True, stop=True)
                    pe.matmul(bank[5][0:P, 384:385 + NT], ones, cnt, start=True, stop=True).then_inc(sums_done, 1)
                    pe.wait_ge(cnt_ready, 3)
                else:
                    x_turn(0, 0)
                    pe.wait_ge(w2_ready, 1 + R)
                pe.wait_ge(s["w0_loaded"], 16 * (1 + DC * l))

                def x_turns(i, last_turn=False):
                    for k in range(U):
                        if k < U - 1:
                            x_turn(i, k + 1)
                        elif not last_turn:
                            x_turn(i + 1, 0)
                        products(W0 + U * i + k, k, 6 + k % 2, TN, x_rhs, 2 * R * H + PIECE, k == 0)

                MEET = 2
                with pe.Fori(0, MEET) as i:
                    x_turns(i)
                if l == 0:
                    pe.wait_ge(rows_ready, 1)
                    for c in range(RC):
                        pe.transpose(bank[2][:, c * ROWS:(c + 1) * ROWS], ev[:, c, :, 0], ident[0:ROWS, 0:ROWS])
                        pe.transpose(bank[3][:, c * ROWS:(c + 1) * ROWS], ev[:, c, :, 2], ident[0:ROWS, 0:ROWS])
                    ends = small[0:ROWS, c_ends]
                    pe.transpose(bank[4][0:RC, 256:256 + ROWS], small[0:ROWS, c_ta], ident[0:ROWS, 0:ROWS])
                    pe.transpose(bank[4][0:R * HM, 384:384 + ROWS], ends[:, 0:R * HM], ident[0:ROWS, 0:ROWS])
                    pe.transpose(bank[5][0:R * HM, 0:ROWS], ends[:, R * HM:2 * R * HM], ident[0:ROWS, 0:ROWS]
                                 ).then_inc(turned, 1)
                    pe.wait_ge(s["turned_taken"], 1)
                with pe.Fori(MEET, NT // U - 1) as i:
                    x_turns(i)
                x_turns(NT // U - 1, True)

                pe.wait_ge(s["w_loaded"], 16 * DC * (1 + (R - 1) * l))

                def dense(n, k, between):
                    for u, (r, first, n_cols) in enumerate(UNIT):
                        b = (UNITS * k + u) % DBANKS
                        pe.wait_ge(s["dense_out"], UNITS * n + u + 1)
                        for c in range(DC):
                            last = pe.matmul(bank[b][0:TN, 0:n_cols], xT_slot(k, TN)[:, c, :],
                                             w_cols(r, first, n_cols)[:, c, :],
                                             start=(c == 0), stop=(c == DC - 1))
                        last.then_inc(s["dense_done"], 1)
                        if (k, u) in between:
                            between[k, u]()

                def dense_turn(i, last_turn=False, between=()):
                    for k in range(U):
                        pe.wait_ge(s["drow_loaded"][k], 16 * (l * (NT // U) + i + 1))
                        dense(U * i + k, k, between)

                with pe.Fori(0, 1) as i:
                    dense_turn(i)
                pe.wait_ge(s["qend_ready"], l + 1)
                pe.transpose(bank[5][0:R * H, 0:ROWS], small[0:ROWS, c_last][:, 0:R * H], ident[0:ROWS, 0:ROWS]
                             ).then_inc(s["qend_turned"], 1)
                pe.wait_ge(s["qcarry_ready"], l + 1)
                pe.transpose(bank[5][0:ROWS, 0:R * H], flag[0:R * H, CARRY, 0:ROWS], ident[0:R * H, 0:R * H]
                             ).then_inc(s["qcarry_turned"], 1)
                pe.wait_ge(s["qcarry_taken"], l + 1)
                with pe.Fori(1, NT // U - 1) as i:
                    dense_turn(i)

                def turn_k(h):
                    if h == 0:
                        pe.wait_ge(s["k_ready"], l + 1)
                    else:
                        pe.wait_ge(s["k_added"], HM * l + h)
                    k_lanes = k_edge[:, 0:STEPS * H].rearrange("p (r c h) -> p c h r", c=RC, h=H)
                    for c in range(RC):
                        last = pe.transpose(bank[5][0:ROWS, c * P:(c + 1) * P], k_lanes[:, c, h, :], ident[:, :])
                    last.then_inc(s["k_turned"], 1)

                def turn_ends(w):
                    pe.wait_ge(s["end_ready"], 2 * l + w + 1)
                    pe.transpose(bank[5][0:H, 0:ROWS], small[0:ROWS, c_last][:, 0:H], ident[0:ROWS, 0:ROWS]
                                 ).then_inc(s["end_turned"], 1)

                def turn_carry(w):
                    pe.wait_ge(s["carry_ready"], 2 * l + w + 1)
                    pe.transpose(bank[5][0:ROWS, 0:H], flag[0:H, CARRY, 0:ROWS], ident[0:H, 0:H]
                                 ).then_inc(s["carry_turned"], 1)

                def turn_e(h):
                    pe.wait_ge(s["e_ready"], l + 1)
                    for c in range(RC):
                        last = pe.transpose(bank[E_BANK[h]][:, c * ROWS:(c + 1) * ROWS], amax[:, h, c * P:(c + 1) * P],
                                            ident[0:ROWS, 0:ROWS])
                    last.then_inc(s["e_turned"], 1)

                meets = [lambda h=h: turn_k(h) for h in range(H)]
                meets += [lambda f=f, w=w: f(w) for w in range(2) for f in (turn_ends, turn_carry)]
                if H > 1:
                    spots = [(3, 0), (3, 1), (3, 2), (3, 3), (3, 5), (4, 0), (4, 2), (4, 3)]
                else:
                    meets.append(lambda: turn_e(0))
                    spots = [(3, 2), (3, 3), (3, 4), (3, 5), (4, 0), (4, 2)]
                pe.sem_inc(s["step_done"], GS)
                dense_turn(NT // U - 1, True, dict(zip(spots, meets)))
                pe.wait_ge(s["dense_out"], DBANKS + UNITS * NT)
                if H > 1:
                    for h in range(H):
                        turn_e(h)
                pe.wait_ge(s["w_ready"], l + 1)

                HB2 = ROWW[l] // 2
                with pe.Fori(0, STEPS // GS) as i:
                    for j in range(GS):
                        st = GS * i + j
                        slot = j % AHEAD
                        pe.wait_ge(s["row_gathered"][j], 16 * (i + 1))
                        pe.wait_ge(s["S_built"] if H > 1 else s["hot_built"], st + 1 + (AHEAD if H > 1 else 0))
                        pe.wait_ge(s["sum_added"], st + 1)
                        for half in range(2):
                            for m in range(max(H // 2, 1)):
                                h = half * (H // 2) + m
                                w = HW if H > 1 else HB2
                                last = pe.matmul(bank[2 * slot + half][0:TN, m * w:(m + 1) * w],
                                                 one_hots[l][:, slot, h, :],
                                                 ring[:, j, half * HB2 + m * w:half * HB2 + (m + 1) * w],
                                                 start=True, stop=True)
                        last.then_inc(s["step_done"], 1)

        @block.scalar
        def _(act):
            def gate(sm, value):
                act.wait_ge(sm, value)
                act.sem_inc(act_gate, 1)

            for a, arr in enumerate((q1, k1)):
                act.dma_start(qkw[:, :, a, :], arr.rearrange("(c p) h -> p c h", p=P), allow_slow_non_contiguous=True
                              ).then_inc(qk_loaded, 16)

            act.wait_ge(consts_ready, 1)
            nc.scalar.copy(hi_numbers, small[0:TN, c_it].unsqueeze(2).to_broadcast([TN, NT, HA])).then_inc(numbers_set, 1)
            nc.scalar.copy(lo_numbers, iota_n[0:TN, :].unsqueeze(2).to_broadcast([TN, TN, HA])).then_inc(numbers_set, 1)

            for l in range(2):
                s = LS[l]
                H = HEADS[l]
                W0 = WT if l == 0 else 0
                act.sem_inc(s["xT_ready"], 2)
                act.sem_inc(s["qk_copied"], 2)
                act.sem_inc(s["dense_out"], DBANKS)
                if H > 1:
                    act.sem_inc(s["S_built"], AHEAD)
                act.sem_inc(s["qk_done"], 2)

                def take(n, pair, slot, rows):
                    act.wait_ge(s["xT_turned"], n + 1 + (3 if l == 0 else U))
                    act.wait_ge(s["qk_done"], n + 1)
                    nc.scalar.copy(xT_slot(slot, rows), turned_chunks(pair).rearrange("p (c n) -> p c n", c=DC)[:, :, 0:rows]
                                   ).then_inc(s["xT_ready"], 1)

                if l == 0:
                    take(0, 0, 0, P)
                    for i, last_turn in turns(act, WT, DC):
                        for c in range(DC):
                            n = DC * i + c
                            if c < DC - 1 or not last_turn:
                                take(n + 1, (c + 1) % 3, (c + 1) % 3, P)
                            gate(s["qk_done"], n + 3)
                            nc.scalar.copy(qk_cols(0)[:, c, :, bass.ds(i, 1), :].rearrange("p a r h -> p a (r h)"),
                                           bank[6][:, 0:2 * H].rearrange("p (a h) -> p a h", a=2)
                                           ).then_inc(s["qk_copied"], 1)

                def exp_hidden(t, k):
                    act.wait_ge(LS[0]["h_ready"], t + 1)
                    gate(LS[0]["u_ready"], t + 1)
                    nc.scalar.activation(heads(ring[0:TN, PAT[k], 0:D], HEADS[0]), node_sum(0, t), ACT.Exp
                                         ).then_inc(LS[0]["exp_ready"], 1)

                def x_turns(i, last_turn=False):
                    for k in range(U):
                        t = U * i + k
                        n = W0 + t
                        if l == 1 and (k + 2 < U or not last_turn):
                            exp_hidden(t + 2, (k + 2) % U)
                        if k < U - 1 or not last_turn:
                            act.wait_ge(s["xT_stored"][(k + 1) % U], 16 * (i + 1 + (k + 1) // U))
                            take(n + 1, PAT[(k + 1) % U], (k + 1) % U, TN)
                        gate(s["qk_done"], n + 3)
                        acc = bank[6 + k % 2][0:TN]
                        nc.scalar.copy(qk_node[0:TN, bass.ds(t, 1), 0:2 * R * H].rearrange("p a b -> p (a b)"), acc[:, 0:2 * R * H])
                        act.wait_ge(s["piece_stored"][PAT[k]], 16 * (PAT.count(PAT[k]) * i + PAT[:k].count(PAT[k]) + 1))
                        nc.scalar.copy(ring[0:TN, 5 + PAT[k], 0:PIECE], acc[:, 2 * R * H:2 * R * H + PIECE]
                                       ).then_inc(s["qk_copied"], 1)

                if l == 0:
                    act.wait_ge(piece_ones_set, 1)
                else:
                    exp_hidden(0, 0)
                    exp_hidden(1, 1)
                take(W0, 0, 0, TN)
                def load_w(c):
                    act.dma_start(wsb[:, bass.ds(c, 1), NQK + D:].rearrange("p o (r f) -> p (o r) f", r=R - 1),
                                  W1[1:R, bass.ds(c * P, P), :].rearrange("r p f -> p r f")).then_inc(s["w_loaded"], 16)

                with act.Fori(0, NT // U - 1) as i:
                    x_turns(i)
                    if l == 0:
                        load_w(i)
                if l == 0:
                    for c in range(NT // U - 1, DC):
                        load_w(c)
                x_turns(NT // U - 1, True)

                act.sem_inc(s["dense_done"], 2 * UNITS)

                def exponentials():
                    act.wait_ge(s["diff_ready"], l + 1)
                    nc.scalar.activation(amax[:, 0:H, :], alpha[:, 0:H, :], ACT.Exp).then_inc(s["e_ready"], 1)

                def dense_turn(i, last_turn=False, between=()):
                    for k in range(U):
                        n = U * i + k
                        for u, (r, first, n_cols) in enumerate(UNIT):
                            unit = R * k + r
                            slot = unit % U
                            if u % 2 == 0:
                                act.wait_ge(s["staged_stored"][slot], 16 * (l * STAGED + R * i + unit // U + 1))
                            act.wait_ge(s["dense_done"], 2 * UNITS + UNITS * n + u + 1)
                            o_ = ring[0:TN, slot, first:first + n_cols]
                            i_ = bank[(UNITS * k + u) % DBANKS][0:TN, 0:n_cols]
                            if H > 1:
                                h0, nh = first // PIECE, n_cols // PIECE
                                o_ = heads(ring[0:TN, slot, 0:ROWW[l]], H)[:, h0:h0 + nh, 0:PIECE]
                                i_ = heads(i_, nh)
                            nc.scalar.copy(o_, i_).then_inc(s["dense_out"], 1)
                            if (k, u) in between:
                                between[k, u]()

                act.wait_ge(s["ones_set"], l + 1)
                with act.Fori(0, NT // U - 1) as i:
                    dense_turn(i)
                dense_turn(NT // U - 1, True, {(U - 1, 4 if H > 1 else 1): exponentials})

                if H > 1:
                    act.wait_ge(s["w_ready"], l + 1)
                    with act.Fori(0, STEPS // GS) as i:
                        for j in range(GS):
                            st = GS * i + j
                            slot = j % AHEAD
                            act.wait_ge(s["hot_built"], st + 1)
                            gate(s["step_done"], st + 1 + GS - AHEAD)
                            for h in range(H):
                                last = nc.scalar.activation(one_hots[l][:, slot, h, :], hot[:, slot, :], ACT.Copy,
                                                            scale=wE[:, bass.ds(st, 1), h:h + 1].rearrange("p a b -> p (a b)"))
                            last.then_inc(s["S_built"], 1)

                if l == 1:
                    mv = small[0:TN, c_mv].rearrange("p (t a) -> p t a", a=2)
                    for i, last_turn in turns(act, NT, U):
                        for k in range(U):
                            t = U * i + k
                            if k == 0:
                                act.wait_ge(var_ready, i + 1)
                                nc.scalar.activation(deviation, deviation, ACT.Sqrt).then_inc(dev_ready, 1)
                                act.wait_ge(s["h_ready"], i + 1)
                            gate(s["h_stored"][k], 16 * (i + 1))
                            m = mv[:, bass.ds(t, 1), :].rearrange("p a b -> p (a b)")
                            nc.scalar.activation(heads(ring[0:TN, k, 0:D], H), node_sum(l, t), ACT.Identity,
                                                 scale=m[:, 1:2], bias=m[:, 0:1]).then_inc(s["h_out"], 1)

        @block.gpsimd
        def _(pool):
            chain = [0]

            def link(ins):
                chain[0] += 1
                ins.then_inc(pool_step, 1)
                pool.wait_ge(pool_step, chain[0])

            def gate(sm, value):
                pool.wait_ge(sm, value)
                pool.sem_inc(pool_gate, 1)

            link(nc.gpsimd.iota(iota_n[:, :], [[1, TN]], base=0, channel_multiplier=0,
                                allow_small_or_imprecise_dtypes=True))
            link(nc.gpsimd.iota(small[:, c_it], [[1, NT]], base=0, channel_multiplier=0,
                                allow_small_or_imprecise_dtypes=True))
            pool.sem_inc(consts_ready, 1)
            link(nc.gpsimd.memset(ident[:, :], 0.0))
            link(nc.gpsimd.affine_select(out=ident[:, :], in_=ident[:, :], compare_op=ALU.not_equal, fill=1.0,
                                         base=0, pattern=[[-1, P]], channel_multiplier=1))
            link(nc.gpsimd.memset(below, 1.0))
            link(nc.gpsimd.affine_select(out=below, in_=below, compare_op=ALU.is_gt, fill=0.0,
                                         base=0, pattern=[[1, TN]], channel_multiplier=-1))
            link(nc.gpsimd.memset(ones, 1.0))
            link(nc.gpsimd.memset(zero_bf, 0.0))
            link(nc.gpsimd.iota(small[:, c_t125], [[P, NT]], base=0, channel_multiplier=0,
                                allow_small_or_imprecise_dtypes=True))
            link(nc.gpsimd.iota(small[:, c_trash], [[TN, NT]], base=STEPS * P, channel_multiplier=1,
                                allow_small_or_imprecise_dtypes=True))
            link(nc.gpsimd.iota(small[:, c_sio], [[1, RC]], base=0, channel_multiplier=RC,
                                allow_small_or_imprecise_dtypes=True))
            pool.sem_inc(consts_ready, 1)
            nc.gpsimd.memset(zeros, 0.0).then_inc(zeros_set, 1)
            pool.wait_ge(zeros_set, 1)
            for m in range(2):
                pool.dma_start(qfill[m][0:STEPS * P, :].rearrange("(p y) q -> p (y q)", p=P),
                               zeros[:, 0:STEPS * R * HEADS[m]]).then_inc(fills_zeroed, 16)

            pool.wait_ge(etab_stored, 16)
            pool.wait_ge(cursor_ready, 1)

            TILE_MOVES = 16 * 7

            def place(i, n):
                first = i * P
                seen = {sort_step: 0, sort_moved: 0}

                def then(ins, by):
                    done = sort_step if by == 1 else sort_moved
                    seen[done] += by
                    ins.then_inc(done, by)
                    if by == 1:
                        pool.wait_ge(sort_step, seen[done])
                    else:
                        gate(sort_moved, 16 + TILE_MOVES * i + seen[done])

                def row_sum(v):
                    w = P // 2
                    while w:
                        then(nc.gpsimd.tensor_tensor(v[:, 0:w], v[:, 0:w], v[:, w:2 * w], ALU.add), 1)
                        w //= 2

                if n < P:
                    then(nc.gpsimd.memset(s_row, -1.0), 1)
                for a, arr in enumerate((src, etype, dst)):
                    then(pool.dma_start(s_int[0:n, a:a + 1], arr[bass.ds(first, n)].rearrange("(p o) -> p o", o=1),
                                        allow_slow_non_contiguous=True), 16)
                then(pool.dma_start(s_rowi[0:n, 0:n], dst[bass.ds(first, n)].partition_broadcast(n)), 16)
                then(nc.gpsimd.tensor_copy(s_row[0:n, 0:n], s_rowi[0:n, 0:n]), 1)
                then(nc.gpsimd.tensor_copy(s_edge[0:n, :], s_int[0:n, :]), 1)
                then(nc.gpsimd.tensor_scalar(s_edge[0:n, 0:1], s_edge[0:n, 0:1], float(R), s_edge[0:n, 1:2],
                                             ALU.mult, ALU.add), 1)
                then(nc.gpsimd.tensor_scalar(s_equal[0:n, :], s_row[0:n, :], s_edge[0:n, 2:3], None, ALU.is_equal), 1)
                then(nc.gpsimd.tensor_tensor(s_count[0:n, :], s_equal[0:n, :], s_before[0:n, :], ALU.mult), 1)
                row_sum(s_equal[0:n, :])
                row_sum(s_count[0:n, :])
                then(nc.gpsimd.indirect_dma_start(
                    s_base[0:n], None, cursor[0:N], bass.IndirectOffsetOnAxis(ap=s_int[0:n, 2:3], axis=0)), 16)
                then(nc.gpsimd.tensor_tensor(s_rank[0:n], s_base[0:n], s_count[0:n, 0:1], ALU.add), 1)
                then(nc.gpsimd.tensor_copy(s_pos[0:n].bitcast(I32), s_rank[0:n]), 1)
                then(nc.gpsimd.tensor_tensor(s_new[0:n], s_base[0:n], s_equal[0:n, 0:1], ALU.add), 1)
                then(nc.gpsimd.indirect_dma_start(
                    etab, bass.IndirectOffsetOnAxis(ap=s_pos[0:n].bitcast(I32), axis=0), s_edge[0:n, :], None), 16)
                then(nc.gpsimd.tensor_tensor(s_last[0:n], s_count[0:n, 0:1], s_equal[0:n, 0:1], ALU.subtract), 1)
                then(nc.gpsimd.tensor_scalar(s_last[0:n], s_last[0:n], -1.0, None, ALU.is_equal), 1)
                then(nc.gpsimd.tensor_tensor(s_rank[0:n], s_edge[0:n, 2:3], s_lane[0:n], ALU.subtract), 1)
                then(nc.gpsimd.tensor_tensor(s_rank[0:n], s_rank[0:n], s_last[0:n], ALU.mult), 1)
                then(nc.gpsimd.tensor_tensor(s_rank[0:n], s_rank[0:n], s_lane[0:n], ALU.add), 1)
                then(nc.gpsimd.tensor_copy(s_at[0:n].bitcast(I32), s_rank[0:n]), 1)
                then(nc.gpsimd.indirect_dma_start(
                    cursor, bass.IndirectOffsetOnAxis(ap=s_at[0:n].bitcast(I32), axis=0), s_new[0:n], None), 16)
                assert seen[sort_moved] == TILE_MOVES
                pool.sem_clear(sort_step)

            out_of_order = pool.value_load(small[0:1, c_tot][:, NT:NT + 1].bitcast(I32), min_val=0, max_val=E)
            with pool.If(out_of_order > 0):
                nc.gpsimd.memset(s_before, 1.0).then_inc(sort_step, 1)
                pool.wait_ge(sort_step, 1)
                nc.gpsimd.affine_select(out=s_before, in_=s_before, compare_op=ALU.is_gt, fill=0.0,
                                        base=0, pattern=[[-1, P]], channel_multiplier=1).then_inc(sort_step, 1)
                pool.wait_ge(sort_step, 2)
                nc.gpsimd.iota(s_lane, [[1, 1]], base=N, channel_multiplier=1,
                               allow_small_or_imprecise_dtypes=True).then_inc(sort_step, 1)
                pool.wait_ge(sort_step, 3)
                pool.dma_start(cursor[0:N].rearrange("(t p) o -> p (t o)", p=TN), small[0:TN, c_cur],
                               allow_slow_non_contiguous=True).then_inc(sort_moved, 16)
                pool.wait_ge(sort_moved, 16)
                pool.sem_clear(sort_step)
                with pool.Fori(0, E // P) as i:
                    place(i, P)
                if E % P:
                    place(E // P, E % P)

            pool.wait_ge(steps_ready, 1)
            etab_rows = etab.rearrange("(i j) a -> i (j a)", j=P)
            for c in range(RC):
                nc.gpsimd.indirect_dma_start(
                    ev[:, c, :, :].rearrange("r j a -> r (j a)"), None, etab_rows,
                    bass.IndirectOffsetOnAxis(ap=small[0:ROWS, c_is].bitcast(I32)[:, c:c + 1], axis=0),
                ).then_inc(ev_gathered, 16)

            for l in range(2):
                s = LS[l]
                H = HEADS[l]
                pool.wait_ge(start_ready, 1)
                pool.wait_ge(fills_zeroed, 32)
                for t in range(NT):
                    pool.wait_ge(s["qk_copied"], 2 + (WT if l == 0 else 0) + t + 1)
                    nc.gpsimd.indirect_dma_start(
                        qfill[l], bass.IndirectOffsetOnAxis(ap=start_at[0:TN, t:t + 1], axis=0),
                        qk_node[0:TN, t, 0:R * H], None).then_inc(s["q_scattered"], 16)

                pool.wait_ge(s["k_stored"], 16 * (l + 1))
                pool.wait_ge(lanes_ready, 1)
                pool.sem_inc(s["k_taken"], 2)

                def fetch(m, g, turn_):
                    gate(s["k_taken"], m + 1)
                    nc.gpsimd.tensor_copy(kidx[:, g, :], row_idx[:, bass.ds(m * KG, KG)]).then_inc(s["kidx_staged"], 1)
                    gate(s["kidx_staged"], m + 1)
                    for j in range(KG):
                        nc.gpsimd.indirect_dma_start(
                            kring[:, (g * KG + j) * H:(g * KG + j + 1) * H], None, ktab[l],
                            bass.IndirectOffsetOnAxis(ap=kidx[:, g, j:j + 1], axis=0)).then_inc(s["k_gathered"][g], 16)

                def take(m, g, turn_):
                    gate(s["k_gathered"][g], 16 * KG * (turn_ + 1))
                    nc.gpsimd.tensor_copy(k_edge[:, bass.ds(m * KG * H, KG * H)],
                                          kring[:, g * KG * H:(g + 1) * KG * H]).then_inc(s["k_taken"], 1)

                fetch(0, 0, 0)
                for i, last in turns(pool, STEPS // KG, 2):
                    fetch(2 * i + 1, 1, i)
                    take(2 * i, 0, i)
                    if not last:
                        fetch(2 * i + 2, 0, i + 1)
                    take(2 * i + 1, 1, i)
                pool.wait_ge(s["k_taken"], 2 + STEPS // KG)
                pool.sem_inc(s["k_ready"], 1)

                pool.wait_ge(s["k_added"], HM * l + H)
                nc.gpsimd.memset(big[0:TN, K_AT:ACCW], 0.0).then_inc(s["sums_zeroed"], 1)
                pool.wait_ge(s["e_ready"], l + 1)
                nc.gpsimd.memset(big[0:TN, ALPHA_AT:AMAX_AT], 0.0).then_inc(s["sums_zeroed"], 1)

                for i in range(U):
                    pool.wait_ge(s["staged_stored"][i], 16 * (l + 1) * STAGED)
                half = GS // 2
                with pool.Fori(0, STEPS // GS) as i:
                    for g in range(2):
                        m = 2 * i + g
                        gate(s["step_done"], half * (m + 1))
                        nc.gpsimd.tensor_copy(gidx[:, g, :], row_idx[:, bass.ds(m * half, half)]
                                              ).then_inc(s["gidx_staged"], 1)
                        gate(s["gidx_staged"], m + 1)
                        for j in range(half):
                            nc.gpsimd.indirect_dma_start(
                                ring[:, g * half + j, 0:ROWW[l]], None, xrtab[l],
                                bass.IndirectOffsetOnAxis(ap=gidx[:, g, j:j + 1], axis=0)
                            ).then_inc(s["row_gathered"][g * half + j], 16)
                if l == 1:
                    pool.wait_ge(s["brow_loaded"], 16 * (l + 1))
                    with pool.Fori(0, NT // U) as i:
                        for k in range(U):
                            t = U * i + k
                            gate(s["x_loaded"][k], 16 * (i + 2))
                            nc.gpsimd.tensor_tensor(residual(t), residual(t), brow[0:TN, :], ALU.add).then_inc(s["x_added"], 1)

        @block.vector
        def _(dve):
            chain = [0]

            def link(ins):
                chain[0] += 1
                ins.then_inc(dve_step, 1)
                dve.wait_ge(dve_step, chain[0])

            def gate(sm, value):
                dve.wait_ge(sm, value)
                dve.sem_inc(dve_gate, 1)

            def floor(dst_f_, y, as_int):
                link(nc.vector.tensor_copy(as_int, y))
                link(nc.vector.tensor_copy(dst_f_, as_int))
                link(nc.vector.tensor_tensor(y, dst_f_, y, ALU.is_gt))
                link(nc.vector.tensor_tensor(dst_f_, dst_f_, y, ALU.subtract))

            dve.sem_inc(LS[1]["x_used"], U)
            link(nc.vector.memset(rows_i[:, 0:2, :], 0))
            nc.vector.memset(rows_i[:, 2, :], PAD_DST).then_inc(pads_set, 1)
            dve.wait_ge(dst_loaded, 16)
            link(nc.vector.tensor_copy(dst_f, dst_i))
            link(nc.vector.tensor_scalar(d_y, dst_f, 0.5, 1.0 / TN, ALU.add, ALU.mult))
            floor(d_hi, d_y, d_i)
            link(nc.vector.scalar_tensor_tensor(out=d_lo_16, in0=d_hi, scalar=-float(TN), in1=dst_f, op0=ALU.mult, op1=ALU.add))
            link(nc.vector.tensor_copy(d_hi_16, d_hi))
            nc.vector.memset(ring[0:TN, 5:8, PIECE:HC0[0]], 1.0).then_inc(piece_ones_set, 1)

            dve.wait_ge(consts_ready, 2)
            dve.wait_ge(numbers_set, 2)
            with dve.Fori(0, HROUNDS) as n_:
                for part in range(3):
                    dve.wait_ge(hot_used, 3 * n_ + part + 1)
                    off, n = n_ * NT + sum(HPARTS[:part]), HPARTS[part]
                    for one_hot, digit, numbers, size in ((hhi[part], d_hi_16, hi_numbers, NT), (hlo[part], d_lo_16, lo_numbers, TN)):
                        last = nc.vector.tensor_tensor(one_hot[:, :, 0:n], numbers[:, :, 0:n],
                                                       digit[:, bass.ds(off, n)].unsqueeze(1).to_broadcast([TN, size, n]),
                                                       ALU.is_equal)
                    last.then_inc(hot_ready, 1)
            dve.wait_ge(edges_loaded, 16 * 8)
            link(nc.vector.scalar_tensor_tensor(out=ev_rows[:, :, 0], in0=rows_i[:, 0, :], scalar=float(R),
                                                in1=rows_i[:, 1, :], op0=ALU.mult, op1=ALU.add))
            link(nc.vector.tensor_copy(ev_rows[:, :, 1], rows_i[:, 1, :]))
            nc.vector.tensor_copy(ev_rows[:, :, 2], rows_i[:, 2, :]).then_inc(etab_src, 1)
            link(nc.vector.memset(small[:, c_cnt], 0.0))
            link(nc.vector.tensor_tensor(d_falls, d_this, d_next, ALU.is_gt))
            link(nc.vector.tensor_reduce(small[0:ORDER_P, c_cnt][:, NT:NT + 1], d_falls, AX.X, ALU.add))

            dve.wait_ge(counts_done, 1)
            nc.vector.tensor_copy(counts, bank[7][0:NT, 0:TN]).then_inc(cnt_ready, 1)
            dve.wait_ge(sums_done, 1)
            nc.vector.tensor_copy(small[0:TN, c_cnt][:, 0:NT], bank[4][0:TN, 256:256 + NT]).then_inc(cnt_ready, 1)
            dve.wait_ge(sums_done, 2)
            cnt, tot, inc, rp, y, f, St, cur = (small[:, c] for c in (c_cnt, c_tot, c_inc, c_rp, c_y, c_f, c_St, c_cur))
            cnt, tot, falls = cnt[:, 0:NT], tot[:, 0:NT], tot[:, NT:NT + 1]
            link(nc.vector.tensor_copy(tot, bank[5][:, 384:384 + NT]))
            link(nc.vector.tensor_copy(falls.bitcast(I32), bank[5][:, 384 + NT:385 + NT]))
            nc.vector.tensor_copy(rp[0:TN], bank[5][0:TN, 320:320 + NT]).then_inc(cnt_ready, 1)
            dve.wait_ge(cnt_ready, 3)
            link(nc.vector.memset(y, 1.0))
            link(nc.vector.tensor_tensor_scan(inc, y, tot, 0.0, ALU.mult, ALU.add))
            link(nc.vector.tensor_tensor(inc, inc, tot, ALU.subtract))
            link(nc.vector.tensor_tensor(rp[0:TN], inc[0:TN], rp[0:TN], ALU.add))
            nc.vector.tensor_copy(cur[0:TN], rp[0:TN]).then_inc(cursor_ready, 1)
            link(nc.vector.tensor_scalar(y, inc, 1.0 / P, None, ALU.mult))
            floor(f, y, St.bitcast(I32))
            link(nc.vector.tensor_tensor(St, f, small[:, c_it], ALU.add))
            hit = pen[0:ROWS, 0:RC * (NT - 1)].rearrange("r (c t) -> r c t", c=RC)
            sio, ts, is_, t8, tn, ta = (small[0:ROWS, c] for c in (c_sio, c_ts, c_is, c_t8, c_tn, c_ta))
            link(nc.vector.tensor_tensor(hit, St[0:ROWS, 1:NT].unsqueeze(1).to_broadcast([ROWS, RC, NT - 1]),
                                         sio.unsqueeze(2).to_broadcast([ROWS, RC, NT - 1]), ALU.is_le))
            link(nc.vector.tensor_reduce(ts, hit, AX.X, ALU.add))
            link(nc.vector.tensor_tensor(ta, sio, ts, ALU.subtract))
            nc.vector.tensor_copy(is_.bitcast(I32), ta).then_inc(steps_ready, 1)
            n_ = slice(0, TN)
            link(nc.vector.tensor_tensor(rp[n_], rp[n_], small[n_, c_t125], ALU.add))
            link(nc.vector.tensor_tensor(rp[n_], rp[n_], small[n_, c_trash], ALU.subtract))
            link(nc.vector.tensor_scalar(y[n_], cnt[n_], 0.0, None, ALU.is_gt))
            link(nc.vector.tensor_tensor(rp[n_], rp[n_], y[n_], ALU.mult))
            link(nc.vector.tensor_tensor(rp[n_], rp[n_], small[n_, c_trash], ALU.add))
            nc.vector.tensor_copy(start_at[n_, :], rp[n_]).then_inc(start_ready, 1)

            link(nc.vector.tensor_scalar(t8, ts, KEY, None, ALU.mult))
            link(nc.vector.tensor_scalar(tn, ts, float(TN), None, ALU.mult))
            dve.wait_ge(ev_gathered, 16 * RC)
            link(nc.vector.tensor_copy(ta, ts))
            link(nc.vector.tensor_copy(rel[0:ROWS, :].rearrange("r (c j) -> r c j", c=RC), ev[:, :, :, 1]))
            link(nc.vector.tensor_tensor(key.rearrange("r (c j) -> r c j", c=RC), ev[:, :, :, 2],
                                         t8.unsqueeze(2).to_broadcast([ROWS, RC, P]), ALU.add))
            link(nc.vector.tensor_tensor(ev[:, :, :, 2], ev[:, :, :, 2],
                                         tn.unsqueeze(2).to_broadcast([ROWS, RC, P]), ALU.subtract))
            NQ = R * HM
            ends = small[0:ROWS, c_ends]
            link(nc.vector.tensor_copy(ends[:, 0:NQ], key[:, 0:1].to_broadcast([ROWS, NQ])))
            nc.vector.tensor_copy(ends[:, NQ:2 * NQ], key[:, RL - 1:RL].to_broadcast([ROWS, NQ])).then_inc(rows_ready, 1)
            r_ = slice(0, ROWS)
            link(nc.vector.memset(pen[r_, :], 0.0))
            link(nc.vector.tensor_tensor(pen[r_, 1:RL], key[:, 1:RL], key[:, 0:RL - 1], ALU.not_equal))
            link(nc.vector.tensor_scalar(same[r_, :], pen[r_, 0:RL], -1.0, 1.0, ALU.mult, ALU.add))
            link(nc.vector.tensor_scalar(pen[r_, :], pen[r_, :], -BIG, None, ALU.mult))
            link(nc.vector.memset(flag[:, :, :], 0.0))
            dve.wait_ge(turned, 1)
            link(nc.vector.tensor_copy(flag[:, RUN, 0:ROWS], bank[5][0:NQ, 0:ROWS]))
            link(nc.vector.tensor_copy(flag[:, CARRY, 0:ROWS], bank[4][0:NQ, 384:384 + ROWS]))
            for l in range(2):
                link(nc.vector.tensor_scalar(acc_at[:, l, :], bank[4][0:RC, 256:256 + ROWS], float(ROWW[l]), None, ALU.mult))
            link(nc.vector.tensor_copy(row_idx[:, :].rearrange("p (r c) -> p c r", c=RC),
                                       bank[2][:, 0:STEPS].rearrange("p (c r) -> p c r", c=RC)))
            link(nc.vector.tensor_copy(dloc[:, 0:STEPS].rearrange("p (r c) -> p c r", c=RC),
                                       bank[3][:, 0:STEPS].rearrange("p (c r) -> p c r", c=RC)))
            dve.sem_inc(LS[0]["turned_taken"], 1)
            link(nc.vector.memset(dloc[:, STEPS:], -1.0))
            k0 = flag[:, CARRY, 0:ROWS]
            link(nc.vector.tensor_tensor(flag[:, EQ, 1:ROWS], k0[:, 1:ROWS], flag[:, RUN, 0:ROWS - 1], ALU.is_equal))
            link(nc.vector.tensor_tensor(flag[:, UNI, 0:ROWS], k0, flag[:, RUN, 0:ROWS], ALU.is_equal))
            link(nc.vector.tensor_tensor(flag[:, CONT, 0:ROWS], flag[:, UNI, 0:ROWS], flag[:, EQ, 0:ROWS], ALU.mult))
            link(nc.vector.tensor_tensor(flag[:, CONTPEN_B, 0:ROWS], flag[:, UNI, 0:ROWS], flag[:, EQ, 1:ROWS + 1], ALU.mult))
            for a, b in ((EQPEN, EQ), (CONTPEN, CONT), (CONTPEN_B, CONTPEN_B)):
                link(nc.vector.tensor_scalar(flag[:, a, :], flag[:, b, :], -1.0, BIG, ALU.add, ALU.mult))
            dve.sem_inc(lanes_ready, 1)

            for l in range(2):
                s = LS[l]
                H = HEADS[l]
                HW = HWS[l]
                RWL = ROWW[l]
                dve.wait_ge(s["xT_turned"], (3 + WT if l == 0 else U) + NT)
                nc.vector.memset(ring[0:TN, 0:U, 0:RWL].rearrange("p u (h w) -> p u h w", h=H)[:, :, :, D // H:HW], 1.0
                                 ).then_inc(s["ones_set"], 1)

                dve.wait_ge(s["q_loaded"], 16 * (l + 1))
                raw = qf_raw[:, 0:RL * R * H].rearrange("r (x q) -> r q x", q=R * H)
                c_in = small[0:ROWS, c_carry]
                c_out = small[0:ROWS, c_last]
                for q in range(R * H):
                    link(nc.vector.tensor_tensor_scan(qf[:, q, :], same[0:ROWS, :], raw[:, q, :], 0.0, ALU.mult, ALU.add))
                nc.vector.tensor_copy(c_out[:, 0:R * H], qf[:, 0:R * H, RL - 1]).then_inc(s["qend_ready"], 1)
                dve.wait_ge(s["qend_turned"], l + 1)
                fl = flag[0:R * H]
                link(nc.vector.tensor_tensor_scan(fl[:, RUN, 0:ROWS], fl[:, CONT, 0:ROWS], bank[5][0:R * H, 0:ROWS],
                                                  0.0, ALU.mult, ALU.add))
                link(nc.vector.memset(fl[:, CARRY, 0:1], 0.0))
                nc.vector.tensor_tensor(fl[:, CARRY, 1:ROWS], fl[:, RUN, 0:ROWS - 1], fl[:, EQ, 1:ROWS], ALU.mult
                                        ).then_inc(s["qcarry_ready"], 1)
                dve.wait_ge(s["qcarry_turned"], l + 1)
                link(nc.vector.tensor_copy(c_in[:, 0:R * H], bank[5][0:ROWS, 0:R * H]))
                dve.sem_inc(s["qcarry_taken"], 1)
                for q in range(R * H):
                    link(nc.vector.tensor_tensor_scan(qf[:, q, :], same[0:ROWS, :], raw[:, q, :], c_in[:, q:q + 1],
                                                      ALU.mult, ALU.add))
                for r in range(R):
                    link(nc.vector.scalar_tensor_tensor(
                        out=qf[:, r * H:(r + 1) * H, :], in0=rel[0:ROWS, :].unsqueeze(1).to_broadcast([ROWS, H, RL]),
                        scalar=float(r), in1=qf[:, r * H:(r + 1) * H, :], op0=ALU.is_equal, op1=ALU.mult))
                al = alpha[:, 0:H, :]
                link(nc.vector.tensor_tensor(al, qf[:, 0:H, :], qf[:, H:2 * H, :], ALU.add))
                for r in range(2, R):
                    link(nc.vector.tensor_tensor(al, al, qf[:, r * H:(r + 1) * H, :], ALU.add))
                nc.vector.memset(big[0:TN, 0:ALPHA_AT], 0.0).then_inc(s["sums_zeroed"], 1)
                if l == 0:
                    dve.sem_inc(w2_used, 4)
                    dve.sem_inc(w2_ready, 1)
                    dve.wait_ge(qk_loaded, 64)
                    w2_terms = small[:, c_w2].rearrange("p (c a) -> p c a", a=2)
                    with dve.Fori(0, R) as r:
                        dve.wait_ge(w2_ready, r + 1)
                        for c in range(DC):
                            dve.wait_ge(w2_loaded[c % 2], 16 * (DC // 2 * r + c // 2 + 1))
                            w_tile, product = ring[:, 5 + c % 2, 0:D], ring[:, 7, 0:D]
                            for a, row in enumerate((q2_row, k2_row)):
                                dve.wait_ge(w2_used, 4 + 2 * (DC * r + c) + a)
                                nc.vector.tensor_tensor_reduce(product, w_tile, row, 1.0, 0.0, ALU.mult, ALU.add,
                                                               w2_terms[:, c, a:a + 1]).then_inc(w2_used, 1)
                        gate(w2_used, 4 + 2 * DC * (r + 1))
                        nc.vector.tensor_scalar(qk_cols(1)[:, :, :, bass.ds(r, 1), 0].rearrange("p c a r -> p c (a r)"),
                                                w2_terms, 1.0, None, ALU.mult).then_inc(w2_ready, 1)
                for h in range(H):
                    dve.wait_ge(s["k_turned"], HM * l + h + 1)
                    nc.vector.tensor_tensor(alpha[:, h, :], alpha[:, h, :], bank[5][0:ROWS, :], ALU.add).then_inc(s["k_added"], 1)
                dve.wait_ge(s["k_added"], HM * l + H)
                link(nc.vector.scalar_tensor_tensor(out=al, in0=al, scalar=SLOPE, in1=al, op0=ALU.mult, op1=ALU.max))
                fl = flag[0:H]
                for w in range(2):
                    def scan(h, first):
                        if w == 0:
                            return nc.vector.tensor_tensor_scan(amax[:, h, :], pen[0:ROWS, 0:RL], alpha[:, h, :],
                                                                first, ALU.add, ALU.max)
                        return nc.vector.tensor_tensor_scan(amax[:, h, ::-1], pen[0:ROWS, RL:0:-1], amax[:, h, ::-1],
                                                            first, ALU.add, ALU.max)
                    for h in range(H):
                        link(scan(h, -BIG))
                    nc.vector.tensor_copy(c_out[:, 0:H], amax[:, 0:H, RL - 1 if w == 0 else 0]).then_inc(s["end_ready"], 1)
                    dve.wait_ge(s["end_turned"], 2 * l + w + 1)
                    turned_ends = bank[5][0:H, 0:ROWS]
                    if w == 0:
                        link(nc.vector.tensor_tensor_scan(fl[:, RUN, 0:ROWS], fl[:, CONTPEN, 0:ROWS], turned_ends,
                                                          -BIG, ALU.add, ALU.max))
                        link(nc.vector.memset(fl[:, CARRY, 0:1], -BIG))
                        last = nc.vector.tensor_tensor(fl[:, CARRY, 1:ROWS], fl[:, RUN, 0:ROWS - 1],
                                                       fl[:, EQPEN, 1:ROWS], ALU.add)
                    else:
                        link(nc.vector.tensor_tensor_scan(fl[:, RUN, ROWS - 1::-1], fl[:, CONTPEN_B, ROWS - 1::-1],
                                                          turned_ends[:, ::-1], -BIG, ALU.add, ALU.max))
                        link(nc.vector.memset(fl[:, CARRY, ROWS - 1:ROWS], -BIG))
                        last = nc.vector.tensor_tensor(fl[:, CARRY, 0:ROWS - 1], fl[:, RUN, 1:ROWS],
                                                       fl[:, EQPEN, 1:ROWS], ALU.add)
                    last.then_inc(s["carry_ready"], 1)
                    dve.wait_ge(s["carry_turned"], 2 * l + w + 1)
                    link(nc.vector.tensor_copy(c_in[:, 0:H], bank[5][0:ROWS, 0:H]))
                    for h in range(H):
                        link(scan(h, c_in[:, h:h + 1]))
                nc.vector.tensor_tensor(al, al, amax[:, 0:H, :], ALU.subtract).then_inc(s["diff_ready"], 1)
                for h in range(H):
                    dve.wait_ge(s["e_turned"], HM * l + h + 1)
                    link(nc.vector.tensor_copy(wE[:, 0:STEPS, h].rearrange("p (r c) -> p c r", c=RC),
                                               bank[E_BANK[h]][:, 0:STEPS].rearrange("p (c r) -> p c r", c=RC)))
                link(nc.vector.memset(wE[:, STEPS:, :], 0.0))
                dve.sem_inc(s["w_ready"], 1)

                nc.vector.memset(big[0:TN, AMAX_AT:K_AT], 0.0).then_inc(s["sums_zeroed"], 1)
                dve.sem_inc(s["sum_added"], AHEAD)
                dve.wait_ge(s["dense_done"], UNITS * (NT + 2))

                def one_hot(st, slot):
                    at = dloc[:, bass.ds(st, 1)]
                    if H > 1:
                        dve.wait_ge(s["S_built"], st + 1)
                        nc.vector.tensor_scalar(hot[:, slot, :], iota_n[:, :], at, None, ALU.is_equal
                                                ).then_inc(s["hot_built"], 1)
                    else:
                        dve.wait_ge(s["step_done"], st + 1 + GS - AHEAD)
                        nc.vector.tensor_scalar(one_hots[l][:, slot, 0, :], iota_n[:, :], at,
                                                wE[:, bass.ds(st, 1), 0:1].rearrange("p a b -> p (a b)"),
                                                ALU.is_equal, ALU.mult).then_inc(s["hot_built"], 1)

                for j in range(AHEAD):
                    one_hot(j, j)
                dve.wait_ge(s["sums_zeroed"], 4 * (l + 1))
                with dve.Fori(0, STEPS // GS) as i:
                    for j in range(GS):
                        st = GS * i + j
                        one_hot(st + AHEAD, j % AHEAD)
                        at = dve.value_load(acc_at[j % RC:j % RC + 1, l, bass.ds(i * (GS // RC) + j // RC, 1)],
                                            min_val=0, max_val=(NT - 1) * RWL)
                        dve.wait_ge(s["step_done"], GS + st + 1)
                        dve.wait_ge(s["sum_added"], AHEAD + st)
                        tile = big[0:TN, bass.ds(at, RWL)].rearrange("p (a w) -> p a w", a=2)
                        nc.vector.tensor_tensor(tile, tile, banks[0:TN, 2 * (j % AHEAD):2 * (j % AHEAD) + 2, 0:RWL // 2],
                                                ALU.add).then_inc(s["sum_added"], 1)

                dve.wait_ge(s["sum_added"], AHEAD + STEPS)
                z = small[0:TN, c_z][:, 0:NT * H]
                link(nc.vector.tensor_scalar(z.rearrange("p (t h) -> p t h", h=H),
                                             big[0:TN, 0:NT * RWL].rearrange("p (t h w) -> p t h w", t=NT, h=H)[:, :, :, D // H],
                                             SOFTMAX_EPS, None, ALU.add))
                link(nc.vector.reciprocal(z, z))
                dve.wait_ge(s["brow_loaded"], 16 * (l + 1))

                def divide(t, add):
                    for h in range(H):
                        u = node_sum(l, t)[:, h, :]
                        last = nc.vector.scalar_tensor_tensor(out=u, in0=u, scalar=z[:, bass.ds(t * H + h, 1)],
                                                              in1=add[:, h * (D // H):(h + 1) * (D // H)],
                                                              op0=ALU.mult, op1=ALU.add)
                    return last

                if l == 0:
                    dve.sem_inc(s["h_ready"], 2)
                    divide(0, brow[0:TN, :]).then_inc(s["u_ready"], 1)
                    divide(1, brow[0:TN, :]).then_inc(s["u_ready"], 1)
                    for i, last_turn in turns(dve, NT, U):
                        for k in range(U):
                            t = U * i + k
                            if k + 2 < U or not last_turn:
                                divide(t + 2, brow[0:TN, :]).then_inc(s["u_ready"], 1)
                            e = ring[0:TN, PAT[k], 0:D]
                            dve.wait_ge(s["exp_ready"], t + 1)
                            nc.vector.tensor_scalar(e, e, 1.0, -1.0, ALU.min, ALU.add).then_inc(s["e_set"], 1)
                            dve.wait_ge(s["e_set"], t + 1)
                            gate(LS[1]["xT_turned"], t + 1)
                            nc.vector.scalar_tensor_tensor(out=heads(x_slot(k)[0:TN, :], H), in0=node_sum(l, t), scalar=0.0,
                                                           in1=heads(e, H), op0=ALU.max, op1=ALU.add).then_inc(s["h_ready"], 1)
                else:
                    stats = same[0:TN, 0:12 * U].rearrange("p (t a) -> p t a", a=12)
                    tile_mv = same[0:TN, 12 * U:14 * U].rearrange("p (t a) -> p t a", a=2)
                    mv = small[0:TN, c_mv].rearrange("p (t a) -> p t a", a=2)
                    PER_TURN = 3 * U + 1

                    def with_residual(t):
                        gate(s["x_added"], t + 1)
                        divide(t, residual(t)).then_inc(s["x_used"], 1)

                    def statistics(t, k):
                        gate(s["x_used"], U + t + 1)
                        for half in range(2):
                            nc.vector.bn_stats(stats[:, k, 6 * half:6 * half + 6],
                                               node_sum(l, t)[:, 0, half * HALF:(half + 1) * HALF]).then_inc(s["e_set"], 1)

                    def variances(i):
                        gate(s["e_set"], PER_TURN * i + 2 * U)
                        for k in range(U):
                            nc.vector.bn_aggr(tile_mv[:, k, :], stats[:, k, :].rearrange("p (a b) -> p a b", a=2)
                                              ).then_inc(s["e_set"], 1)
                        dve.wait_ge(s["e_set"], PER_TURN * i + 3 * U)
                        nc.vector.tensor_scalar(deviation, tile_mv[:, :, 1], NORM_EPS, None, ALU.add).then_inc(var_ready, 1)

                    def inverses(i):
                        dve.wait_ge(dev_ready, i + 1)
                        nc.vector.reciprocal(deviation, deviation).then_inc(s["e_set"], 1)

                    def factors(i, between):
                        turn_mv = mv[:, bass.ds(U * i, U), :]
                        gate(s["e_set"], PER_TURN * (i + 1) + between)
                        nc.vector.scalar_tensor_tensor(out=turn_mv[:, :, 0], in0=tile_mv[:, :, 0], scalar=-1.0,
                                                       in1=deviation, op0=ALU.mult, op1=ALU.mult)
                        nc.vector.tensor_scalar(turn_mv[:, :, 1], deviation, 1.0, None, ALU.mult).then_inc(s["h_ready"], 1)

                    def norm_turn(i, first=False, last=False):
                        for k in range(U):
                            t = U * i + k
                            if k < U - 1 or not last:
                                with_residual(t + 1)
                            if not first and k == 0:
                                variances(i - 1)
                            if not first and k == 2:
                                factors(i - 1, 4)
                            statistics(t, k)
                            if not first and k == 1:
                                inverses(i - 1)

                    with_residual(0)
                    norm_turn(0, first=True)
                    with dve.Fori(1, NT // U - 1) as i:
                        norm_turn(i)
                    norm_turn(NT // U - 1, last=True)
                    variances(NT // U - 1)
                    inverses(NT // U - 1)
                    factors(NT // U - 1, 0)


_INS = ["x", "src", "dst", "edge_type_3", "L0_gnn_W1", "L0_gnn_q1", "L0_gnn_k1", "L0_gnn_b1",
        "L0_gnn_W2", "L0_gnn_q2", "L0_gnn_k2", "L0_gnn_b2"]


def kernel(**inputs):
    import numpy as np
    import concourse.bacc as bacc
    from concourse.bass_utils import run_bass_kernel_spmd

    nc = bacc.Bacc("TRN2", target_bir_lowering=False, num_devices=1)
    arrays, args = {}, []
    for name in _INS:
        a = np.ascontiguousarray(inputs[name])
        arrays[f"in_{name}"] = a
        args.append(nc.dram_tensor(f"in_{name}", a.shape, mybir.dt.from_np(a.dtype), kind="ExternalInput").ap())
    shape = inputs["x"].shape
    args.append(nc.dram_tensor("out_0", shape, F32, kind="ExternalOutput").ap())
    rgat_kernel(nc, *args)
    r = run_bass_kernel_spmd(nc, [arrays], core_ids=[0])
    return r.results[0]["out_0"]
```
